# Optimizing a Trainium2 kernel written in Bass

```python
import numpy as np
import jax
import jax.numpy as jnp

def _softmax(x, axis=-1):
    return jax.nn.softmax(x, axis=axis)

def _gelu(x):
    return jax.nn.gelu(x, approximate=True)

def _silu(x):
    return jax.nn.silu(x)

def _sigmoid(x):
    return jax.nn.sigmoid(x)

def _layernorm(x, axis=-1, eps=1e-05):
    m = jnp.mean(x, axis=axis, keepdims=True)
    v = jnp.var(x, axis=axis, keepdims=True)
    return (x - m) / jnp.sqrt(v + eps)

def _scatter_add(tgt, idx, src, axis=0):
    return tgt.at[idx].add(src)

def _segment_sum(src, seg, n):
    return jax.ops.segment_sum(src, seg, n)
kernel_name = 'mk_seq_preln_d2_jaxref_r8_54032d'

def setup_inputs(seed: int=0):
    np.random.seed(seed)
    _w = jnp.asarray

    def _L0_attn_setup():
        import jax, jax.numpy as jnp
        import numpy as np
        B, T, H, NH = (2, 256, 128, 16)
        D = H // NH
        K_CONV = 4

        def _dwconv_silu(x, w):
            Kc = w.shape[1]
            xp = jnp.pad(x, ((0, 0), (Kc - 1, 0), (0, 0))).transpose(0, 2, 1)
            y = jax.lax.conv_general_dilated(xp, w[:, None, :], (1,), 'VALID', feature_group_count=w.shape[0], dimension_numbers=('NCH', 'OIH', 'NCH'))
            return jax.nn.silu(y.transpose(0, 2, 1))

        def _l2norm(x, eps=1e-06):
            return x * jax.lax.rsqrt(jnp.sum(x * x, -1, keepdims=True) + eps)

        def _forward(hidden, Wq, Wk, Wv, conv_q, conv_k, conv_v, Wb, Wa, A_log, dt_bias, Wg, norm_w, Wo):
            Bh, Tt, Hh = hidden.shape
            nh = A_log.shape[0]
            d = Hh // nh
            q = _dwconv_silu(hidden @ Wq.T, conv_q).reshape(Bh, Tt, nh, d)
            k = _dwconv_silu(hidden @ Wk.T, conv_k).reshape(Bh, Tt, nh, d)
            v = _dwconv_silu(hidden @ Wv.T, conv_v).reshape(Bh, Tt, nh, d)
            q = _l2norm(q) * d ** (-0.5)
            k = _l2norm(k)
            beta = jax.nn.sigmoid(hidden @ Wb.T)
            g = -jnp.exp(A_log) * jax.nn.softplus(hidden @ Wa.T + dt_bias)

            def step(S, inp):
                qt, kt, vt, gt, bt = inp
                S = S * jnp.exp(gt)[..., None, None]
                pred = jnp.einsum('bhk,bhkv->bhv', kt, S)
                dv = (vt - pred) * bt[..., None]
                S = S + jnp.einsum('bhk,bhv->bhkv', kt, dv)
                ot = jnp.einsum('bhk,bhkv->bhv', qt, S)
                return (S, ot)
            xs = (q.transpose(1, 0, 2, 3), k.transpose(1, 0, 2, 3), v.transpose(1, 0, 2, 3), g.transpose(1, 0, 2), beta.transpose(1, 0, 2))
            S0 = jnp.zeros((Bh, nh, d, d), hidden.dtype)
            _, o = jax.lax.scan(step, S0, xs)
            o = o.transpose(1, 0, 2, 3)
            gate = (hidden @ Wg.T).reshape(Bh, Tt, nh, d)
            o = o * jax.lax.rsqrt(jnp.mean(o * o, -1, keepdims=True) + 1e-05) * norm_w
            o = o * jax.nn.silu(gate)
            return o.reshape(Bh, Tt, Hh) @ Wo.T
        key = jax.random.key(seed)
        ks = jax.random.split(key, 16)
        s = 0.02
        return {'hidden': jax.random.normal(ks[0], (B, T, H), jnp.float32), 'Wq': jax.random.normal(ks[1], (H, H), jnp.float32) * s, 'Wk': jax.random.normal(ks[2], (H, H), jnp.float32) * s, 'Wv': jax.random.normal(ks[3], (H, H), jnp.float32) * s, 'conv_q': jax.random.normal(ks[4], (H, K_CONV), jnp.float32) * 0.5, 'conv_k': jax.random.normal(ks[5], (H, K_CONV), jnp.float32) * 0.5, 'conv_v': jax.random.normal(ks[6], (H, K_CONV), jnp.float32) * 0.5, 'Wb': jax.random.normal(ks[7], (NH, H), jnp.float32) * s, 'Wa': jax.random.normal(ks[8], (NH, H), jnp.float32) * s, 'A_log': jnp.log(jax.random.uniform(ks[9], (NH,), jnp.float32, 1.0, 16.0)), 'dt_bias': jnp.log(jnp.expm1(jax.random.uniform(ks[10], (NH,), jnp.float32, 0.001, 0.1))), 'Wg': jax.random.normal(ks[11], (H, H), jnp.float32) * s, 'norm_w': jnp.ones((D,), jnp.float32), 'Wo': jax.random.normal(ks[12], (H, H), jnp.float32) * s}
    _L0_attn_in = _L0_attn_setup()

    def _L0_ffn_setup():
        import jax, jax.numpy as jnp
        import numpy as np
        DIM = 128
        HID = 512
        E = 8
        TOPK = 2
        ALPHA = 2.0
        B, T = (1, 256)
        DOWN_SCALE = 0.01
        key = jax.random.key(seed)
        ks = jax.random.split(key, 8)
        s = 1.0 / np.sqrt(DIM)
        sh = 1.0 / np.sqrt(HID)
        return {'x': jax.random.normal(ks[0], (B, T, DIM), jnp.float32), 'w_router': jax.random.uniform(ks[1], (DIM, E), jnp.float32, -s, s), 'w_up': jax.random.uniform(ks[2], (E - 1, DIM, HID), jnp.float32, -s, s), 'w_gate': jax.random.uniform(ks[3], (E - 1, DIM, HID), jnp.float32, -s, s), 'w_down': jax.random.normal(ks[4], (E - 1, HID, DIM), jnp.float32) * DOWN_SCALE, 'ws_up': jax.random.uniform(ks[5], (DIM, HID), jnp.float32, -s, s), 'ws_gate': jax.random.uniform(ks[6], (DIM, HID), jnp.float32, -s, s), 'ws_down': jax.random.normal(ks[7], (HID, DIM), jnp.float32) * DOWN_SCALE}
    _L0_ffn_in = _L0_ffn_setup()

    def _L1_attn_setup():
        import jax, jax.numpy as jnp
        import numpy as np
        BASE_FREQUENCY = 10000.0
        LRP = 17
        MIN_L = 1.0 - LRP / 100.0
        SDT_L = (BASE_FREQUENCY - MIN_L * BASE_FREQUENCY) * 2.0
        ARM_ATTENTION = 2.0
        HEADS_DIM = 64

        def _nrope(xs, base, angle_range):
            N, T, d = xs.shape
            half = d // 2
            inv_freq = base ** (-jnp.arange(half, dtype=jnp.float32) / half)
            pos = jnp.arange(T, dtype=jnp.float32)
            scale = angle_range / jnp.maximum(T - 1, 1)
            ang = pos[:, None] * inv_freq[None, :] * scale
            cos, sin = (jnp.cos(ang), jnp.sin(ang))
            x1, x2 = (xs[..., :half], xs[..., half:])
            return jnp.concatenate([x1 * cos - x2 * sin, x1 * sin + x2 * cos], axis=-1)
        key = jax.random.key(seed)
        ks = jax.random.split(key, 9)
        B, T, E = (4, 128, 128)
        x = jax.random.normal(ks[0], (B, T, E), dtype=jnp.float32)

        def w(k):
            return jax.random.normal(k, (E, E), dtype=jnp.float32) * 0.02
        z = jnp.zeros((E,), dtype=jnp.float32)
        return {'x': x, 'Wq': w(ks[1]), 'bq': z, 'Wk': w(ks[2]), 'bk': z, 'Wv': w(ks[3]), 'bv': z, 'Wo': w(ks[4]), 'bo': z, 'nrope_freq': jnp.zeros((1,), dtype=jnp.float32)}
    _L1_attn_in = _L1_attn_setup()

    def _L1_ffn_setup():
        import jax, jax.numpy as jnp
        import numpy as np
        DIM = 128

        def _reference_tuple_inner(x, W_r, W_k, W_v, mu_r, mu_k):
            B, T, C = x.shape
            x_prev = jnp.concatenate([jnp.zeros((B, 1, C), x.dtype), x[:, :-1, :]], axis=1)
            xr = mu_r * x + (1.0 - mu_r) * x_prev
            xk = mu_k * x + (1.0 - mu_k) * x_prev
            r = jax.nn.sigmoid(jnp.einsum('btc,dc->btd', xr, W_r))
            k = jnp.einsum('btc,dc->btd', xk, W_k)
            k_act = jnp.square(jax.nn.relu(k))
            out = r * jnp.einsum('btc,dc->btd', k_act, W_v)
            new_state = x[:, -1, :]
            return (out, new_state)
        key = jax.random.key(seed)
        ks = jax.random.split(key, 6)
        B, T, C = (8, 256, DIM)
        x = jax.random.normal(ks[0], (B, T, C), dtype=jnp.float32)
        s = 1.0 / np.sqrt(C)
        W_r = jax.random.uniform(ks[1], (C, C), jnp.float32, -s, s)
        W_k = jax.random.uniform(ks[2], (C, C), jnp.float32, -s, s)
        W_v = jax.random.uniform(ks[3], (C, C), jnp.float32, -s, s)
        mu_r = jax.random.uniform(ks[4], (C,), jnp.float32)
        mu_k = jax.random.uniform(ks[5], (C,), jnp.float32)
        return {'x': x, 'W_r': W_r, 'W_k': W_k, 'W_v': W_v, 'mu_r': mu_r, 'mu_k': mu_k}
    _L1_ffn_in = _L1_ffn_setup()
    _d = {'L0_attn_hidden': _L0_attn_in['hidden'], 'L0_attn_Wq': _L0_attn_in['Wq'], 'L0_attn_Wk': _L0_attn_in['Wk'], 'L0_attn_Wv': _L0_attn_in['Wv'], 'L0_attn_conv_q': _L0_attn_in['conv_q'], 'L0_attn_conv_k': _L0_attn_in['conv_k'], 'L0_attn_conv_v': _L0_attn_in['conv_v'], 'L0_attn_Wb': _L0_attn_in['Wb'], 'L0_attn_Wa': _L0_attn_in['Wa'], 'L0_attn_A_log': _L0_attn_in['A_log'], 'L0_attn_dt_bias': _L0_attn_in['dt_bias'], 'L0_attn_Wg': _L0_attn_in['Wg'], 'L0_attn_norm_w': _L0_attn_in['norm_w'], 'L0_attn_Wo': _L0_attn_in['Wo'], 'L0_ffn_w_router': _L0_ffn_in['w_router'], 'L0_ffn_w_up': _L0_ffn_in['w_up'], 'L0_ffn_w_gate': _L0_ffn_in['w_gate'], 'L0_ffn_w_down': _L0_ffn_in['w_down'], 'L0_ffn_ws_up': _L0_ffn_in['ws_up'], 'L0_ffn_ws_gate': _L0_ffn_in['ws_gate'], 'L0_ffn_ws_down': _L0_ffn_in['ws_down'], 'L1_attn_Wq': _L1_attn_in['Wq'], 'L1_attn_bq': _L1_attn_in['bq'], 'L1_attn_Wk': _L1_attn_in['Wk'], 'L1_attn_bk': _L1_attn_in['bk'], 'L1_attn_Wv': _L1_attn_in['Wv'], 'L1_attn_bv': _L1_attn_in['bv'], 'L1_attn_Wo': _L1_attn_in['Wo'], 'L1_attn_bo': _L1_attn_in['bo'], 'L1_attn_nrope_freq': _L1_attn_in['nrope_freq'], 'L1_ffn_W_r': _L1_ffn_in['W_r'], 'L1_ffn_W_k': _L1_ffn_in['W_k'], 'L1_ffn_W_v': _L1_ffn_in['W_v'], 'L1_ffn_mu_r': _L1_ffn_in['mu_r'], 'L1_ffn_mu_k': _L1_ffn_in['mu_k']}
    _x0 = _d['L0_attn_hidden']
    _d['L0_attn_hidden'] = jax.random.normal(jax.random.fold_in(jax.random.key(seed), 1), (8, 512, 128), dtype=_x0.dtype)
    del _x0
    return _d

def reference(L0_attn_hidden, L0_attn_Wq, L0_attn_Wk, L0_attn_Wv, L0_attn_conv_q, L0_attn_conv_k, L0_attn_conv_v, L0_attn_Wb, L0_attn_Wa, L0_attn_A_log, L0_attn_dt_bias, L0_attn_Wg, L0_attn_norm_w, L0_attn_Wo, L0_ffn_w_router, L0_ffn_w_up, L0_ffn_w_gate, L0_ffn_w_down, L0_ffn_ws_up, L0_ffn_ws_gate, L0_ffn_ws_down, L1_attn_Wq, L1_attn_bq, L1_attn_Wk, L1_attn_bk, L1_attn_Wv, L1_attn_bv, L1_attn_Wo, L1_attn_bo, L1_attn_nrope_freq, L1_ffn_W_r, L1_ffn_W_k, L1_ffn_W_v, L1_ffn_mu_r, L1_ffn_mu_k):

    def _L0_attn_ref(hidden, Wq, Wk, Wv, conv_q, conv_k, conv_v, Wb, Wa, A_log, dt_bias, Wg, norm_w, Wo):
        import jax, jax.numpy as jnp
        import numpy as np
        B, T, H, NH = (2, 256, 128, 16)
        D = H // NH
        K_CONV = 4

        def _dwconv_silu(x, w):
            Kc = w.shape[1]
            xp = jnp.pad(x, ((0, 0), (Kc - 1, 0), (0, 0))).transpose(0, 2, 1)
            y = jax.lax.conv_general_dilated(xp, w[:, None, :], (1,), 'VALID', feature_group_count=w.shape[0], dimension_numbers=('NCH', 'OIH', 'NCH'))
            return jax.nn.silu(y.transpose(0, 2, 1))

        def _l2norm(x, eps=1e-06):
            return x * jax.lax.rsqrt(jnp.sum(x * x, -1, keepdims=True) + eps)

        def _forward(hidden, Wq, Wk, Wv, conv_q, conv_k, conv_v, Wb, Wa, A_log, dt_bias, Wg, norm_w, Wo):
            Bh, Tt, Hh = hidden.shape
            nh = A_log.shape[0]
            d = Hh // nh
            q = _dwconv_silu(hidden @ Wq.T, conv_q).reshape(Bh, Tt, nh, d)
            k = _dwconv_silu(hidden @ Wk.T, conv_k).reshape(Bh, Tt, nh, d)
            v = _dwconv_silu(hidden @ Wv.T, conv_v).reshape(Bh, Tt, nh, d)
            q = _l2norm(q) * d ** (-0.5)
            k = _l2norm(k)
            beta = jax.nn.sigmoid(hidden @ Wb.T)
            g = -jnp.exp(A_log) * jax.nn.softplus(hidden @ Wa.T + dt_bias)

            def step(S, inp):
                qt, kt, vt, gt, bt = inp
                S = S * jnp.exp(gt)[..., None, None]
                pred = jnp.einsum('bhk,bhkv->bhv', kt, S)
                dv = (vt - pred) * bt[..., None]
                S = S + jnp.einsum('bhk,bhv->bhkv', kt, dv)
                ot = jnp.einsum('bhk,bhkv->bhv', qt, S)
                return (S, ot)
            xs = (q.transpose(1, 0, 2, 3), k.transpose(1, 0, 2, 3), v.transpose(1, 0, 2, 3), g.transpose(1, 0, 2), beta.transpose(1, 0, 2))
            S0 = jnp.zeros((Bh, nh, d, d), hidden.dtype)
            _, o = jax.lax.scan(step, S0, xs)
            o = o.transpose(1, 0, 2, 3)
            gate = (hidden @ Wg.T).reshape(Bh, Tt, nh, d)
            o = o * jax.lax.rsqrt(jnp.mean(o * o, -1, keepdims=True) + 1e-05) * norm_w
            o = o * jax.nn.silu(gate)
            return o.reshape(Bh, Tt, Hh) @ Wo.T
        return _forward(hidden, Wq, Wk, Wv, conv_q, conv_k, conv_v, Wb, Wa, A_log, dt_bias, Wg, norm_w, Wo)

    def _L0_ffn_ref(x, w_router, w_up, w_gate, w_down, ws_up, ws_gate, ws_down):
        import jax, jax.numpy as jnp
        import numpy as np
        DIM = 128
        HID = 512
        E = 8
        TOPK = 2
        ALPHA = 2.0
        B, T = (1, 256)
        DOWN_SCALE = 0.01
        logits = x @ w_router
        probs = jax.nn.softmax(logits.astype(jnp.float32), axis=-1).astype(logits.dtype)
        topk_vals, topk_idx = jax.lax.top_k(probs, TOPK)
        up = jnp.einsum('btd,edh->ebth', x, w_up)
        gate = jax.nn.silu(jnp.einsum('btd,edh->ebth', x, w_gate))
        exp_out = jnp.einsum('ebth,ehd->ebtd', up * gate, w_down)
        out = jnp.zeros_like(x)
        eids = jnp.arange(E - 1)
        for i in range(TOPK - 1):
            idx_i = topk_idx[..., i]
            sel = (idx_i[None, :, :] == eids[:, None, None]).astype(x.dtype)
            gathered = jnp.einsum('ebt,ebtd->btd', sel, exp_out)
            out = out + ALPHA * topk_vals[..., i:i + 1] * gathered
        shared = x @ ws_up * jax.nn.silu(x @ ws_gate) @ ws_down
        return out + shared

    def _L1_attn_ref(x, Wq, bq, Wk, bk, Wv, bv, Wo, bo, nrope_freq):
        import jax, jax.numpy as jnp
        import numpy as np
        BASE_FREQUENCY = 10000.0
        LRP = 17
        MIN_L = 1.0 - LRP / 100.0
        SDT_L = (BASE_FREQUENCY - MIN_L * BASE_FREQUENCY) * 2.0
        ARM_ATTENTION = 2.0
        HEADS_DIM = 64

        def _nrope(xs, base, angle_range):
            N, T, d = xs.shape
            half = d // 2
            inv_freq = base ** (-jnp.arange(half, dtype=jnp.float32) / half)
            pos = jnp.arange(T, dtype=jnp.float32)
            scale = angle_range / jnp.maximum(T - 1, 1)
            ang = pos[:, None] * inv_freq[None, :] * scale
            cos, sin = (jnp.cos(ang), jnp.sin(ang))
            x1, x2 = (xs[..., :half], xs[..., half:])
            return jnp.concatenate([x1 * cos - x2 * sin, x1 * sin + x2 * cos], axis=-1)
        B, T, E = x.shape
        HD = HEADS_DIM
        H = E // HD
        half = HD // 2
        q = (x @ Wq + bq).reshape(B, T, H, HD).transpose(0, 2, 1, 3)
        k = (x @ Wk + bk).reshape(B, T, H, HD).transpose(0, 2, 1, 3)
        v = (x @ Wv + bv).reshape(B, T, H, HD).transpose(0, 2, 1, 3)
        q_content, q_spatial = (q[..., :half], q[..., half:])
        k_content, k_spatial = (k[..., :half], k[..., half:])
        base = jax.nn.sigmoid(nrope_freq[0]) * SDT_L + MIN_L * BASE_FREQUENCY
        rng = ARM_ATTENTION * jnp.pi
        q_spatial = _nrope(q_spatial.reshape(B * H, T, half), base, rng).reshape(B, H, T, half)
        k_spatial = _nrope(k_spatial.reshape(B * H, T, half), base, rng).reshape(B, H, T, half)
        q = jnp.concatenate([q_content, q_spatial], axis=-1)
        k = jnp.concatenate([k_content, k_spatial], axis=-1)
        score = jnp.einsum('bhqd,bhkd->bhqk', q, k) / jnp.sqrt(jnp.float32(HD))
        attn = jax.nn.softmax(score, axis=-1)
        out = jnp.einsum('bhqk,bhkd->bhqd', attn, v)
        out = out.transpose(0, 2, 1, 3).reshape(B, T, E)
        return out @ Wo + bo

    def _L1_ffn_ref(x, W_r, W_k, W_v, mu_r, mu_k):
        import jax, jax.numpy as jnp
        import numpy as np
        DIM = 128

        def _reference_tuple_inner(x, W_r, W_k, W_v, mu_r, mu_k):
            B, T, C = x.shape
            x_prev = jnp.concatenate([jnp.zeros((B, 1, C), x.dtype), x[:, :-1, :]], axis=1)
            xr = mu_r * x + (1.0 - mu_r) * x_prev
            xk = mu_k * x + (1.0 - mu_k) * x_prev
            r = jax.nn.sigmoid(jnp.einsum('btc,dc->btd', xr, W_r))
            k = jnp.einsum('btc,dc->btd', xk, W_k)
            k_act = jnp.square(jax.nn.relu(k))
            out = r * jnp.einsum('btc,dc->btd', k_act, W_v)
            new_state = x[:, -1, :]
            return (out, new_state)
        return _reference_tuple_inner(x, W_r, W_k, W_v, mu_r, mu_k)[0]
    x = L0_attn_hidden
    x = x + _L0_attn_ref(_layernorm(x, axis=-1), L0_attn_Wq, L0_attn_Wk, L0_attn_Wv, L0_attn_conv_q, L0_attn_conv_k, L0_attn_conv_v, L0_attn_Wb, L0_attn_Wa, L0_attn_A_log, L0_attn_dt_bias, L0_attn_Wg, L0_attn_norm_w, L0_attn_Wo)
    x = x + _L0_ffn_ref(_layernorm(x, axis=-1), L0_ffn_w_router, L0_ffn_w_up, L0_ffn_w_gate, L0_ffn_w_down, L0_ffn_ws_up, L0_ffn_ws_gate, L0_ffn_ws_down)
    x = x + _L1_attn_ref(_layernorm(x, axis=-1), L1_attn_Wq, L1_attn_bq, L1_attn_Wk, L1_attn_bk, L1_attn_Wv, L1_attn_bv, L1_attn_Wo, L1_attn_bo, L1_attn_nrope_freq)
    x = x + _L1_ffn_ref(_layernorm(x, axis=-1), L1_ffn_W_r, L1_ffn_W_k, L1_ffn_W_v, L1_ffn_mu_r, L1_ffn_mu_k)
    return x

_drawn_inputs = setup_inputs


def setup_inputs(seed=0):
    import zlib

    import numpy as np

    out = dict(_drawn_inputs(seed))
    spreads = {'L0_attn_norm_w': (1.0, 0.6),
     'L1_attn_bq': (0.0, 0.8),
     'L1_attn_bk': (0.0, 2.0),
     'L1_attn_bv': (0.0, 0.325),
     'L1_attn_bo': (0.0, 0.1)}
    factors = {'L0_attn_Wb': 8.0,
     'L0_attn_Wa': 8.0,
     'L0_attn_A_log': 8.0,
     'L0_attn_dt_bias': 8.0,
     'L0_ffn_w_router': 2.937,
     'L0_ffn_w_up': 2.781,
     'L0_ffn_w_gate': 2.881,
     'L0_ffn_w_down': 2.794,
     'L1_attn_Wq': 8.0,
     'L1_attn_Wk': 8.0,
     'L1_attn_Wv': 8.0,
     'L1_ffn_W_r': 3.132,
     'L1_ffn_mu_r': 6.215}
    for name, (base, spread) in spreads.items():
        noise = np.random.default_rng([zlib.crc32(name.encode()), seed]).standard_normal(out[name].shape)
        drawn = base * np.exp(spread * noise) if base else spread * noise
        out[name] = jnp.asarray(drawn.astype(out[name].dtype))
    for name, factor in factors.items():
        out[name] = (out[name] * factor).astype(out[name].dtype)
    return out
```

```python
from contextlib import ExitStack

import numpy as np

import concourse.bass as bass
from concourse import mybir

F32 = mybir.dt.float32
I32 = mybir.dt.int32
ALU = mybir.AluOpType
ACT = mybir.ActivationFunctionType
AX_X = mybir.AxisListType.X

P = 128
BANK = 512


class Core:

    def __init__(self, nc, ctx):
        self.nc, self.ctx, self.sems = nc, ctx, []

    def sb(self, name, shape, dt=F32, ctx=None):
        return (ctx or self.ctx).enter_context(self.nc.sbuf_tensor(name, shape, dt))

    def sem(self, name):
        self.sems.append(self.nc.alloc_semaphore(name))
        return self.sems[-1]

    def end_layer_part(self):
        self.nc.clear_and_free_semaphores(self.sems)
        self.nc.all_engine_barrier()
        self.sems = []


def bc(ap, axis, n):
    shape = list(ap.shape)
    shape.insert(axis, n)
    return ap.unsqueeze(axis).to_broadcast(shape)


def delta_in(core, g, din):
    nc, B, T = core.nc, g.B, g.T
    TB = T // P
    bank = g.bank
    with ExitStack() as ctx:
        sb = lambda n, s, dt=F32: core.sb(n, s, dt, ctx)
        w_rows = sb("A_w_rows", [P, 5, P])
        wba_rows = sb("A_wba_rows", [2 * g.NH, P])
        conv = sb("A_conv", [P, 3, g.KC])
        taps = sb("A_taps", [P, 3 * g.KC, P])
        wT = sb("A_wT", [P, 3 * g.KC + 1, P])
        wbaT = sb("A_wbaT", [P, 2 * g.NH])
        stats = sb("A_stats", [P, g.NT, 6])
        mv = sb("A_mv", [P, g.NT, 2])
        std = sb("A_std", [P, g.NT])
        rstd = sb("A_rstd", [P, g.NT])
        x = sb("A_x", [P, g.NT, P])
        xn = sb("A_xn", [P, g.NT, P])
        xnT = sb("A_xnT", [P, B, g.KC - 1 + T])
        proj = sb("A_proj", [P, 6, T])
        ab = sb("A_ab", [2 * g.NH, 2, T])

        s_x, s_w, s_small, s_id = core.sem("A_x_loaded"), core.sem("A_w_loaded"), core.sem("A_small_loaded"), core.sem("A_identity")
        s_st, s_mv, s_std, s_rstd = (core.sem("A_" + n) for n in ("stats", "mv", "std", "rstd"))
        s_xn, s_tr, s_ev, s_pad = (core.sem("A_" + n) for n in ("xn", "tr", "evac", "pad"))
        s_tap, s_wtr, s_wev = (core.sem("A_" + n) for n in ("tap", "wtr", "wevac"))
        s_mm, s_act, s_abc = (core.sem("A_" + n) for n in ("mm", "act", "abcopy"))
        s_outs = [core.sem(f"A_moved{i}") for i in range(6)]
        s_abm = [core.sem(f"A_abmoved{i}") for i in range(2)]

        x_rows_dram = g.x_dram.rearrange("b t c -> (b t) c").rearrange("(n p) c -> p n c", p=P)
        HALF = g.NT // 2
        NOUT = 5

        with nc.Block() as block:

            @block.sync
            def _(sp):
                for i in range(2):
                    sp.dma_start(x[:, i * HALF:(i + 1) * HALF, :],
                                 x_rows_dram[:, i * HALF:(i + 1) * HALF, :]).then_inc(s_x, 16)
                for i, n in enumerate(("Wq", "Wk", "Wv", "Wg", "Wo")):
                    sp.dma_start(w_rows[:, i, :], din["L0_attn_" + n]).then_inc(s_w, 16)
                sp.dma_start(wba_rows[0:g.NH, :], din["L0_attn_Wb"]).then_inc(s_w, 16)
                sp.dma_start(wba_rows[g.NH:, :], din["L0_attn_Wa"]).then_inc(s_w, 16)
                for i, n in enumerate("qkv"):
                    sp.dma_start(conv[:, i, :], din["L0_attn_conv_" + n]).then_inc(s_w, 16)
                for dst, n, times in ((g.norm_w, "norm_w", g.NH), (g.A_log, "A_log", B), (g.dt_bias, "dt_bias", B)):
                    sp.dma_start(dst[:, :], bc(din["L0_attn_" + n], 0, times)).then_inc(s_small, 16)
                for b in range(B):
                    rows = slice(b * g.NH, (b + 1) * g.NH)
                    for i, dst in enumerate((g.q, g.k, g.v)):
                        n = b * 3 + i
                        sp.wait_ge(s_act, b * 4 + i + 1)
                        sp.dma_start(dst[rows, :, :], proj[:, n % 6, :]).then_inc(s_outs[n % 6], 16)
                    sp.wait_ge(s_abc, b + 1)
                    sp.dma_start(g.beta[rows, :], ab[0:g.NH, b % 2, :]).then_inc(s_abm[b % 2], 16)
                    sp.dma_start(g.z[rows, :], ab[g.NH:, b % 2, :]).then_inc(s_abm[b % 2], 16)
                sp.wait_ge(s_small, 16 * 3)
                for s in s_outs:
                    sp.wait_ge(s, 16 * (3 * B // 6))
                for s in s_abm:
                    sp.wait_ge(s, 16 * B)

            @block.gpsimd
            def _(pool):
                nc.gpsimd.memset(g.ident[:, :], 0.0).then_inc(s_pad, 1)
                pool.wait_ge(s_pad, 1)
                nc.gpsimd.affine_select(out=g.ident[:, :], in_=g.ident[:, :], compare_op=ALU.not_equal,
                                        fill=1.0, base=0, pattern=[[-1, P]],
                                        channel_multiplier=1).then_inc(s_id, 1)
                nc.gpsimd.memset(xnT[:, :, 0:g.KC - 1], 0.0).then_inc(s_pad, 1)

            @block.vector
            def _(dve):
                dve.wait_ge(s_x, 32)
                for t in range(g.NT):
                    nc.vector.bn_stats(stats[:, t, :], x[:, t, :]).then_inc(s_st, 1)
                for t in range(g.NT):
                    dve.wait_ge(s_st, t + 1)
                    nc.vector.bn_aggr(mv[:, t, :], stats[:, t, :]).then_inc(s_mv, 1)
                dve.wait_ge(s_w, 16 * 10)
                for i in range(3):
                    for j in range(g.KC):
                        nc.vector.tensor_scalar(taps[:, i * g.KC + j, :], w_rows[:, i, :],
                                                conv[:, i, j:j + 1], None, ALU.mult).then_inc(s_tap, 1)
                dve.wait_ge(s_std, 1)
                nc.vector.reciprocal(rstd[:, :], std[:, :]).then_inc(s_rstd, 1)
                dve.wait_ge(s_rstd, 1)
                for t in range(g.NT):
                    nc.vector.tensor_scalar(xn[:, t, :], x[:, t, :], mv[:, t, 0:1], rstd[:, t:t + 1],
                                            ALU.subtract, ALU.mult).then_inc(s_xn, 1)
                for i in range(4):
                    dve.wait_ge(s_wtr, i + 1)
                    if i < 3:
                        nc.vector.tensor_copy(wT[:, i * 4:i * 4 + 4, :], bank(2 + i)).then_inc(s_wev, 1)
                    else:
                        nc.vector.tensor_copy(wT[:, 12, :], bank(5)[:, 0:P]).then_inc(s_wev, 1)
                        nc.vector.tensor_copy(g.woT[:, :], bank(5)[:, P:2 * P]).then_inc(s_wev, 1)
                        nc.vector.tensor_copy(wbaT[:, :], bank(5)[:, 2 * P:2 * P + 2 * g.NH]).then_inc(s_wev, 1)
                for b in range(B):
                    dve.wait_ge(s_mm, b * NOUT + NOUT)
                    if b >= 2:
                        dve.wait_ge(s_abm[b % 2], 32 * (b // 2))
                    nc.vector.tensor_copy(ab[:, b % 2, :],
                                          bank(2 + (b * NOUT + 4) % 6)[0:2 * g.NH, :]).then_inc(s_abc, 1)

            @block.scalar
            def _(act):
                act.wait_ge(s_mv, g.NT)
                nc.scalar.activation(std[:, :], mv[:, :, 1], ACT.Sqrt, bias=g.eps5[:, :]).then_inc(s_std, 1)
                for b in range(B):
                    act.wait_ge(s_tr, b + 1)
                    nc.scalar.copy(xnT[:, b, g.KC - 1:], bank(b % 2)).then_inc(s_ev, 1)
                for b in range(B):
                    for i in range(4):
                        n = b * NOUT + i
                        act.wait_ge(s_mm, n + 1)
                        if i < 3:
                            m = b * 3 + i
                            if m >= 6:
                                act.wait_ge(s_outs[m % 6], 16 * (m // 6))
                            dst = proj[:, m % 6, :]
                        else:
                            dst = g.gateT[:, b, :]
                        nc.scalar.activation(dst, bank(2 + n % 6), ACT.Silu).then_inc(s_act, 1)

            @block.tensor
            def _(pe):
                pe.wait_ge(s_id, 1)
                pe.wait_ge(s_w, 16 * 10)
                for i in range(3):
                    for j in range(g.KC):
                        n = i * g.KC + j
                        pe.wait_ge(s_tap, n + 1)
                        tr = nc.tensor.transpose(bank(2 + i)[:, j * P:(j + 1) * P], taps[:, n, :], g.ident[:, :])
                    tr.then_inc(s_wtr, 1)
                nc.tensor.transpose(bank(5)[:, 0:P], w_rows[:, 3, :], g.ident[:, :])
                nc.tensor.transpose(bank(5)[:, P:2 * P], w_rows[:, 4, :], g.ident[:, :])
                nc.tensor.transpose(bank(5)[:, 2 * P:2 * P + 2 * g.NH], wba_rows[:, :],
                                    g.ident[0:2 * g.NH, 0:2 * g.NH]).then_inc(s_wtr, 1)
                for b in range(B):
                    if b >= 2:
                        pe.wait_ge(s_ev, b - 1)
                    for t in range(TB):
                        pe.wait_ge(s_xn, b * TB + t + 1)
                        tr = nc.tensor.transpose(bank(b % 2)[:, t * P:(t + 1) * P], xn[:, b * TB + t, :],
                                                 g.ident[:, :])
                    tr.then_inc(s_tr, 1)
                pe.wait_ge(s_wev, 6)
                pe.wait_ge(s_pad, 2)
                for b in range(B):
                    pe.wait_ge(s_ev, b + 1)
                    for i in range(NOUT):
                        n = b * NOUT + i
                        if n >= 6:
                            m = n - 6
                            if m % NOUT == 4:
                                pe.wait_ge(s_abc, m // NOUT + 1)
                            else:
                                pe.wait_ge(s_act, m // NOUT * 4 + m % NOUT + 1)
                        o = bank(2 + n % 6)
                        if i < 3:
                            for j in range(g.KC):
                                mm = nc.tensor.matmul(o, wT[:, i * g.KC + j, :], xnT[:, b, j:j + T],
                                                      start=(j == 0), stop=(j == g.KC - 1))
                        elif i == 3:
                            mm = nc.tensor.matmul(o, wT[:, 12, :], xnT[:, b, g.KC - 1:], start=True, stop=True)
                        else:
                            mm = nc.tensor.matmul(o[0:2 * g.NH, :], wbaT[:, :], xnT[:, b, g.KC - 1:],
                                                  start=True, stop=True)
                        mm.then_inc(s_mm, 1)


class Chain:

    def __init__(self, eng, sem):
        self.eng, self.sem, self.n = eng, sem, 0

    def __call__(self, ins):
        ins.then_inc(self.sem, 1)
        self.n += 1
        self.eng.wait_ge(self.sem, self.n)


def delta_rule(core, g):
    nc, T, D = core.nc, g.T, g.D
    C = 4
    N = T // C
    RB = 16
    with ExitStack() as ctx:
        sb = lambda n, s, dt=F32: core.sb(n, s, dt, ctx)
        kt = sb("B_kt", [P, D, N, C])
        S = sb("B_S", [P, N + 1, D * D])
        early = S[:, :, :].rearrange("p n x -> p (n x)")
        E = early[:, 0:C * T].rearrange("p (e t) -> p e t", e=C)
        G = early[:, C * T:2 * C * T].rearrange("p (e t) -> p e t", e=C)
        KK = early[:, 2 * C * T:3 * C * T].rearrange("p (n x) -> p n x", x=C * C)
        Gam = sb("B_Gam", [P, N])
        X = sb("B_X", [P, 2 * D, N, C])
        QK = sb("B_QK", [P, N, C * C])
        V = g.k[:, :, :].rearrange("p d t -> p (d t)").rearrange("p (n c v) -> p n c v", c=C, v=D)
        P1 = sb("B_P1", [P, 2 * RB, C, D, D + 1])
        P2 = sb("B_P2", [P, 2, D * D, C + 1])
        s512 = [sb(f"B_s{i}", [P, T])[:, :] for i in range(2)]
        s512 += [early[:, (3 * C + i) * T:(3 * C + i + 1) * T] for i in range(2)]
        s_dve, s_act, s_pool = core.sem("B_dve"), core.sem("B_act"), core.sem("B_pool")
        s_ru, s_r1, s_p2, s_r2, s_dec = (core.sem("B_" + n) for n in ("u_placed", "R1", "P2", "R2", "decayed"))
        s_p1 = core.sem("B_P1")
        s_sig, s_ea, s_ee, s_EE, s_sq, s_rt = (core.sem("B_" + n) for n in ("sig", "ea", "ee", "EE", "sq", "rt"))
        s_z, s_G, s_ss, s_X, s_o, s_osq, s_ort = (core.sem("B_" + n) for n in ("z", "G", "ss", "X", "o", "osq", "ort"))

        q4 = g.q[:, :, :].rearrange("p d (n c) -> p d n c", c=C)
        k4 = g.k[:, :, :].rearrange("p d (n c) -> p d n c", c=C)
        v4 = g.v[:, :, :].rearrange("p d (n c) -> p d n c", c=C)
        o4 = g.o[:, :, :].rearrange("p d (n c) -> p d n c", c=C)
        E4 = E.rearrange("p e (n c) -> p e n c", c=C)
        G4 = G.rearrange("p e (n c) -> p e n c", c=C)
        b3 = g.beta[:, :].rearrange("p (n c) -> p n c", c=C)
        tmp = P1[:, :, :, :, :].rearrange("p a b c d -> p (a b c d)")
        sqk = tmp[:, 0:2 * D * T].rearrange("p (u d t) -> p u d t", u=2, d=D)

        with nc.Block() as block:

            def decay_blocks(act, lo, hi):
                for n in range(lo, hi):
                    act.wait_ge(s_r2, n + 1)
                    nc.scalar.activation(P2[:, n % 2, :, C], S[:, n, :], ACT.Copy,
                                         scale=Gam[:, n:n + 1]).then_inc(s_dec, 1)

            @block.scalar
            def _(act):
                nc.scalar.activation(sqk[:, 0], g.q[:, :, :], ACT.Square).then_inc(s_sq, 1)
                nc.scalar.activation(sqk[:, 1], g.k[:, :, :], ACT.Square).then_inc(s_sq, 1)
                nc.scalar.activation(g.beta[:, :], g.beta[:, :], ACT.Sigmoid).then_inc(s_sig, 1)
                act.wait_ge(s_z, 1)
                nc.scalar.activation(s512[1], s512[0], ACT.Exp).then_inc(s_ee, 1)
                nc.scalar.activation(g.A_log[:, :], g.A_log[:, :], ACT.Exp).then_inc(s_ea, 1)
                act.wait_ge(s_G, 1)
                nc.scalar.activation(E, G, ACT.Exp).then_inc(s_EE, 1)
                act.wait_ge(s_ss, 1)
                nc.scalar.activation(s512[2], s512[2], ACT.Sqrt, bias=g.eps6[:, :]).then_inc(s_rt, 1)
                nc.scalar.activation(s512[3], s512[3], ACT.Sqrt, bias=g.eps6[:, :]).then_inc(s_rt, 1)
                act.wait_ge(s_X, 1)
                act_pre = 0
                for m in range(N // RB):
                    if m >= 2:
                        act.wait_ge(s_r1, (m - 1) * RB)
                    for i in range(C):
                        nc.scalar.copy(P1[:, (m % 2) * RB:(m % 2) * RB + RB, i, :, D],
                                       X[:, D:2 * D, m * RB:(m + 1) * RB, i].rearrange("p v n -> p n v")
                                       ).then_inc(s_ru, 1)
                    if m == 0:
                        continue
                    decay_blocks(act, (m - 1) * RB, m * RB)
                decay_blocks(act, N - RB, N)
                act.wait_ge(s_o, 1)
                nc.scalar.activation(sqk[:, 0], g.o[:, :, :], ACT.Square).then_inc(s_osq, 1)
                act.wait_ge(s_ss, 2)
                nc.scalar.activation(s512[1], s512[0], ACT.Sqrt, scale=1.0 / D,
                                     bias=g.eps5[:, :]).then_inc(s_ort, 1)

            @block.vector
            def _(dve):
                do = Chain(dve, s_dve)
                v = nc.vector
                do(v.tensor_scalar(g.z[:, :], g.z[:, :], g.dt_bias[:, :], None, ALU.add))
                do(v.tensor_scalar(s512[0], g.z[:, :], -1.0, None, ALU.mult))
                v.tensor_tensor(s512[0], s512[0], g.z[:, :], ALU.min).then_inc(s_z, 1)
                dve.wait_ge(s_sq, 2)
                do(v.tensor_reduce(s512[2], sqk[:, 0].rearrange("p d t -> p t d"), AX_X, ALU.add))
                v.tensor_reduce(s512[3], sqk[:, 1].rearrange("p d t -> p t d"), AX_X, ALU.add).then_inc(s_ss, 1)
                dve.wait_ge(s_ee, 1)
                e, s, s2, p = s512[1], tmp[:, 0:T], tmp[:, T:2 * T], tmp[:, 2 * T:3 * T]
                do(v.tensor_scalar(s, e, 2.0, None, ALU.add))
                do(v.reciprocal(s, s))
                do(v.tensor_tensor(s, s, e, ALU.mult))
                do(v.tensor_tensor(s2, s, s, ALU.mult))
                do(v.tensor_scalar(p, s2, 2.0 / 17, None, ALU.mult))
                for c in (15, 13, 11, 9, 7, 5, 3):
                    do(v.scalar_tensor_tensor(out=p, in0=p, scalar=2.0 / c, in1=s2, op0=ALU.add, op1=ALU.mult))
                do(v.scalar_tensor_tensor(out=p, in0=p, scalar=2.0, in1=s, op0=ALU.add, op1=ALU.mult))
                do(v.scalar_tensor_tensor(out=p, in0=g.z[:, :], scalar=0.0, in1=p, op0=ALU.max, op1=ALU.add))
                dve.wait_ge(s_ea, 1)
                do(v.memset(G, 0.0))
                do(v.tensor_scalar(G[:, 0, :], p, g.A_log[:, :], -1.0, ALU.mult, ALU.mult))
                for d in range(1, C):
                    do(v.tensor_tensor(G4[:, d, :, d:C], G4[:, d - 1, :, d:C], G4[:, 0, :, 0:C - d], ALU.add))
                v.nop().then_inc(s_G, 1)
                dve.wait_ge(s_rt, 2)
                do(v.reciprocal(s512[2], s512[2]))
                do(v.reciprocal(s512[3], s512[3]))
                do(v.tensor_scalar(s512[2], s512[2], float(D) ** -0.5, None, ALU.mult))
                do(v.tensor_tensor(g.q[:, :, :], g.q[:, :, :], bc(s512[2], 1, D), ALU.mult))
                do(v.tensor_tensor(g.k[:, :, :], g.k[:, :, :], bc(s512[3], 1, D), ALU.mult))
                dve.wait_ge(s_EE, 1)
                dve.wait_ge(s_sig, 1)
                gam, nbg = s512[0], s512[1]
                gam3 = gam.rearrange("p (n c) -> p n c", c=C)
                for i in range(C):
                    do(v.tensor_copy(gam3[:, :, i], E4[:, i, :, i]))
                do(v.scalar_tensor_tensor(out=nbg, in0=gam, scalar=-1.0, in1=g.beta[:, :],
                                          op0=ALU.mult, op1=ALU.mult))
                do(v.tensor_tensor(X[:, 0:D, :, :].rearrange("p d n c -> p d (n c)"), g.k[:, :, :],
                                   bc(nbg, 1, D), ALU.mult))
                do(v.tensor_tensor(X[:, D:2 * D, :, :].rearrange("p d n c -> p d (n c)"), g.v[:, :, :],
                                   bc(g.beta[:, :], 1, D), ALU.mult))
                for i in range(C):
                    if i == C - 1:
                        do(v.tensor_copy(kt[:, :, :, i], k4[:, :, :, i]))
                    else:
                        do(v.tensor_tensor(kt[:, :, :, i], k4[:, :, :, i],
                                           bc(E4[:, C - 2 - i, :, C - 1], 1, D), ALU.mult))
                do(v.memset(QK[:, :, :], 0.0))
                for d in range(C):
                    w = C - d
                    pr = tmp[:, 0:N * w * D].rearrange("p (n i d) -> p n i d", n=N, i=w)
                    for first, coef, start in ((q4, QK, 0), (k4, KK, 1)):
                        if d < start:
                            continue
                        diag = coef[:, :, d * C::C + 1]
                        for i in range(w):
                            do(v.tensor_tensor(pr[:, :, i, :], first[:, :, :, i + d].rearrange("p d n -> p n d"),
                                               k4[:, :, :, i].rearrange("p d n -> p n d"), ALU.mult))
                        do(v.tensor_reduce(diag, pr, AX_X, ALU.add))
                        if d > 0:
                            do(v.tensor_tensor(diag, diag, E4[:, d - 1, :, d:C], ALU.mult))
                        if start:
                            do(v.scalar_tensor_tensor(out=diag, in0=diag, scalar=-1.0, in1=b3[:, :, d:C],
                                                      op0=ALU.mult, op1=ALU.mult))
                for i in range(1, C):
                    pr = tmp[:, 0:N * 2 * D * i].rearrange("p (n x j) -> p n x j", n=N, x=2 * D)
                    sm = tmp[:, N * 6 * D:N * 8 * D].rearrange("p (n x) -> p n x", n=N)
                    do(v.tensor_tensor(pr, X[:, :, :, 0:i].rearrange("p x n j -> p n x j"),
                                       bc(KK[:, :, i * C:i * C + i], 2, 2 * D), ALU.mult))
                    do(v.tensor_reduce(sm, pr, AX_X, ALU.add))
                    do(v.tensor_tensor(X[:, :, :, i], X[:, :, :, i], sm.rearrange("p n x -> p x n"), ALU.add))
                do(v.tensor_tensor(g.q[:, :, :], g.q[:, :, :], bc(gam, 1, D), ALU.mult))
                do(v.tensor_copy(Gam[:, :], E4[:, C - 1, :, C - 1]))
                v.memset(S[:, 0, :], 0.0).then_inc(s_r2, 1)
                v.nop().then_inc(s_X, 1)
                for n in range(N):
                    r = n % (2 * RB)
                    if n % RB == 0:
                        dve.wait_ge(s_ru, C * (n // RB + 1))
                    dve.wait_ge(s_r2, n + 1)
                    v.tensor_tensor(P1[:, r, :, :, 0:D], bc(S[:, n, :].rearrange("p (v k) -> p v k", k=D), 1, C),
                                    bc(X[:, 0:D, n, :].rearrange("p k c -> p c k"), 2, D),
                                    ALU.mult).then_inc(s_p1, 1)
                    dve.wait_ge(s_p1, n + 1)
                    v.tensor_reduce(V[:, n, :, :], P1[:, r, :, :, :], AX_X, ALU.add).then_inc(s_r1, 1)
                    dve.wait_ge(s_r1, n + 1)
                    v.tensor_tensor(P2[:, n % 2, :, 0:C].rearrange("p (v k) c -> p v k c", k=D),
                                    bc(V[:, n, :, :].rearrange("p c v -> p v c"), 2, D),
                                    bc(kt[:, :, n, :], 1, D), ALU.mult).then_inc(s_p2, 1)
                    dve.wait_ge(s_p2, n + 1)
                    dve.wait_ge(s_dec, n + 1)
                    v.tensor_reduce(S[:, n + 1, :], P2[:, n % 2, :, :], AX_X, ALU.add).then_inc(s_r2, 1)
                dve.wait_ge(s_r2, N + 1)
                HB = RB
                for n0 in range(0, N, HB):
                    for i in range(C):
                        pr = tmp[:, 0:HB * D * (D + i + 1)].rearrange("p (n v x) -> p n v x", n=HB, v=D)
                        do(v.tensor_tensor(pr[:, :, :, 0:D],
                                           S[:, n0:n0 + HB, :].rearrange("p n (v k) -> p n v k", k=D),
                                           bc(q4[:, :, n0:n0 + HB, i].rearrange("p d n -> p n d"), 2, D), ALU.mult))
                        do(v.tensor_tensor(pr[:, :, :, D:D + i + 1],
                                           V[:, n0:n0 + HB, 0:i + 1, :].rearrange("p n j v -> p n v j"),
                                           bc(QK[:, n0:n0 + HB, i * C:i * C + i + 1], 2, D), ALU.mult))
                        do(v.tensor_reduce(o4[:, :, n0:n0 + HB, i].rearrange("p v n -> p n v"), pr, AX_X, ALU.add))
                v.nop().then_inc(s_o, 1)
                dve.wait_ge(s_osq, 1)
                v.tensor_reduce(s512[0], sqk[:, 0].rearrange("p d t -> p t d"), AX_X, ALU.add).then_inc(s_ss, 1)
                dve.wait_ge(s_ort, 1)
                do(v.reciprocal(s512[1], s512[1]))
                do(v.tensor_tensor(g.o[:, :, :], g.o[:, :, :], bc(s512[1], 1, D), ALU.mult))


def delta_out(core, g):
    nc = core.nc
    T, B = g.T, g.B
    with ExitStack() as ctx:
        oT = core.sb("C_oT", [P, B, T], F32, ctx)
        zero = core.sb("C_zero", [P, P], F32, ctx)
        s_x, s_zero, s_filled = core.sem("C_x_loaded"), core.sem("C_zero"), core.sem("C_filled")
        s_oT = [core.sem(f"C_oT{b}") for b in range(B)]
        s_g, s_mm, s_add = (core.sem("C_" + n) for n in ("gated", "mm", "added"))
        with nc.Block() as block:

            @block.gpsimd
            def _(pool):
                nc.gpsimd.memset(zero[:, :], 0.0).then_inc(s_zero, 1)
                pool.wait_ge(s_zero, 1)
                pool.dma_start(g.sorted_x.rearrange("(n p) c -> p n c", p=P),
                               bc(zero[:, :], 1, g.sorted_x.shape[0] // P)).then_inc(s_filled, 16)
                pool.wait_ge(s_filled, 16)

            @block.sync
            def _(sp):
                sp.dma_start(g.x[:, :, :], g.x_dram.rearrange("b t c -> (b t) c").rearrange(
                    "(n p) c -> p n c", p=P)).then_inc(s_x, 16)
                for b in range(B):
                    sp.dma_start(oT[:, b, :], g.o[b * g.NH:(b + 1) * g.NH, :, :]).then_inc(s_oT[b], 16)

            @block.vector
            def _(dve):
                for b in range(B):
                    dve.wait_ge(s_oT[b], 16)
                    nc.vector.scalar_tensor_tensor(out=oT[:, b, :], in0=oT[:, b, :], scalar=g.norm_w[:, :],
                                                   in1=g.gateT[:, b, :], op0=ALU.mult, op1=ALU.mult).then_inc(s_g, 1)
                dve.wait_ge(s_x, 16)
                for b in range(B):
                    dve.wait_ge(s_mm, b + 1)
                    xb = g.x[:, b * 4:b * 4 + 4, :].rearrange("p a c -> p (a c)")
                    nc.vector.tensor_tensor(xb, xb, g.bank(b), ALU.add).then_inc(s_add, 1)

            @block.tensor
            def _(pe):
                for b in range(B):
                    pe.wait_ge(s_g, b + 1)
                    for t in range(4):
                        mm = nc.tensor.matmul(g.bank(b)[:, t * P:(t + 1) * P], oT[:, b, t * P:(t + 1) * P],
                                              g.woT[:, :], start=True, stop=True)
                    mm.then_inc(s_mm, 1)


def layer_norm(core, g, name, xn, xT, pad):
    nc, TB = core.nc, g.T // P
    with ExitStack() as ctx:
        stats = core.sb(name + "_stats", [P, g.NT, 6], F32, ctx)
        mv = core.sb(name + "_mv", [P, g.NT, 2], F32, ctx)
        rstd = core.sb(name + "_rstd", [P, g.NT], F32, ctx)
        s_st, s_mv, s_std, s_rstd, s_xn, s_tr, s_ev, s_pad = (
            core.sem(f"{name}_{n}") for n in ("stats", "mv", "std", "rstd", "xn", "tr", "evac", "pad"))
        with nc.Block() as block:

            @block.gpsimd
            def _(pool):
                if pad:
                    nc.gpsimd.memset(xT[:, :, 0:pad], 0.0).then_inc(s_pad, 1)

            @block.vector
            def _(dve):
                for t in range(g.NT):
                    nc.vector.bn_stats(stats[:, t, :], g.x[:, t, :]).then_inc(s_st, 1)
                for t in range(g.NT):
                    dve.wait_ge(s_st, t + 1)
                    nc.vector.bn_aggr(mv[:, t, :], stats[:, t, :]).then_inc(s_mv, 1)
                dve.wait_ge(s_std, 1)
                nc.vector.reciprocal(rstd[:, :], rstd[:, :]).then_inc(s_rstd, 1)
                dve.wait_ge(s_rstd, 1)
                for t in range(g.NT):
                    nc.vector.tensor_scalar(xn[:, t, :], g.x[:, t, :], mv[:, t, 0:1], rstd[:, t:t + 1],
                                            ALU.subtract, ALU.mult).then_inc(s_xn, 1)

            @block.scalar
            def _(act):
                act.wait_ge(s_mv, g.NT)
                nc.scalar.activation(rstd[:, :], mv[:, :, 1], ACT.Sqrt, bias=g.eps5[:, :]).then_inc(s_std, 1)
                for b in range(g.B):
                    act.wait_ge(s_tr, b + 1)
                    nc.scalar.copy(xT[:, b, pad:], g.bank(b)).then_inc(s_ev, 1)

            @block.tensor
            def _(pe):
                for b in range(g.B):
                    for t in range(TB):
                        pe.wait_ge(s_xn, b * TB + t + 1)
                        tr = nc.tensor.transpose(g.bank(b)[:, t * P:(t + 1) * P], xn[:, b * TB + t, :],
                                                 g.ident[:, :])
                    tr.then_inc(s_tr, 1)


def moe(core, g, din):
    nc, T, B, NT = core.nc, g.T, g.B, g.NT
    E = din["L0_ffn_w_router"].shape[1]
    NX = E - 1
    HID = din["L0_ffn_ws_up"].shape[1]
    HC = HID // P
    NS = (NT * P + E * (P - 1)) // P
    ALPHA = 2.0
    with ExitStack() as ctx:
        sb = lambda n, s, dt=F32: core.sb(n, s, dt, ctx)
        xn, xT = sb("M_xn", [P, NT, P]), sb("M_xT", [P, B, T])
        layer_norm(core, g, "M_ln", xn, xT, 0)
        w_up, w_gate = sb("M_w_up", [P, NX * HID]), sb("M_w_gate", [P, NX * HID])
        w_down = sb("M_w_down", [P, NX * HC * P])
        ws_up, ws_gate, ws_down = sb("M_ws_up", [P, HID]), sb("M_ws_gate", [P, HID]), sb("M_ws_down", [P, HC, P])
        w_r = sb("M_w_router", [P, E])
        weight = sb("M_weight", [P, NT])
        slot = sb("M_slot", [P, NT], I32)
        tile_expert = sb("M_tile_expert", [1, NS], I32)
        s_wr, s_ws, s_wx = (core.sem("M_" + n) for n in ("router_loaded", "shared_loaded", "experts_loaded"))
        with ExitStack() as rctx:
            rb = lambda n, s, dt=F32: core.sb(n, s, dt, rctx)
            route(core, g, din, rb, xT, w_r, weight, slot, tile_expert, E, NS, ALPHA, s_wr)
        experts(core, g, din, sb, xn, xT, w_up, w_gate, w_down, ws_up, ws_gate, ws_down,
                slot, tile_expert, weight, NX, HID, HC, NS, s_ws, s_wx)


def route(core, g, din, rb, xT, w_r, weight, slot, tile_expert, E, NS, ALPHA, s_wr):
    nc, NT, T = core.nc, g.NT, g.T
    lg, oh = rb("R_logits", [P, NT, E]), rb("R_onehot", [P, NT, E])
    ex, rank = rb("R_exp", [P, NT, E]), rb("R_rank", [P, NT, E])
    cum = [rb(f"R_cum{i}", [P, NT, E]) for i in range(2)]
    tot = rb("R_tot", [P, NT, E])
    mx, best, slot_f = rb("R_max", [P, NT]), rb("R_best", [P, NT]), rb("R_slot_f", [P, NT])
    iota_e, iota_t = rb("R_iota_e", [P, E]), rb("R_iota_t", [P, NS])
    low, ones = rb("R_lower", [P, P]), rb("R_ones", [P, P])
    big = rb("R_big", [P, E, NS])
    big2 = rb("R_big2", [P, NS, E])
    nt, end = rb("R_ntiles", [P, E]), [rb(f"R_end{i}", [P, E]) for i in range(2)]
    te = rb("R_te", [P, NS])
    s_c, s_lg, s_ex, s_sub, s_oh, s_cnt, s_dve = (
        core.sem("R_" + n) for n in ("const", "logits", "exp", "sub", "onehot", "count", "dve"))
    with nc.Block() as block:

        @block.sync
        def _(sp):
            sp.dma_start(w_r[:, :], din["L0_ffn_w_router"]).then_inc(s_wr, 16)
            sp.wait_ge(s_wr, 16)

        @block.gpsimd
        def _(pool):
            nc.gpsimd.iota(iota_e[:, :], [[1, E]], base=-E, channel_multiplier=0,
                           allow_small_or_imprecise_dtypes=True).then_inc(s_c, 1)
            nc.gpsimd.iota(iota_t[:, :], [[1, NS]], base=0, channel_multiplier=0,
                           allow_small_or_imprecise_dtypes=True).then_inc(s_c, 1)
            nc.gpsimd.memset(ones[:, :], 1.0).then_inc(s_c, 1)
            pool.wait_ge(s_c, 3)
            nc.gpsimd.affine_select(out=low[:, :], in_=ones[:, :], compare_op=ALU.is_gt, fill=0.0, base=0,
                                    pattern=[[1, P]], channel_multiplier=-1).then_inc(s_c, 1)

        @block.tensor
        def _(pe):
            pe.wait_ge(s_wr, 16)
            for t in range(NT):
                b, o = t // 4, t % 4 * P
                mm = nc.tensor.matmul(g.bank(0)[:, t * E:(t + 1) * E], xT[:, b, o:o + P], w_r[:, :],
                                      start=True, stop=True)
            mm.then_inc(s_lg, 1)
            pe.wait_ge(s_c, 4)
            pe.wait_ge(s_oh, 1)
            ohf = oh[:, :, :].rearrange("p t e -> p (t e)")
            nc.tensor.matmul(g.bank(1)[:, 0:NT * E], low[:, :], ohf, start=True, stop=True).then_inc(s_cnt, 1)
            nc.tensor.matmul(g.bank(2)[:, 0:NT * E], ones[:, :], ohf, start=True, stop=True).then_inc(s_cnt, 1)

        @block.scalar
        def _(act):
            act.wait_ge(s_sub, 1)
            nc.scalar.activation(ex[:, :, :], ex[:, :, :], ACT.Exp).then_inc(s_ex, 1)

        @block.vector
        def _(dve):
            v, do = nc.vector, Chain(dve, s_dve)
            dve.wait_ge(s_lg, 1)
            do(v.tensor_copy(lg[:, :, :].rearrange("p t e -> p (t e)"), g.bank(0)[:, 0:NT * E]))
            do(v.tensor_reduce(mx[:, :], lg[:, :, :], AX_X, ALU.max))
            v.tensor_tensor(ex[:, :, :], lg[:, :, :], bc(mx[:, :], 2, E), ALU.subtract).then_inc(s_sub, 1)
            do(v.tensor_tensor(oh[:, :, :], lg[:, :, :], bc(mx[:, :], 2, E), ALU.is_equal))
            dve.wait_ge(s_c, 4)
            do(v.tensor_tensor(oh[:, :, :], oh[:, :, :], bc(iota_e[:, :], 1, NT), ALU.mult))
            do(v.tensor_reduce(best[:, :], oh[:, :, :], AX_X, ALU.min))
            v.tensor_tensor(oh[:, :, :], bc(iota_e[:, :], 1, NT), bc(best[:, :], 2, E),
                            ALU.is_equal).then_inc(s_oh, 1)
            dve.wait_ge(s_oh, 1)
            dve.wait_ge(s_ex, 1)
            do(v.tensor_reduce(weight[:, :], ex[:, :, :], AX_X, ALU.add))
            do(v.reciprocal(weight[:, :], weight[:, :]))
            do(v.tensor_scalar(best[:, :], best[:, :], -1.0, ALPHA, ALU.is_lt, ALU.mult))
            do(v.tensor_tensor(weight[:, :], weight[:, :], best[:, :], ALU.mult))
            dve.wait_ge(s_cnt, 2)
            do(v.tensor_copy(rank[:, :, :].rearrange("p t e -> p (t e)"), g.bank(1)[:, 0:NT * E]))
            do(v.tensor_copy(tot[:, :, :].rearrange("p t e -> p (t e)"), g.bank(2)[:, 0:NT * E]))
            src, i, w = tot, 0, 1
            while w < NT:
                dst = cum[i % 2]
                do(v.tensor_copy(dst[:, 0:w, :], src[:, 0:w, :]))
                do(v.tensor_tensor(dst[:, w:, :], src[:, w:, :], src[:, 0:NT - w, :], ALU.add))
                src, i, w = dst, i + 1, 2 * w
            do(v.tensor_scalar(te[:, :], iota_t[:, :], float(P), None, ALU.mult))
            do(v.tensor_tensor(big[:, :, :], bc(src[:, NT - 1, :], 2, NS), bc(te[:, :], 1, E), ALU.is_gt))
            do(v.tensor_reduce(nt[:, :], big[:, :, :], AX_X, ALU.add))
            esrc, i, w = nt, 0, 1
            while w < E:
                dst = end[i % 2]
                do(v.tensor_copy(dst[:, 0:w], esrc[:, 0:w]))
                do(v.tensor_tensor(dst[:, w:], esrc[:, w:], esrc[:, 0:E - w], ALU.add))
                esrc, i, w = dst, i + 1, 2 * w
            do(v.tensor_tensor(big2[:, :, :], bc(esrc[:, :], 1, NS), bc(iota_t[:, :], 2, E), ALU.is_le))
            do(v.tensor_reduce(te[:, :], big2[:, :, :], AX_X, ALU.add))
            do(v.tensor_scalar(te[:, :], te[:, :], float(E - 2), None, ALU.min))
            do(v.tensor_copy(tile_expert[:, :], te[0:1, :]))
            do(v.tensor_tensor(nt[:, :], esrc[:, :], nt[:, :], ALU.subtract))
            do(v.tensor_scalar(nt[:, :], nt[:, :], float(P), None, ALU.mult))
            do(v.tensor_tensor(rank[:, :, :], rank[:, :, :], src[:, :, :], ALU.add))
            do(v.tensor_tensor(rank[:, :, :], rank[:, :, :], tot[:, :, :], ALU.subtract))
            do(v.tensor_tensor(rank[:, :, :], rank[:, :, :], bc(nt[:, :], 1, NT), ALU.add))
            do(v.tensor_tensor(rank[:, :, :], rank[:, :, :], oh[:, :, :], ALU.mult))
            do(v.tensor_reduce(slot_f[:, :], rank[:, :, :], AX_X, ALU.add))
            do(v.tensor_copy(slot[:, :], slot_f[:, :]))


def experts(core, g, din, sb, xn, xT, w_up, w_gate, w_down, ws_up, ws_gate, ws_down,
            slot, tile_expert, weight, NX, HID, HC, NS, s_ws, s_wx):
    nc, T, B, NT = core.nc, g.T, g.B, g.NT
    bank = g.bank
    NG = (NS + 3) // 4
    xd = sb("X_xd", [P, NG * 4, P])
    xdT = sb("X_xdT", [P, 2, 4 * P])
    sg = sb("X_sg", [P, 2, T])
    hT = sb("X_hT", [P, 2, HC, T])
    h = sb("X_h", [P, 2, HID])
    eT = sb("X_eT", [P, 2, HC * P])
    s_sc, s_ld = core.sem("X_scattered"), core.sem("X_sorted_loaded")
    s_up, s_gt, s_silu, s_h, s_y, s_yadd = (core.sem("X_s_" + n) for n in ("up", "gate", "silu", "h", "y", "yadd"))
    s_xt, s_xe, s_eu, s_eg, s_es, s_eh, s_et, s_ee, s_ey, s_ye, s_yo, s_gi = (
        core.sem("X_e_" + n) for n in ("xT", "xT_evac", "up", "gate", "silu", "h", "hT", "hT_evac", "y",
                                       "y_evac", "y_written", "gathered"))
    xs_dram = g.sorted_x
    s_fin = core.sem("X_added")
    with nc.Block() as block:

        @block.sync
        def _(sp):
            sp.dma_start(ws_up[:, :], din["L0_ffn_ws_up"]).then_inc(s_ws, 16)
            sp.dma_start(ws_gate[:, :], din["L0_ffn_ws_gate"]).then_inc(s_ws, 16)
            sp.dma_start(ws_down[:, :, :], din["L0_ffn_ws_down"].rearrange("(c p) n -> p c n", p=P)).then_inc(s_ws, 16)
            sp.dma_start(w_up[:, :].rearrange("p (e n) -> p e n", e=NX),
                         din["L0_ffn_w_up"].rearrange("e p n -> p e n")).then_inc(s_wx, 16)
            sp.dma_start(w_gate[:, :].rearrange("p (e n) -> p e n", e=NX),
                         din["L0_ffn_w_gate"].rearrange("e p n -> p e n")).then_inc(s_wx, 16)
            sp.dma_start(w_down[:, :].rearrange("p (e n) -> p e n", e=NX * HC),
                         din["L0_ffn_w_down"].rearrange("e (c p) n -> p (e c) n", p=P)).then_inc(s_wx, 16)
            sp.wait_ge(s_sc, 16 * NT)
            sp.dma_start(xd[:, :, :], xs_dram.rearrange("(n p) c -> p n c", p=P)).then_inc(s_ld, 16)
            for j in range(NS):
                sp.wait_ge(s_ye, j + 1)
                sp.dma_start(g.sorted_y[j * P:(j + 1) * P, :], xd[:, j, :]).then_inc(s_yo, 16)
            sp.wait_ge(s_yo, 16 * NS)

        @block.gpsimd
        def _(pool):
            for t in range(NT):
                nc.gpsimd.indirect_dma_start(xs_dram, bass.IndirectOffsetOnAxis(slot[:, t:t + 1], 0),
                                             xn[:, t, :], None).then_inc(s_sc, 16)
            pool.wait_ge(s_sc, 16 * NT)
            pool.wait_ge(s_yo, 16 * NS)
            for t in range(NT):
                nc.gpsimd.indirect_dma_start(xn[:, t, :], None, g.sorted_y[0:NS * P, :],
                                             bass.IndirectOffsetOnAxis(slot[:, t:t + 1], 0)).then_inc(s_gi, 16)
            pool.wait_ge(s_gi, 16 * NT)

        @block.tensor
        def _(pe):
            pe.wait_ge(s_ws, 48)

            def shared_down(b):
                pe.wait_ge(s_h, (b + 1) * HC)
                if b >= 2:
                    pe.wait_ge(s_yadd, b - 1)
                for t in range(T // P):
                    for c in range(HC):
                        mm = nc.tensor.matmul(bank(4 + b % 2)[:, t * P:(t + 1) * P],
                                              hT[:, b % 2, c, t * P:(t + 1) * P], ws_down[:, c, :],
                                              start=(c == 0), stop=(c == HC - 1))
                mm.then_inc(s_y, 1)

            for b in range(B):
                for c in range(HC):
                    n = b * HC + c
                    if n >= 2:
                        pe.wait_ge(s_h, n - 1)
                    nc.tensor.matmul(bank(n % 2), ws_up[:, c * P:(c + 1) * P], xT[:, b, :],
                                     start=True, stop=True).then_inc(s_up, 1)
                    nc.tensor.matmul(bank(2 + n % 2), ws_gate[:, c * P:(c + 1) * P], xT[:, b, :],
                                     start=True, stop=True).then_inc(s_gt, 1)
                if b >= 1:
                    shared_down(b - 1)
            shared_down(B - 1)
            pe.wait_ge(s_h, B * HC)
            pe.wait_ge(s_yadd, B)
            pe.wait_ge(s_ld, 16)
            pe.wait_ge(s_wx, 48)

            def x_columns(q):
                if q >= 1:
                    pe.wait_ge(s_xe, q)
                for t in range(4):
                    tr = nc.tensor.transpose(bank(4)[:, t * P:(t + 1) * P], xd[:, q * 4 + t, :], g.ident[:, :])
                tr.then_inc(s_xt, 1)

            def h_columns(j):
                pe.wait_ge(s_eh, j + 1)
                if j >= 2:
                    pe.wait_ge(s_ee, j - 1)
                for c in range(HC):
                    tr = nc.tensor.transpose(bank(5 + j % 2)[:, c * P:(c + 1) * P], h[:, j % 2, c * P:(c + 1) * P],
                                             g.ident[:, :])
                tr.then_inc(s_et, 1)

            def down(j, e):
                pe.wait_ge(s_ee, j + 1)
                if j >= 1:
                    pe.wait_ge(s_ye, j)
                for c in range(HC):
                    mm = nc.tensor.matmul(bank(7)[:, 0:P], eT[:, j % 2, c * P:(c + 1) * P],
                                          w_down[:, bass.ds(e * (HC * P) + c * P, P)],
                                          start=(c == 0), stop=(c == HC - 1))
                mm.then_inc(s_ey, 1)

            x_columns(0)
            experts_of = {}
            for j in range(NS):
                if j % 4 == 0 and j // 4 + 1 < NG:
                    if j >= 4:
                        pe.wait_ge(s_ey, j - 2)
                    x_columns(j // 4 + 1)
                e = pe.value_load(tile_expert[0:1, j:j + 1], min_val=0, max_val=NX - 1)
                experts_of[j] = e
                pe.wait_ge(s_xe, j // 4 + 1)
                if j >= 2:
                    pe.wait_ge(s_eh, j - 1)
                xc = xdT[:, (j // 4) % 2, (j % 4) * P:(j % 4 + 1) * P]
                nc.tensor.matmul(bank(j % 2), xc, w_up[:, bass.ds(e * HID, HID)], start=True, stop=True).then_inc(s_eu, 1)
                nc.tensor.matmul(bank(2 + j % 2), xc, w_gate[:, bass.ds(e * HID, HID)], start=True,
                                 stop=True).then_inc(s_eg, 1)
                if j >= 1:
                    h_columns(j - 1)
                if j >= 2:
                    down(j - 2, experts_of[j - 2])
            h_columns(NS - 1)
            down(NS - 2, experts_of[NS - 2])
            down(NS - 1, experts_of[NS - 1])

        @block.scalar
        def _(act):
            for n in range(B * HC):
                act.wait_ge(s_gt, n + 1)
                if n >= 2:
                    act.wait_ge(s_h, n - 1)
                nc.scalar.activation(sg[:, n % 2, :], bank(2 + n % 2), ACT.Silu).then_inc(s_silu, 1)
            act.wait_ge(s_h, B * HC)

            def x_evac(q):
                act.wait_ge(s_xt, q + 1)
                if q >= 2:
                    act.wait_ge(s_eg, (q - 1) * 4)
                nc.scalar.copy(xdT[:, q % 2, :], bank(4)).then_inc(s_xe, 1)

            def y_evac(j):
                act.wait_ge(s_ey, j + 1)
                act.wait_ge(s_xt, j // 4 + 1)
                nc.scalar.copy(xd[:, j, :], bank(7)[:, 0:P]).then_inc(s_ye, 1)

            x_evac(0)
            for j in range(NS):
                if j % 4 == 0 and j // 4 + 1 < NG:
                    x_evac(j // 4 + 1)
                act.wait_ge(s_eg, j + 1)
                if j >= 2:
                    act.wait_ge(s_eh, j - 1)
                nc.scalar.activation(sg[:, j % 2, :], bank(2 + j % 2), ACT.Silu).then_inc(s_es, 1)
                if j >= 1:
                    act.wait_ge(s_et, j)
                    if j >= 3:
                        act.wait_ge(s_ey, j - 2)
                    nc.scalar.copy(eT[:, (j - 1) % 2, :], bank(5 + (j - 1) % 2)).then_inc(s_ee, 1)
                if j >= 2:
                    y_evac(j - 2)
            act.wait_ge(s_et, NS)
            act.wait_ge(s_ey, NS - 2)
            nc.scalar.copy(eT[:, (NS - 1) % 2, :], bank(5 + (NS - 1) % 2)).then_inc(s_ee, 1)
            y_evac(NS - 2)
            y_evac(NS - 1)

        def add_shared(dve, b):
            dve.wait_ge(s_y, b + 1)
            xb = g.x[:, b * 4:b * 4 + 4, :].rearrange("p a c -> p (a c)")
            nc.vector.tensor_tensor(xb, xb, bank(4 + b % 2), ALU.add).then_inc(s_yadd, 1)

        @block.vector
        def _(dve):
            v = nc.vector
            for b in range(B):
                for c in range(HC):
                    n = b * HC + c
                    dve.wait_ge(s_silu, n + 1)
                    dve.wait_ge(s_up, n + 1)
                    if b >= 2:
                        dve.wait_ge(s_y, b - 1)
                    v.tensor_tensor(hT[:, b % 2, c, :], sg[:, n % 2, :], bank(n % 2), ALU.mult).then_inc(s_h, 1)
                if b >= 1:
                    add_shared(dve, b - 1)
            add_shared(dve, B - 1)
            for j in range(NS):
                dve.wait_ge(s_es, j + 1)
                dve.wait_ge(s_eu, j + 1)
                if j >= 2:
                    dve.wait_ge(s_et, j - 1)
                v.tensor_tensor(h[:, j % 2, :], sg[:, j % 2, :], bank(j % 2), ALU.mult).then_inc(s_eh, 1)
            dve.wait_ge(s_yadd, B)
            dve.wait_ge(s_gi, 16 * NT)
            for t in range(NT):
                v.scalar_tensor_tensor(out=g.x[:, t, :], in0=xn[:, t, :], scalar=weight[:, t:t + 1],
                                       in1=g.x[:, t, :], op0=ALU.mult, op1=ALU.add).then_inc(s_fin, 1)

def attention(core, g, din):
    nc, T, B, NT = core.nc, g.T, g.B, g.NT
    bank = g.bank
    HD = 64
    NHD = P // HD
    HALF, R = HD // 2, HD // 4
    KT = T // P
    BASE, LRP, ARM = 10000.0, 17, 2.0
    MIN_L = 1.0 - LRP / 100.0
    SDT_L = (BASE - MIN_L * BASE) * 2.0
    with ExitStack() as ctx:
        sb = lambda n, s, dt=F32: core.sb(n, s, dt, ctx)
        qm = sb("T_qm", [P, NHD, B * T])
        kT = sb("T_kT", [P, B * T])
        vr = sb("T_vr", [P, NT, P])
        wo = sb("T_wo", [P, P])
        bo = sb("T_bo", [P, P])
        orow = sb("T_o", [P, NT, P])
        with ExitStack() as pctx:
            pb = lambda n, s, dt=F32: core.sb(n, s, dt, pctx)
            xT = pb("T_xT", [P, B, T])
            layer_norm(core, g, "T_ln", orow, xT, 0)
            w = pb("T_w", [P, 5, P])
            bcol = pb("T_bcol", [P, 4])
            bv = pb("T_bv", [P, P])
            freq = pb("T_freq", [P, 4])
            ch = pb("T_ch", [P, 2])
            chi = pb("T_chi", [P, 6], I32)
            cos, sin = pb("T_cos", [P, 2, T]), pb("T_sin", [P, 2, T])
            ang, sq = pb("T_ang", [P, T]), pb("T_sq", [P, T])
            t1, t2 = pb("T_t1", [P, 4, T]), pb("T_t2", [P, 4, T])
            s_w, s_b, s_rot, s_dve, s_act = (core.sem("T_" + n) for n in ("w", "b", "rot", "dve", "act"))
            s_io, s_mm, s_t, s_q, s_vm, s_ve = (core.sem("T_" + n) for n in ("iota", "mm", "t", "q", "vmm", "vevac"))
            s_f1, s_f2, s_f3, s_z, s_tab, s_bo = (core.sem("T_" + n) for n in ("f1", "f2", "f3", "zero", "tab", "bo"))
            with nc.Block() as block:

                @block.sync
                def _(sp):
                    for i, n in enumerate(("Wq", "Wk", "Wv")):
                        sp.dma_start(w[:, i, :], din["L1_attn_" + n]).then_inc(s_w, 16)
                    sp.dma_start(wo[:, :], din["L1_attn_Wo"]).then_inc(s_w, 16)
                    sp.dma_start(bo[:, :], bc(din["L1_attn_bo"], 0, P)).then_inc(s_b, 16)
                    sp.dma_start(bv[:, :], bc(din["L1_attn_bv"], 0, P)).then_inc(s_b, 16)
                    sp.dma_start(freq[:, 0:1], bc(din["L1_attn_nrope_freq"], 0, P)).then_inc(s_b, 16)
                    for i, n in enumerate(("bq", "bk")):
                        col = din["L1_attn_" + n].unsqueeze(1)
                        sp.dma_start(bcol[:, i:i + 1], col).then_inc(s_b, 16)
                        for h in range(NHD):
                            o = h * HD
                            sp.dma_start(bcol[o:o + HALF, 2 + i:3 + i], col[o:o + HALF, :]).then_inc(s_b, 16)
                            o += HALF
                            sp.dma_start(bcol[o:o + R, 2 + i:3 + i], col[o + R:o + 2 * R, :]).then_inc(s_b, 16)
                            sp.dma_start(bcol[o + R:o + 2 * R, 2 + i:3 + i], col[o:o + R, :]).then_inc(s_b, 16)
                    sp.wait_ge(s_b, 16 * (3 + 2 * (1 + 3 * NHD)))
                    sp.wait_ge(s_w, 64)

                @block.gpsimd
                def _(pool):
                    nc.gpsimd.memset(qm[:, :, :], 0.0).then_inc(s_z, 1)
                    nc.gpsimd.iota(chi[:, 0:1], [[0, 1]], base=0, channel_multiplier=1).then_inc(s_io, 1)
                    nc.gpsimd.iota(ang[:, :], [[1, T]], base=0, channel_multiplier=0,
                                   allow_small_or_imprecise_dtypes=True).then_inc(s_io, 1)
                    pool.wait_ge(s_b, 16 * (3 + 2 * (1 + 3 * NHD)))
                    pool.wait_ge(s_z, 1)
                    nc.gpsimd.tensor_tensor(g.x[:, :, :], g.x[:, :, :], bc(bo[:, :], 1, NT), ALU.add).then_inc(s_bo, 1)
                    pool.wait_ge(s_bo, 1)
                    for b in range(B):
                        for i in range(2):
                            n = b * 2 + i
                            if n >= 1:
                                pool.wait_ge(s_q, b * 4 + 2 * i)
                            pool.wait_ge(s_t, 2 * n + 2)
                            a, c = t1[:, n % 4, :], t2[:, n % 4, :]
                            if i == 0:
                                for h in range(NHD):
                                    if h:
                                        pool.wait_ge(s_q, b * 4 + h)
                                    r = slice(h * HD, (h + 1) * HD)
                                    nc.gpsimd.tensor_tensor(qm[r, h, b * T:(b + 1) * T], a[r, :], c[r, :],
                                                            ALU.add).then_inc(s_q, 1)
                            else:
                                nc.gpsimd.tensor_tensor(kT[:, b * T:(b + 1) * T], a, c, ALU.add).then_inc(s_q, 2)

                @block.scalar
                def _(act):
                    act.wait_ge(s_b, 16 * (3 + 2 * (1 + 3 * NHD)))
                    nc.scalar.activation(freq[:, 1:2], freq[:, 0:1], ACT.Sigmoid).then_inc(s_f1, 1)
                    act.wait_ge(s_f2, 1)
                    nc.scalar.activation(freq[:, 2:3], freq[:, 2:3], ACT.Ln).then_inc(s_f1, 1)
                    act.wait_ge(s_f1, 2)
                    act.wait_ge(s_f3, 1)
                    nc.scalar.activation(freq[:, 3:4], ch[:, 0:1], ACT.Exp, scale=freq[:, 2:3]).then_inc(s_act, 1)
                    act.wait_ge(s_tab, 1)
                    nc.scalar.activation(sin[:, 1, :], ang[:, :], ACT.Sin).then_inc(s_act, 1)
                    nc.scalar.activation(sq[:, :], ang[:, :], ACT.Sin, scale=0.5).then_inc(s_act, 1)

                @block.vector
                def _(dve):
                    v, do = nc.vector, Chain(dve, s_dve)
                    dve.wait_ge(s_w, 64)
                    do(v.memset(w[:, 3:5, :], 0.0))
                    for i in range(2):
                        for h in range(NHD):
                            o = h * HD + HALF
                            do(v.tensor_scalar(w[:, 3 + i, o:o + R], w[:, i, o + R:o + 2 * R], -1.0, None, ALU.mult))
                            do(v.tensor_copy(w[:, 3 + i, o + R:o + 2 * R], w[:, i, o:o + R]))
                    v.nop().then_inc(s_rot, 1)
                    dve.wait_ge(s_io, 2)
                    do(v.tensor_scalar(chi[:, 1:2], chi[:, 0:1], R - 1, None, ALU.bitwise_and))
                    do(v.tensor_scalar(chi[:, 2:3], chi[:, 0:1], HALF, None, ALU.bitwise_and))
                    do(v.tensor_scalar(chi[:, 3:4], chi[:, 0:1], R, None, ALU.bitwise_and))
                    do(v.tensor_copy(ch[:, 0:1], chi[:, 1:2]))
                    do(v.tensor_copy(ch[:, 1:2], chi[:, 2:3]))
                    do(v.tensor_scalar(ch[:, 0:1], ch[:, 0:1], -1.0 / R, None, ALU.mult))
                    do(v.tensor_scalar(ch[:, 1:2], ch[:, 1:2], 1.0 / HALF, None, ALU.mult))
                    f = freq
                    sgn = t1[:, 0, 0:1]
                    do(v.tensor_copy(sgn, chi[:, 3:4]))
                    do(v.tensor_scalar(sgn, sgn, 2.0 / R, -1.0, ALU.mult, ALU.add))
                    dve.wait_ge(s_b, 16 * (3 + 2 * (1 + 3 * NHD)))
                    do(v.tensor_scalar(bcol[:, 2:4], bcol[:, 2:4], sgn, ch[:, 1:2], ALU.mult, ALU.mult))
                    dve.wait_ge(s_f1, 1)
                    v.tensor_scalar(f[:, 2:3], f[:, 1:2], SDT_L, MIN_L * BASE, ALU.mult, ALU.add).then_inc(s_f2, 1)
                    v.nop().then_inc(s_f3, 1)
                    dve.wait_ge(s_act, 1)
                    scale = ARM * float(np.pi) / max(T - 1, 1)
                    do(v.tensor_scalar(ang[:, :], ang[:, :], f[:, 3:4], scale, ALU.mult, ALU.mult))
                    do(v.tensor_scalar(ang[:, :], ang[:, :], -float(np.pi), 3.1415925, ALU.add, ALU.min))
                    v.tensor_scalar(ang[:, :], ang[:, :], -3.1415925, None, ALU.max).then_inc(s_tab, 1)
                    dve.wait_ge(s_act, 3)
                    rot = ch[:, 1:2]
                    do(v.tensor_tensor(sq[:, :], sq[:, :], sq[:, :], ALU.mult))
                    do(v.tensor_scalar(sq[:, :], sq[:, :], 2.0, -2.0, ALU.mult, ALU.add))
                    do(v.tensor_scalar(cos[:, 1, :], sq[:, :], rot, 1.0, ALU.mult, ALU.add))
                    do(v.tensor_scalar(sin[:, 1, :], sin[:, 1, :], rot, -1.0, ALU.mult, ALU.mult))
                    qs = float(HD) ** -0.5
                    do(v.tensor_scalar(cos[:, 0, :], cos[:, 1, :], qs, None, ALU.mult))
                    do(v.tensor_scalar(sin[:, 0, :], sin[:, 1, :], qs, None, ALU.mult))
                    for b in range(B):
                        for i in range(2):
                            n = b * 2 + i
                            dve.wait_ge(s_mm, 2 * n + 1)
                            if n >= 4:
                                dve.wait_ge(s_q, (n // 2 - 2) * 4 + 2 + 2 * i)
                            v.scalar_tensor_tensor(out=t1[:, n % 4, :], in0=bank(2 * i), scalar=bcol[:, i:i + 1],
                                                   in1=cos[:, i, :], op0=ALU.add, op1=ALU.mult).then_inc(s_t, 1)
                            dve.wait_ge(s_mm, 2 * n + 2)
                            v.scalar_tensor_tensor(out=t2[:, n % 4, :], in0=bank(2 * i + 1),
                                                   scalar=bcol[:, 2 + i:3 + i], in1=sin[:, i, :], op0=ALU.add,
                                                   op1=ALU.mult).then_inc(s_t, 1)
                        dve.wait_ge(s_vm, b + 1)
                        v.tensor_tensor(vr[:, b * 4:b * 4 + 4, :], bank(4 + b % 2).rearrange("p (a c) -> p a c", c=P),
                                        bc(bv[:, :], 1, 4), ALU.add).then_inc(s_ve, 1)

                @block.tensor
                def _(pe):
                    pe.wait_ge(s_rot, 1)
                    for b in range(B):
                        for i in range(2):
                            for k in range(2):
                                n = (b * 2 + i) * 2 + k
                                if b >= 1:
                                    pe.wait_ge(s_t, n - 3)
                                nc.tensor.matmul(bank(2 * i + k), w[:, i + 3 * k, :], xT[:, b, :],
                                                 start=True, stop=True).then_inc(s_mm, 1)
                        if b >= 2:
                            pe.wait_ge(s_ve, b - 1)
                        for t in range(KT):
                            mm = nc.tensor.matmul(bank(4 + b % 2)[:, t * P:(t + 1) * P],
                                                  xT[:, b, t * P:(t + 1) * P], w[:, 2, :], start=True, stop=True)
                        mm.then_inc(s_vm, 1)

        with ExitStack() as actx:
            ab = lambda n, s, dt=F32: core.sb(n, s, dt, actx)
            pr = ab("U_p", [P, 3, T])
            pT = ab("U_pT", [P, 2, T])
            nmax, ssum = ab("U_nmax", [P, B * NHD * KT]), ab("U_sum", [P, B * NHD * KT])
            oT = ab("U_oT", [P, 2, T])
            s_sc, s_mx, s_ex, s_pt, s_pe, s_pv, s_rc, s_or, s_ot, s_oe, s_y, s_ya = (
                core.sem("U_" + n) for n in ("scores", "max", "exp", "pT", "pT_evac", "pv", "recip", "o", "oT",
                                             "oT_evac", "y", "added"))
            N = B * NHD * KT

            def where(n):
                b, rest = divmod(n, NHD * KT)
                qt, h = divmod(rest, NHD)
                return b, h, qt

            with nc.Block() as block:

                @block.tensor
                def _(pe):
                    def scores(n):
                        b, h, qt = where(n)
                        if n >= 3:
                            pe.wait_ge(s_ex, n - 2)
                        nc.tensor.matmul(bank(n % 3), qm[:, h, b * T + qt * P:b * T + (qt + 1) * P],
                                         kT[:, b * T:(b + 1) * T], start=True, stop=True).then_inc(s_sc, 1)

                    def turn(n):
                        pe.wait_ge(s_ex, n + 1)
                        if n >= 2:
                            pe.wait_ge(s_pe, n - 1)
                        for c in range(KT):
                            tr = nc.tensor.transpose(bank(3 + n % 2)[:, c * P:(c + 1) * P],
                                                     pr[:, n % 3, c * P:(c + 1) * P], g.ident[:, :])
                        tr.then_inc(s_pt, 1)

                    def values(n):
                        b, h, qt = where(n)
                        pe.wait_ge(s_pe, n + 1)
                        if n >= 2:
                            pe.wait_ge(s_or, n - 1)
                        for c in range(KT):
                            mm = nc.tensor.matmul(bank(5 + n % 2)[:, 0:P], pT[:, n % 2, c * P:(c + 1) * P],
                                                  vr[:, b * KT + c, :], start=(c == 0), stop=(c == KT - 1))
                        mm.then_inc(s_pv, 1)

                    def project(t):
                        pe.wait_ge(s_or, NHD * (t + 1))
                        if t >= 1:
                            pe.wait_ge(s_ya, t)
                        nc.tensor.transpose(bank(7)[:, 0:P], orow[:, t, :], g.ident[:, :]).then_inc(s_ot, 1)
                        pe.wait_ge(s_oe, t + 1)
                        nc.tensor.matmul(bank(7)[:, P:2 * P], oT[:, t % 2, 0:P], wo[:, :],
                                         start=True, stop=True).then_inc(s_y, 1)

                    for n in range(N + 4):
                        if n < N:
                            scores(n)
                        if 1 <= n <= N:
                            turn(n - 1)
                        if 2 <= n <= N + 1:
                            values(n - 2)
                        if n >= 5 and (n - 5) % NHD == 0 and (n - 5) // NHD < NT:
                            project((n - 5) // NHD)

                def o_evac(act, t):
                    act.wait_ge(s_ot, t + 1)
                    nc.scalar.copy(oT[:, t % 2, 0:P], bank(7)[:, 0:P]).then_inc(s_oe, 1)

                @block.scalar
                def _(act):
                    for n in range(N):
                        act.wait_ge(s_mx, n + 1)
                        if n >= 3:
                            act.wait_ge(s_pt, n - 2)
                        nc.scalar.activation(pr[:, n % 3, :], bank(n % 3), ACT.Exp, bias=nmax[:, n:n + 1],
                                             accum_out=ssum[:, n:n + 1]).then_inc(s_ex, 1)
                        if n >= 5 and (n - 5) % NHD == 0:
                            o_evac(act, (n - 5) // NHD)
                    for t in range((N - 6) // NHD + 1, NT):
                        o_evac(act, t)

                @block.vector
                def _(dve):
                    v = nc.vector

                    def finish(n):
                        b, h, qt = where(n)
                        dve.wait_ge(s_rc, n + 1)
                        dve.wait_ge(s_pv, n + 1)
                        v.tensor_scalar(orow[:, b * KT + qt, h * HD:(h + 1) * HD],
                                        bank(5 + n % 2)[:, h * HD:(h + 1) * HD], ssum[:, n:n + 1], None,
                                        ALU.mult).then_inc(s_or, 1)

                    def add(t):
                        dve.wait_ge(s_y, t + 1)
                        v.tensor_tensor(g.x[:, t, :], g.x[:, t, :], bank(7)[:, P:2 * P], ALU.add).then_inc(s_ya, 1)

                    for n in range(N + 2):
                        if n < N:
                            dve.wait_ge(s_sc, n + 1)
                            v.tensor_reduce(nmax[:, n:n + 1], bank(n % 3), AX_X, ALU.max, negate=True).then_inc(s_mx, 1)
                        if 1 <= n <= N:
                            dve.wait_ge(s_ex, n)
                            v.reciprocal(ssum[:, n - 1:n], ssum[:, n - 1:n]).then_inc(s_rc, 1)
                            dve.wait_ge(s_pt, n)
                            if n >= 3:
                                dve.wait_ge(s_pv, n - 2)
                            v.tensor_copy(pT[:, (n - 1) % 2, :], bank(3 + (n - 1) % 2)).then_inc(s_pe, 1)
                        if n >= 2:
                            finish(n - 2)
                        if n >= 6 and (n - 6) % NHD == 0:
                            add((n - 6) // NHD)
                    for t in range((N + 1 - 6) // NHD + 1, NT):
                        add(t)


def channel_mix(core, g, din, out):
    nc, T, B, NT = core.nc, g.T, g.B, g.NT
    bank = g.bank
    KT = T // P
    with ExitStack() as ctx:
        sb = lambda n, s, dt=F32: core.sb(n, s, dt, ctx)
        xn = sb("D_xn", [P, NT, P])
        xT = sb("D_xT", [P, B, 1 + T])
        layer_norm(core, g, "D_ln", xn, xT, 1)
        w, wT = sb("D_w", [P, 3, P]), sb("D_wT", [P, 3, P])
        mu, imu = sb("D_mu", [P, 2]), sb("D_imu", [P, 2])
        mix = sb("D_mix", [P, 2, 2, T])
        rel, ka = sb("D_rel", [P, 2, T]), sb("D_ka", [P, 2, T])
        r, rv = sb("D_r", [P, 2, T]), sb("D_rv", [P, 2, T])
        s_w, s_mu, s_wt, s_we, s_im = (core.sem("D_" + n) for n in ("w", "mu", "wT", "wT_evac", "imu"))
        s_pv, s_mx, s_k, s_r, s_rel, s_ka, s_sig, s_v, s_rv, s_o = (
            core.sem("D_" + n) for n in ("prev", "mixed", "k", "r", "relu", "kact", "sig", "v", "rv", "o"))
        s_out = g.s_out
        out_v = out.rearrange("b (t p) c -> b p t c", p=P)
        with nc.Block() as block:

            @block.sync
            def _(sp):
                for i, n in enumerate(("W_r", "W_k", "W_v")):
                    sp.dma_start(w[:, i, :], din["L1_ffn_" + n]).then_inc(s_w, 16)
                sp.dma_start(mu[:, 0:1], din["L1_ffn_mu_r"].unsqueeze(1)).then_inc(s_mu, 16)
                sp.dma_start(mu[:, 1:2], din["L1_ffn_mu_k"].unsqueeze(1)).then_inc(s_mu, 16)
                for b in range(B):
                    sp.wait_ge(s_o, b + 1)
                    sp.dma_start(out_v[b], g.x[:, b * KT:(b + 1) * KT, :]).then_inc(s_out, 16)
                sp.wait_ge(s_out, 16 * B)

            @block.tensor
            def _(pe):
                pe.wait_ge(s_w, 48)
                for i in range(3):
                    tr = nc.tensor.transpose(bank(0)[:, i * P:(i + 1) * P], w[:, i, :], g.ident[:, :])
                tr.then_inc(s_wt, 1)
                pe.wait_ge(s_we, 1)

                def values(b):
                    pe.wait_ge(s_ka, b + 1)
                    if b >= 2:
                        pe.wait_ge(s_rv, b - 1)
                    for t in range(KT):
                        mm = nc.tensor.matmul(bank(4 + b % 2)[:, t * P:(t + 1) * P], ka[:, b % 2, t * P:(t + 1) * P],
                                              wT[:, 2, :], start=True, stop=True)
                    mm.then_inc(s_v, 1)

                for b in range(B):
                    pe.wait_ge(s_mx, 2 * b + 2)
                    if b >= 2:
                        pe.wait_ge(s_ka, b - 1)
                        pe.wait_ge(s_sig, b - 1)
                    nc.tensor.matmul(bank(b % 2), wT[:, 1, :], mix[:, b % 2, 1, :], start=True, stop=True).then_inc(s_k, 1)
                    for t in range(KT):
                        mm = nc.tensor.matmul(bank(2 + b % 2)[:, t * P:(t + 1) * P],
                                              mix[:, b % 2, 0, t * P:(t + 1) * P], wT[:, 0, :], start=True, stop=True)
                    mm.then_inc(s_r, 1)
                    if b >= 1:
                        values(b - 1)
                values(B - 1)

            def evac(act, b):
                act.wait_ge(s_k, b + 1)
                if b >= 2:
                    act.wait_ge(s_ka, b - 1)
                nc.scalar.activation(rel[:, b % 2, :], bank(b % 2), ACT.Relu).then_inc(s_rel, 1)
                act.wait_ge(s_r, b + 1)
                if b >= 2:
                    act.wait_ge(s_rv, b - 1)
                nc.scalar.activation(r[:, b % 2, :], bank(2 + b % 2), ACT.Sigmoid).then_inc(s_sig, 1)

            @block.scalar
            def _(act):
                act.wait_ge(s_im, 1)
                for b in range(B):
                    if b >= 2:
                        act.wait_ge(s_r, b - 1)
                        act.wait_ge(s_k, b - 1)
                    for i in range(2):
                        nc.scalar.activation(mix[:, b % 2, i, :], xT[:, b, 0:T], ACT.Copy,
                                             scale=imu[:, i:i + 1]).then_inc(s_pv, 1)
                    if b >= 1:
                        evac(act, b - 1)
                evac(act, B - 1)

            def act_k(dve, b):
                dve.wait_ge(s_rel, b + 1)
                if b >= 2:
                    dve.wait_ge(s_v, b - 1)
                nc.vector.tensor_tensor(ka[:, b % 2, :], rel[:, b % 2, :], bank(b % 2), ALU.mult).then_inc(s_ka, 1)

            @block.vector
            def _(dve):
                v = nc.vector
                dve.wait_ge(s_mu, 32)
                v.tensor_scalar(imu[:, :], mu[:, :], -1.0, 1.0, ALU.mult, ALU.add).then_inc(s_im, 1)
                dve.wait_ge(s_wt, 1)
                v.tensor_copy(wT[:, :, :].rearrange("p a c -> p (a c)"), bank(0)[:, 0:3 * P]).then_inc(s_we, 1)

                def gate(b):
                    dve.wait_ge(s_v, b + 1)
                    dve.wait_ge(s_sig, b + 1)
                    if b >= 2:
                        dve.wait_ge(s_o, b - 1)
                    v.tensor_tensor(rv[:, b % 2, :], r[:, b % 2, :], bank(4 + b % 2), ALU.mult).then_inc(s_rv, 1)

                for b in range(B):
                    for i in range(2):
                        dve.wait_ge(s_pv, 2 * b + i + 1)
                        v.scalar_tensor_tensor(out=mix[:, b % 2, i, :], in0=xT[:, b, 1:1 + T], scalar=mu[:, i:i + 1],
                                               in1=mix[:, b % 2, i, :], op0=ALU.mult, op1=ALU.add).then_inc(s_mx, 1)
                    if b >= 1:
                        act_k(dve, b - 1)
                    if b >= 2:
                        gate(b - 2)
                act_k(dve, B - 1)
                gate(B - 2)
                gate(B - 1)

            @block.gpsimd
            def _(pool):
                for b in range(B):
                    pool.wait_ge(s_rv, b + 1)
                    xb = g.x[:, b * KT:(b + 1) * KT, :].rearrange("p a c -> p (a c)")
                    nc.gpsimd.tensor_tensor(xb, xb, rv[:, b % 2, :], ALU.add).then_inc(s_o, 1)


class Globals:
    pass


STAGES = 99


def build(nc, din, out):
    ctx = ExitStack()
    with ctx:
        core = Core(nc, ctx)
        g = Globals()
        g.B, g.T, H = din["L0_attn_hidden"].shape
        assert H == P
        g.NH = din["L0_attn_A_log"].shape[0]
        g.D = P // g.NH
        g.KC = din["L0_attn_conv_q"].shape[1]
        g.NT = g.B * g.T // P
        g.x_dram, g.din, g.out = din["L0_attn_hidden"], din, out
        psum = [ctx.enter_context(nc.psum_tensor(f"bank{i}", [P, BANK], F32)) for i in range(8)]
        g.bank = lambda i: psum[i][:, :]
        g.ident = core.sb("ident", [P, P])
        g.eps5 = core.sb("eps5", [P, 1])
        g.eps6 = core.sb("eps6", [P, 1])
        g.s_out = nc.alloc_semaphore("out_written")
        s_eps = core.sem("eps")
        with nc.Block() as block:

            @block.vector
            def _(dve):
                nc.vector.memset(g.eps5[:, :], 1e-5).then_inc(s_eps, 1)
                nc.vector.memset(g.eps6[:, :], 1e-6).then_inc(s_eps, 1)

        x1_dram = out.rearrange("b t c -> (b t) c").rearrange("(n p) c -> p n c", p=P)
        g.x = core.sb("x", [P, g.NT, P])
        NS = (g.NT + din["L0_ffn_w_router"].shape[1] + 3) // 4 * 4
        g.sorted_x = nc.dram_tensor("sorted_x", [NS * P, P], F32, kind="Internal").ap()
        g.sorted_y = nc.dram_tensor("sorted_y", [NS * P, P], F32, kind="Internal").ap()
        with ExitStack() as actx:
            sb = lambda n, s: core.sb(n, s, F32, actx)
            g.woT, g.norm_w = sb("woT", [P, P]), sb("norm_w", [P, 1])
            g.gateT = sb("gateT", [P, g.B, g.T])
            g.A_log, g.dt_bias = sb("A_log", [P, 1]), sb("dt_bias", [P, 1])
            g.beta, g.z = sb("beta", [P, g.T]), sb("z", [P, g.T])
            g.q, g.v = sb("q", [P, g.D, g.T]), sb("v", [P, g.D, g.T])
            g.k = g.x[:, :, :].rearrange("p n c -> p (n c)").rearrange("p (d t) -> p d t", d=g.D)
            g.o = g.v
            delta_in(core, g, din)
            delta_rule(core, g)
            delta_out(core, g)
        core.end_layer_part()
        if STAGES >= 2:
            moe(core, g, din)
            core.end_layer_part()
        if STAGES >= 3:
            attention(core, g, din)
            core.end_layer_part()
        if STAGES >= 4:
            channel_mix(core, g, din, out)
        else:
            with nc.Block() as block:

                @block.sync
                def _(sp):
                    sp.dma_start(x1_dram, g.x[:, :, :]).then_inc(g.s_out, 16)
                    sp.wait_ge(g.s_out, 16)


def kernel(**inputs):
    import concourse.bacc as bacc
    from concourse.bass_utils import run_bass_kernel_spmd

    nc = bacc.Bacc("TRN2", target_bir_lowering=False, num_devices=1)
    arrays, din = {}, {}
    for name, value in inputs.items():
        a = np.ascontiguousarray(value)
        arrays["in_" + name] = a
        din[name] = nc.dram_tensor("in_" + name, a.shape, mybir.dt.from_np(a.dtype), kind="ExternalInput").ap()
    shape = inputs["L0_attn_hidden"].shape
    out = nc.dram_tensor("out_x", shape, F32, kind="ExternalOutput").ap()
    build(nc, din, out)
    r = run_bass_kernel_spmd(nc, [arrays], core_ids=[0])
    return r.results[0]["out_x"]
```

```python
from contextlib import ExitStack

import numpy as np

import concourse.bass as bass
from concourse import mybir

F32 = mybir.dt.float32
I32 = mybir.dt.int32
ALU = mybir.AluOpType
ACT = mybir.ActivationFunctionType
AX_X = mybir.AxisListType.X

P = 128
BANK = 512


class Core:

    def __init__(self, nc, ctx):
        self.nc, self.ctx, self.sems = nc, ctx, []

    def sb(self, name, shape, dt=F32, ctx=None):
        return (ctx or self.ctx).enter_context(self.nc.sbuf_tensor(name, shape, dt))

    def sem(self, name):
        self.sems.append(self.nc.alloc_semaphore(name))
        return self.sems[-1]

    def end_layer_part(self):
        self.nc.clear_and_free_semaphores(self.sems)
        self.nc.all_engine_barrier()
        self.sems = []


def bc(ap, axis, n):
    shape = list(ap.shape)
    shape.insert(axis, n)
    return ap.unsqueeze(axis).to_broadcast(shape)


def delta_in(core, g, din):
    nc, B, T = core.nc, g.B, g.T
    TB = T // P
    KC = g.KC
    NB2 = 2 * g.NH
    bank = g.bank
    ring = lambda n: bank(2 + n % 6)
    pair = lambda n: bank(n % 2)
    tiles_at = lambda b: max(3 * b - 2, 0)
    gate_at = lambda b: 3 * b + (2 if b + 1 < B else 1)
    SLOTS = 9
    folded = lambda b: b % 2 == 1
    convs_before = lambda b: 3 * b - b // 2
    with ExitStack() as ctx:
        sb = lambda n, s, dt=F32: core.sb(n, s, dt, ctx)
        w_rows = sb("A_w_rows", [P, 5, P])
        wba_rows = sb("A_wba_rows", [P, P])
        conv = sb("A_conv", [P, 3, KC])
        taps = sb("A_taps", [P, KC, P])
        wT = sb("A_wT", [P, 4 + KC, P])
        wbaT = sb("A_wbaT", [P, P])
        stats = sb("A_stats", [P, g.NT, 6])
        mv = sb("A_mv", [P, g.NT, 2])
        rstd = sb("A_rstd", [P, g.NT])
        x = sb("A_x", [P, g.NT, P])
        xn = sb("A_xn", [P, g.NT, P])
        xnT = sb("A_xnT", [P, B, KC - 1 + T])
        proj = sb("A_proj", [P, SLOTS, T])
        ab = sb("A_ab", [NB2, 2, T])

        s_x = [core.sem(f"A_x_loaded{b}") for b in range(B)]
        s_w, s_small, s_id, s_zero = (core.sem("A_" + n) for n in ("w_loaded", "small_loaded", "identity", "zeros"))
        s_st, s_mv, s_std, s_rstd = (core.sem("A_" + n) for n in ("stats", "mv", "std", "rstd"))
        s_xnp, s_xnv, s_pad = (core.sem("A_" + n) for n in ("xn_pool", "xn_dve", "pad"))
        s_tap, s_wtr, s_wev = (core.sem("A_" + n) for n in ("tap", "wtr", "wevac"))
        s_mm, s_pair, s_read, s_first, s_step, s_conv, s_fv, s_act = (core.sem("A_" + n) for n in (
            "mm", "pair", "pair_read", "first_tap", "conv_step", "convolved", "folded_v", "act"))
        s_outs = [core.sem(f"A_moved{i}") for i in range(SLOTS)]
        s_abm = [core.sem(f"A_abmoved{i}") for i in range(2)]

        x_rows_dram = g.x_dram.rearrange("b t c -> (b t) c").rearrange("(n p) c -> p n c", p=P)

        def taken(n):
            b, i = divmod(n, 3)
            return (s_fv, (b + 1) // 2) if i == 2 and folded(b) else (s_conv, convs_before(b) + i + 1)

        with nc.Block() as block:

            @block.sync
            def _(sp):
                def load_x(b):
                    sp.dma_start(x[:, b * TB:(b + 1) * TB, :],
                                 x_rows_dram[:, b * TB:(b + 1) * TB, :]).then_inc(s_x[b], 16)

                load_x(0)
                for i, n in enumerate(("Wq", "Wk", "Wv", "Wg", "Wo")):
                    sp.dma_start(w_rows[:, i, :], din["L0_attn_" + n]).then_inc(s_w, 16)
                sp.wait_ge(s_zero, 1)
                sp.dma_start(wba_rows[0:g.NH, :], din["L0_attn_Wb"]).then_inc(s_w, 16)
                sp.dma_start(wba_rows[g.NH:NB2, :], din["L0_attn_Wa"]).then_inc(s_w, 16)
                for i, n in enumerate("qkv"):
                    sp.dma_start(conv[:, i, :], din["L0_attn_conv_" + n]).then_inc(s_w, 16)
                for b in range(1, B):
                    load_x(b)
                for dst, n, times in ((g.norm_w, "norm_w", g.NH), (g.A_log, "A_log", B), (g.dt_bias, "dt_bias", B)):
                    sp.dma_start(dst[:, :], bc(din["L0_attn_" + n], 0, times)).then_inc(s_small, 16)
                for b in range(B):
                    rows = slice(b * g.NH, (b + 1) * g.NH)
                    for i, dst in enumerate((g.q, g.k, g.v)):
                        n = b * 3 + i
                        sp.wait_ge(s_act, n + 1)
                        sp.dma_start(dst[rows, :, :], proj[:, n % SLOTS, :]).then_inc(s_outs[n % SLOTS], 16)
                    sp.wait_ge(s_read, gate_at(b) + 2)
                    sp.dma_start(g.beta[rows, :], ab[0:g.NH, b % 2, :]).then_inc(s_abm[b % 2], 16)
                    sp.dma_start(g.z[rows, :], ab[g.NH:, b % 2, :]).then_inc(s_abm[b % 2], 16)
                sp.wait_ge(s_small, 16 * 3)
                for i, s in enumerate(s_outs):
                    sp.wait_ge(s, 16 * ((3 * B - i + SLOTS - 1) // SLOTS))
                for s in s_abm:
                    sp.wait_ge(s, 16 * B)

            @block.gpsimd
            def _(pool):
                nc.gpsimd.memset(wba_rows[:, :], 0.0).then_inc(s_zero, 1)
                nc.gpsimd.memset(g.ident[:, :], 0.0).then_inc(s_pad, 1)
                pool.wait_ge(s_pad, 1)
                nc.gpsimd.affine_select(out=g.ident[:, :], in_=g.ident[:, :], compare_op=ALU.not_equal,
                                        fill=1.0, base=0, pattern=[[-1, P]],
                                        channel_multiplier=1).then_inc(s_id, 1)
                nc.gpsimd.memset(xnT[:, :, 0:KC - 1], 0.0).then_inc(s_pad, 1)
                for t in range(0, g.NT, 2):
                    if t % (g.NT // 2) == 0:
                        pool.wait_ge(s_rstd, t // (g.NT // 2) + 1)
                    nc.gpsimd.tensor_scalar(xn[:, t, :], x[:, t, :], mv[:, t, 0:1], rstd[:, t:t + 1],
                                            ALU.subtract, ALU.mult).then_inc(s_xnp, 1)

            @block.vector
            def _(dve):
                v = nc.vector

                def statistics(h):
                    for t in range(h * g.NT // 2, (h + 1) * g.NT // 2):
                        if t % TB == 0:
                            dve.wait_ge(s_x[t // TB], 16)
                        v.bn_stats(stats[:, t, :], x[:, t, :]).then_inc(s_st, 1)
                        if t % TB > 0:
                            dve.wait_ge(s_st, t)
                            v.bn_aggr(mv[:, t - 1, :], stats[:, t - 1, :]).then_inc(s_mv, 1)
                        if t % TB == TB - 1:
                            dve.wait_ge(s_st, t + 1)
                            v.bn_aggr(mv[:, t, :], stats[:, t, :]).then_inc(s_mv, 1)

                def normalize(h):
                    sl = slice(h * g.NT // 2, (h + 1) * g.NT // 2)
                    dve.wait_ge(s_std, h + 1)
                    v.reciprocal(rstd[:, sl], rstd[:, sl]).then_inc(s_rstd, 1)
                    dve.wait_ge(s_rstd, h + 1)
                    for t in range(sl.start + 1, sl.stop, 2):
                        v.tensor_scalar(xn[:, t, :], x[:, t, :], mv[:, t, 0:1], rstd[:, t:t + 1],
                                        ALU.subtract, ALU.mult).then_inc(s_xnv, 1)

                statistics(0)
                dve.wait_ge(s_w, 16 * 10)
                for j in range(KC):
                    v.tensor_scalar(taps[:, j, :], w_rows[:, 2, :], conv[:, 2, j:j + 1], None, ALU.mult).then_inc(s_tap, 1)
                normalize(0)
                statistics(1)
                dve.wait_ge(s_wtr, 1)
                v.tensor_copy(wT[:, 0:4, :], bank(2)).then_inc(s_wev, 1)
                dve.wait_ge(s_wtr, 2)
                v.tensor_copy(wT[:, 4:, :], bank(3)).then_inc(s_wev, 1)
                dve.wait_ge(s_wtr, 3)
                dve.wait_ge(s_small, 48)
                v.tensor_scalar(g.woT[:, :], bank(4)[:, 0:P], g.norm_w[:, :], None, ALU.mult).then_inc(s_wev, 1)
                v.tensor_copy(wbaT[:, :], bank(4)[:, P:2 * P]).then_inc(s_wev, 1)
                normalize(1)
                for b in range(B):
                    outputs = range(2 if folded(b) else 3)
                    for step in range(1, KC):
                        j = KC - 1 - step
                        for i in outputs:
                            c = convs_before(b) + i
                            if step == 1:
                                dve.wait_ge(s_first, c + 1)
                            else:
                                dve.wait_ge(s_step, (KC - 2) * convs_before(b) + (step - 2) * len(outputs) + i + 1)
                            acc = proj[:, (b * 3 + i) % SLOTS, step:]
                            v.scalar_tensor_tensor(
                                out=acc, in0=ring(b * 3 + i)[:, 0:T - step], scalar=conv[:, i, j:j + 1],
                                in1=acc, op0=ALU.mult, op1=ALU.add).then_inc(s_conv if step == KC - 1 else s_step, 1)

            @block.scalar
            def _(act):
                def std(h):
                    sl = slice(h * g.NT // 2, (h + 1) * g.NT // 2)
                    act.wait_ge(s_mv, sl.stop)
                    nc.scalar.activation(rstd[:, sl], mv[:, sl, 1], ACT.Sqrt, bias=g.eps5[:, :]).then_inc(s_std, 1)

                def x_columns(b):
                    r = tiles_at(b)
                    act.wait_ge(s_pair, r + 1)
                    nc.scalar.copy(xnT[:, b, KC - 1:], pair(r)).then_inc(s_read, 1)

                def gate(b):
                    act.wait_ge(s_pair, gate_at(b) + 1)
                    nc.scalar.activation(g.gateT[:, b, :], pair(gate_at(b)), ACT.Silu).then_inc(s_read, 1)

                def beta_and_decay(b):
                    act.wait_ge(s_pair, gate_at(b) + 2)
                    if b >= 2:
                        act.wait_ge(s_abm[b % 2], 32 * (b // 2))
                    nc.scalar.copy(ab[:, b % 2, :], pair(gate_at(b) + 1)[0:NB2, :]).then_inc(s_read, 1)

                def first_taps(b):
                    for i in range(2 if folded(b) else 3):
                        n = b * 3 + i
                        act.wait_ge(s_mm, n + 1)
                        if n >= SLOTS:
                            act.wait_ge(s_outs[n % SLOTS], 16 * (n // SLOTS))
                        nc.scalar.activation(proj[:, n % SLOTS, :], ring(n), ACT.Copy,
                                             scale=conv[:, i, KC - 1:KC]).then_inc(s_first, 1)

                def activate(b):
                    for i in range(3):
                        n = b * 3 + i
                        slot = proj[:, n % SLOTS, :]
                        if i == 2 and folded(b):
                            act.wait_ge(s_mm, n + 1)
                            if n >= SLOTS:
                                act.wait_ge(s_outs[n % SLOTS], 16 * (n // SLOTS))
                            nc.scalar.activation(slot, ring(n), ACT.Silu).then_inc(s_fv, 1)
                            act.wait_ge(s_fv, (b + 1) // 2)
                            nc.scalar.nop().then_inc(s_act, 1)
                        else:
                            act.wait_ge(s_conv, convs_before(b) + i + 1)
                            nc.scalar.activation(slot, slot, ACT.Silu).then_inc(s_act, 1)

                std(0)
                x_columns(0)
                std(1)
                for b in range(B):
                    first_taps(b)
                    if b + 1 < B:
                        x_columns(b + 1)
                    gate(b)
                    if b >= 1:
                        activate(b - 1)
                    beta_and_decay(b)
                activate(B - 1)

            @block.tensor
            def _(pe):
                pe.wait_ge(s_id, 1)
                pe.wait_ge(s_w, 16 * 10)
                for i in range(4):
                    tr = nc.tensor.transpose(bank(2)[:, i * P:(i + 1) * P], w_rows[:, i, :], g.ident[:, :])
                tr.then_inc(s_wtr, 1)
                pe.wait_ge(s_tap, KC)
                for j in range(KC):
                    tr = nc.tensor.transpose(bank(3)[:, j * P:(j + 1) * P], taps[:, j, :], g.ident[:, :])
                tr.then_inc(s_wtr, 1)
                nc.tensor.transpose(bank(4)[:, 0:P], w_rows[:, 4, :], g.ident[:, :])
                nc.tensor.transpose(bank(4)[:, P:2 * P], wba_rows[:, :], g.ident[:, :]).then_inc(s_wtr, 1)

                def free(r):
                    if r >= 2:
                        pe.wait_ge(s_read, r - 1)

                def x_columns(b):
                    r = tiles_at(b)
                    free(r)
                    pe.wait_ge(s_xnp, (b + 1) * TB // 2)
                    pe.wait_ge(s_xnv, (b + 1) * TB // 2)
                    for t in range(TB):
                        tr = nc.tensor.transpose(pair(r)[:, t * P:(t + 1) * P], xn[:, b * TB + t, :],
                                                 g.ident[:, :])
                    tr.then_inc(s_pair, 1)

                x_columns(0)
                pe.wait_ge(s_wev, 4)
                pe.wait_ge(s_pad, 2)
                for b in range(B):
                    pe.wait_ge(s_read, tiles_at(b) + 1)
                    for i in range(3):
                        n = b * 3 + i
                        if n >= 6:
                            pe.wait_ge(*taken(n - 6))
                        if i == 2 and folded(b):
                            for j in range(KC):
                                mm = nc.tensor.matmul(ring(n), wT[:, 4 + j, :], xnT[:, b, j:j + T],
                                                      start=(j == 0), stop=(j == KC - 1))
                        else:
                            mm = nc.tensor.matmul(ring(n), wT[:, i, :], xnT[:, b, KC - 1:], start=True, stop=True)
                        mm.then_inc(s_mm, 1)
                    if b + 1 < B:
                        x_columns(b + 1)
                    for i, w in enumerate((wT[:, 3, :], wbaT[:, :])):
                        r = gate_at(b) + i
                        free(r)
                        nc.tensor.matmul(pair(r), w, xnT[:, b, KC - 1:], start=True, stop=True).then_inc(s_pair, 1)


class Chain:

    def __init__(self, eng, sem):
        self.eng, self.sem, self.n = eng, sem, 0

    def __call__(self, ins):
        ins.then_inc(self.sem, 1)
        self.n += 1
        self.eng.wait_ge(self.sem, self.n)


def delta_rule(core, g):
    nc, T, D = core.nc, g.T, g.D
    bank = g.bank
    C = 4
    N = T // C
    NB = 16
    M = N // NB
    TC = NB * C
    RP = NB // 2
    SR = 3 * NB
    NP = C * C
    W_OF = [C - d for d in range(C)]
    QKP = 4
    EARLY = 2
    PREP = 6 + 2 * C
    W_PIECES = [(i, j, h) for i in range(C) for j in range(i + 1) for h in range(2)]
    GAPS = QKP + PREP + len(W_PIECES)
    assert GAPS <= 4 * NB
    PLACE_AT = [(GAPS + 3) // 4 + i for i in range(C)]
    qk_at = [NB * sum(W_OF[:d]) for d in range(C)]
    kk_at = [None] + [NB * (sum(W_OF) + sum(W_OF[1:d])) for d in range(1, C)]
    with ExitStack() as ctx:
        sb = lambda n, s, dt=F32: core.sb(n, s, dt, ctx)
        kd = sb("B_kd", [P, 2, D, NB, C])
        W = sb("B_W", [P, 2, NB, C, D])
        U = sb("B_U", [P, 2, NB, C, D])
        V = sb("B_V", [P, 2, NB, C, D])
        S = sb("B_S", [P, SR, D, D])
        QK = sb("B_QK", [P, M, NB * NP])
        T2 = sb("B_T2", [P, NB, C - 2])
        T3 = sb("B_T3", [P, 3, NB])
        TW, TU = sb("B_TW", [P, NB, C, C]), sb("B_TU", [P, NB, C, C])
        P1 = sb("B_P1", [P, 2 * RP, C, D, D + 1])
        P2 = sb("B_P2", [P, 2, D * D, C + 1])
        PQ = sb("B_PQ", [P, D, NB * NP])
        XP = sb("B_XP", [P, C * (C + 1) // 2, 2 * D, NB])
        OT = g.work[:, 0:2 * (D + C) * C * NB * D].rearrange("p (a x i n v) -> p a x i n v", a=2, x=D + C, i=C, v=D)
        Gam = sb("B_Gam", [P, N])
        kdc, qgc, nbg = sb("B_kdc", [P, N, C]), sb("B_qgc", [P, N, C]), sb("B_nbg", [P, N, C])
        rq, rk = sb("B_rq", [P, T]), sb("B_rk", [P, T])
        zero = sb("B_zero", [P, P])
        ms = rq
        early = g.work
        E = early[:, 0:C * T].rearrange("p (e t) -> p e t", e=C)
        G = early[:, C * T:2 * C * T].rearrange("p (e t) -> p e t", e=C)
        a_ex, a_s, a_s2, a_p = (early[:, (2 * C + i) * T:(2 * C + i + 1) * T] for i in range(4))
        sqq = early[:, (2 * C + 4) * T:(2 * C + 4 + D) * T].rearrange("p (d t) -> p d t", d=D)
        sqk = P1[:, :, :, :, :].rearrange("p n i v x -> p (n i v x)")[:, 0:D * T].rearrange("p (d t) -> p d t", d=D)
        zabs = a_p
        cfs = early[:, (2 * C + 12) * T:(3 * C + 11) * T].rearrange("p (d n c) -> p d n c", d=C - 1, c=C)

        (s_dve, s_sq, s_ss, s_z, s_ee, s_ea, s_G, s_E, s_rt, s_sig, s_cf) = (core.sem("B_" + n) for n in (
            "dve", "squares", "norms", "z", "exp_z", "exp_A", "G", "E", "roots", "beta", "coefficients"))
        s_xpu, s_act, s_cq, s_cb = (core.sem("B_" + n) for n in ("u_terms", "act", "pair_coefficients_step", "pair_coefficients"))
        s_act1 = core.sem("B_act1")
        s_nbg = core.sem("B_nbg")
        s_G0, s_cp, s_inv, s_opl, s_x, s_zero, s_filled = (core.sem("B_" + n) for n in (
            "G_zeroed", "coefficients_pool", "inverse_rms", "last_products", "x_loaded", "zero", "filled"))
        (s_p1, s_r1, s_p2, s_r2, s_dec, s_ur) = (core.sem("B_" + n) for n in (
            "P1", "R1", "P2", "R2", "decayed", "u_in_ring"))
        (s_pq, s_pqs, s_qk, s_kd, s_prep, s_xp, s_xs, s_w, s_u) = (core.sem("B_" + n) for n in (
            "pq", "pq_summed", "qk", "kd", "prep", "x_products", "x_summed", "w_placed", "u_placed"))
        (s_qg, s_op, s_os, s_oe, s_osq, s_ms, s_rms, s_o, s_pool) = (core.sem("B_" + n) for n in (
            "qg", "o_products", "o_summed", "o_placed", "o_squared", "ms", "rms", "o", "pool"))

        blocks = lambda ap: ap.rearrange("p d (n c) -> p d n c", c=C)
        q4, k4, v4, E4, G4 = (blocks(a) for a in (g.q[:, :, :], g.k, g.v[:, :, :], E, G))
        b3, rq3, rk3 = (a[:, :].rearrange("p (n c) -> p n c", c=C) for a in (g.beta, rq, rk))
        o_bank = lambda m, i: 4 + 2 * (m % 2) + i // 2
        osq = g.q[:, :, :]

        def pairs(ap, at, w):
            return ap[:, at:at + NB * w].rearrange("p (n i) -> p n i", i=w)

        def chunk_pairs(ap, at, w):
            return ap[:, :, at:at + NB * w].rearrange("p m (n i) -> p m n i", i=w)

        nb3 = g.z[:, :].rearrange("p (n c) -> p n c", c=C)

        def pair_coefficients(m0, m1):
            at = slice(m0 * NB, m1 * NB)
            by_chunk = lambda ap: ap.rearrange("p (m n) i -> p m n i", m=m1 - m0)
            out = lambda where, w: chunk_pairs(QK[:, m0:m1, :], where, w)
            dj = [by_chunk(rk3[:, at, 0:C])] + [by_chunk(cfs[:, d - 1, at, 0:C - d]) for d in range(1, C)]
            for d in range(1, C):
                yield dj[d], by_chunk(rk3[:, at, 0:C - d]), by_chunk(E4[:, d - 1, at, d:C])
            for d in range(1, C):
                yield out(kk_at[d], C - d), dj[d], by_chunk(nb3[:, at, d:C])
            for d in range(C):
                yield out(qk_at[d], C - d), dj[d], by_chunk(rq3[:, at, d:C])

        def output_products(eng, m, i):
            at = slice(m * NB, (m + 1) * NB)
            st = m % 3 * NB
            eng.tensor_tensor(OT[:, m % 2, 0:D, i, :, :], S[:, st:st + NB, :, :].rearrange("p n k v -> p k n v"),
                              bc(q4[:, :, at, i], 3, D), ALU.mult)
            for j in range(i + 1):
                ins = eng.tensor_tensor(OT[:, m % 2, D + j, i, :, :], V[:, m % 2, :, j, :],
                                        bc(pairs(QK[:, m, :], qk_at[i - j], W_OF[i - j])[:, :, j], 2, D), ALU.mult)
            return ins

        with nc.Block() as block:

            @block.sync
            def _(sp):
                sp.wait_ge(s_zero, 1)
                sp.dma_start(g.sorted_x.rearrange("(n p) c -> p n c", p=P),
                             bc(zero[:, :], 1, g.sorted_x.shape[0] // P)).then_inc(s_filled, 16)
                sp.wait_ge(s_kd, M)
                sp.wait_ge(s_pq, M)
                sp.wait_ge(s_xp, M * len(W_PIECES))
                sp.dma_start(g.x[:, :, :], g.x_dram.rearrange("b t c -> (b t) c").rearrange(
                    "(n p) c -> p n c", p=P)).then_inc(s_x, 16)
                sp.wait_ge(s_filled, 16)
                sp.wait_ge(s_x, 16)

            @block.tensor
            def _(pe):
                def sum_norm(i):
                    for d in range(D):
                        if d % (D // 2) == 0:
                            pe.wait_ge(s_sq, 2 * i + d // (D // 2) + 1)
                        mm = nc.tensor.matmul(bank(6 + i), g.ident[:, :], (sqk, sqq)[i][:, d, :],
                                              start=(d == 0), stop=(d == D - 1))
                    mm.then_inc(s_ss, 1)

                def sum_pairs(m):
                    pe.wait_ge(s_pq, m + 1)
                    if m >= 2:
                        pe.wait_ge(s_qk, QKP * (m - 1))
                    for d in range(D):
                        mm = nc.tensor.matmul(bank(m % 2)[:, 0:NB * NP], g.ident[:, :], PQ[:, d, :],
                                              start=(d == 0), stop=(d == D - 1))
                    mm.then_inc(s_pqs, 1)

                def sum_x(m, i):
                    n = m * C + i
                    pe.wait_ge(s_xp, m * len(W_PIECES) + (i + 1) * (i + 2))
                    pe.wait_ge(s_xpu, n + 1)
                    if n >= 2:
                        pe.wait_ge(s_w, n - 1)
                        pe.wait_ge(s_u, n - 1)
                    for j in range(i + 1):
                        mm = nc.tensor.matmul(bank(2 + n % 2)[:, 0:2 * D * NB], g.ident[:, :],
                                              XP[:, i * (i + 1) // 2 + j, :, :].rearrange("p x n -> p (x n)"),
                                              start=(j == 0), stop=(j == i))
                    mm.then_inc(s_xs, 1)

                def sum_o(m):
                    for i in range(C):
                        if m < M - 1:
                            pe.wait_ge(s_op, C * m + i + 1)
                        else:
                            pe.wait_ge(s_opl, i + 1)
                        if m >= 2 and i % 2 == 0:
                            pe.wait_ge(s_rms, m - 1)
                            pe.wait_ge(s_oe, C * (m - 2) + i + 2)
                        for x in range(D + i + 1):
                            mm = nc.tensor.matmul(bank(o_bank(m, i))[:, i % 2 * NB * D:(i % 2 + 1) * NB * D],
                                                  g.ident[:, :], OT[:, m % 2, x, i, :, :].rearrange("p n v -> p (n v)"),
                                                  start=(x == 0), stop=(x == D + i))
                        if i % 2 == 1:
                            mm.then_inc(s_os, 1)

                def sum_squares(m):
                    pe.wait_ge(s_osq, m + 1)
                    t = slice(m * TC, (m + 1) * TC)
                    for d in range(D):
                        mm = nc.tensor.matmul(bank(o_bank(m, 0))[:, 0:TC], g.ident[:, :], osq[:, d, t],
                                              start=(d == 0), stop=(d == D - 1))
                    mm.then_inc(s_ms, 1)

                sum_norm(0)
                sum_pairs(0)
                sum_norm(1)
                sum_pairs(1)
                for i in range(C):
                    sum_x(0, i)
                for m in range(M):
                    if m >= 2:
                        sum_squares(m - 2)
                    if m + 1 < M:
                        for i in range(C):
                            sum_x(m + 1, i)
                    if m + 2 < M:
                        sum_pairs(m + 2)
                    if m >= 1:
                        sum_o(m - 1)
                sum_squares(M - 2)
                sum_o(M - 1)
                sum_squares(M - 1)

            @block.gpsimd
            def _(pool):
                def pair_products(m):
                    if m >= 1:
                        pool.wait_ge(s_pqs, m)
                    at = slice(m * NB, (m + 1) * NB)
                    for d in range(C):
                        for first, where in ((q4, qk_at[d]), (k4, kk_at[d])):
                            if where is None:
                                continue
                            w = W_OF[d]
                            ins = nc.gpsimd.tensor_tensor(chunk_pairs(PQ[:, :, :], where, w),
                                                          first[:, :, at, d:C], k4[:, :, at, 0:w], ALU.mult)
                    ins.then_inc(s_pq, 1)

                def decayed_keys(m):
                    pool.wait_ge(s_cp, 2 * C)
                    if m >= 2:
                        pool.wait_ge(s_p2, (m - 1) * NB)
                    at = slice(m * NB, (m + 1) * NB)
                    nc.gpsimd.tensor_tensor(kd[:, m % 2].rearrange("p d n c -> p d (n c)"),
                                            k4[:, :, at, :].rearrange("p d n c -> p d (n c)"),
                                            bc(kdc[:, at, :].rearrange("p n c -> p (n c)"), 1, D),
                                            ALU.mult).then_inc(s_kd, 1)

                def u_terms(m):
                    pool.wait_ge(s_prep, (m + 1) * PREP)
                    at = slice(m * NB, (m + 1) * NB)
                    for i in range(C):
                        if m >= 1:
                            pool.wait_ge(s_xs, (m - 1) * C + i + 1)
                        x0 = i * (i + 1) // 2
                        for j in range(i + 1):
                            ins = nc.gpsimd.tensor_tensor(
                                XP[:, x0 + j, D:2 * D, :], v4[:, :, at, j], bc(TU[:, :, i, j], 1, D), ALU.mult)
                        ins.then_inc(s_xpu, 1)

                def scale_queries(m):
                    pool.wait_ge(s_pq, m + 1)
                    at = slice(m * NB, (m + 1) * NB)
                    nc.gpsimd.tensor_tensor(q4[:, :, at, :].rearrange("p d n c -> p d (n c)"),
                                            q4[:, :, at, :].rearrange("p d n c -> p d (n c)"),
                                            bc(qgc[:, at, :].rearrange("p n c -> p (n c)"), 1, D),
                                            ALU.mult).then_inc(s_qg, 1)

                def normalize(m):
                    t = slice(m * TC, (m + 1) * TC)
                    pool.wait_ge(s_inv, m + 1)
                    nc.gpsimd.tensor_tensor(g.o[:, :, t], g.o[:, :, t], bc(ms[:, t], 1, D), ALU.mult).then_inc(s_o, 1)

                def coefficients():
                    pool.wait_ge(s_rt, 2)
                    pool.wait_ge(s_E, 1)
                    for i in range(C):
                        nc.gpsimd.tensor_tensor(qgc[:, :, i], E4[:, i, :, i], rq3[:, :, i], ALU.mult).then_inc(s_cp, 1)
                        if i < C - 1:
                            nc.gpsimd.tensor_tensor(kdc[:, :, i], E4[:, C - 2 - i, :, C - 1], rk3[:, :, i],
                                                    ALU.mult).then_inc(s_cp, 1)
                        else:
                            nc.gpsimd.tensor_copy(kdc[:, :, i], rk3[:, :, i]).then_inc(s_cp, 1)

                def later_coefficients():
                    at = slice(EARLY * NB, N)
                    pool.wait_ge(s_sig, 1)
                    nc.gpsimd.tensor_scalar(nb3[:, at, :], b3[:, at, :], -1.0, None, ALU.mult).then_inc(s_cb, 1)
                    pool.wait_ge(s_cb, 1)
                    nc.gpsimd.tensor_tensor(nb3[:, at, :], nb3[:, at, :], rk3[:, at, :], ALU.mult).then_inc(s_cb, 1)
                    pool.wait_ge(s_cb, 2)
                    for i in range(C):
                        ins = nc.gpsimd.tensor_tensor(nbg[:, at, i], E4[:, i, at, i], nb3[:, at, i], ALU.mult)
                    ins.then_inc(s_cb, 1)
                    for n, (dst, a, b) in enumerate(pair_coefficients(EARLY, M)):
                        if n == C - 1:
                            pool.wait_ge(s_cb, 3 + n)
                        if n == 2 * (C - 1):
                            pool.wait_ge(s_cb, 3 + n)
                        nc.gpsimd.tensor_tensor(dst, a, b, ALU.mult).then_inc(s_cb, 1)
                    pool.wait_ge(s_cb, 3 + 3 * C - 2)
                    nc.gpsimd.nop().then_inc(s_cf, 1)

                nc.gpsimd.memset(G, 0.0).then_inc(s_G0, 1)
                nc.gpsimd.memset(zero[:, :], 0.0).then_inc(s_zero, 1)
                pair_products(0)
                pair_products(1)
                coefficients()
                decayed_keys(0)
                for m in range(M):
                    if m == 0:
                        later_coefficients()
                    if m >= 1:
                        pool.wait_ge(s_qg, m)
                        pool.wait_ge(s_r1, m * NB)
                        if m >= 3:
                            pool.wait_ge(s_os, 2 * (m - 2))
                        for i in range(C):
                            output_products(nc.gpsimd, m - 1, i).then_inc(s_op, 1)
                    if m + 1 < M:
                        u_terms(m + 1)
                    if m == 0:
                        scale_queries(0)
                    if m + 1 < M:
                        scale_queries(m + 1)
                    if m + 2 < M:
                        pair_products(m + 2)
                    if m + 1 < M:
                        decayed_keys(m + 1)
                    if m >= 2:
                        normalize(m - 2)
                normalize(M - 2)

            @block.scalar
            def _(act):
                chain, beta, half = Chain(act, s_act), g.beta[:, :], D // 2

                def squares(src, dst):
                    for h in range(2):
                        ch = slice(h * half, (h + 1) * half)
                        nc.scalar.activation(dst[:, ch, :], src[:, ch, :], ACT.Square).then_inc(s_sq, 1)

                squares(g.k, sqk)
                nc.scalar.activation(beta, beta, ACT.Exp, scale=-1.0).then_inc(s_act1, 1)
                act.wait_ge(s_z, 1)
                nc.scalar.activation(a_ex, zabs, ACT.Exp).then_inc(s_act1, 1)
                act.wait_ge(s_act1, 2)
                nc.scalar.activation(a_s, a_ex, ACT.Ln, bias=g.two[:, :]).then_inc(s_act1, 1)
                nc.scalar.activation(beta, beta, ACT.Ln, bias=g.one[:, :]).then_inc(s_act1, 1)
                act.wait_ge(s_act1, 4)
                nc.scalar.activation(a_s, a_s, ACT.Exp, scale=-1.0).then_inc(s_ee, 1)
                nc.scalar.activation(beta, beta, ACT.Exp, scale=-1.0).then_inc(s_sig, 1)
                nc.scalar.activation(g.A_log[:, :], g.A_log[:, :], ACT.Exp).then_inc(s_ea, 1)
                squares(g.q[:, :, :], sqq)
                act.wait_ge(s_ss, 2)
                nc.scalar.activation(rk[:, :], bank(6), ACT.Ln, bias=g.eps6[:, :]).then_inc(s_act1, 1)
                chain(nc.scalar.activation(rq[:, :], bank(7), ACT.Ln, scale=float(D), bias=g.eps6d[:, :]))
                act.wait_ge(s_act1, 5)
                nc.scalar.activation(rk[:, :], rk[:, :], ACT.Exp, scale=-0.5).then_inc(s_rt, 1)
                nc.scalar.activation(rq[:, :], rq[:, :], ACT.Exp, scale=-0.5).then_inc(s_rt, 1)
                act.wait_ge(s_G, 1)
                nc.scalar.activation(E, G, ACT.Exp).then_inc(s_E, 1)

                def place_x(m, i):
                    n = m * C + i
                    if m >= 2:
                        act.wait_ge(s_p1, (m - 1) * NB)
                        act.wait_ge(s_ur, 2 * (m - 1))
                    act.wait_ge(s_xs, n + 1)
                    src = bank(2 + n % 2)[:, 0:2 * D * NB].rearrange("p (x n) -> p n x", n=NB)
                    nc.scalar.copy(W[:, m % 2, :, i, :], src[:, :, 0:D]).then_inc(s_w, 1)
                    nc.scalar.copy(U[:, m % 2, :, i, :], src[:, :, D:]).then_inc(s_u, 1)

                def u_to_ring(h):
                    m = h // 2
                    act.wait_ge(s_u, C * (m + 1))
                    if h >= 2:
                        act.wait_ge(s_r1, (h - 1) * RP)
                    n0 = h % 2 * RP
                    nc.scalar.copy(P1[:, n0:n0 + RP, :, :, D].rearrange("p n i v -> p (n i v)"),
                                   U[:, m % 2, n0:n0 + RP, :, :].rearrange("p n i v -> p (n i v)")).then_inc(s_ur, 1)

                def decay(n):
                    act.wait_ge(s_r2, n + 1)
                    nc.scalar.activation(P2[:, n % 2, :, C], S[:, n % SR, :, :].rearrange("p k v -> p (k v)"),
                                         ACT.Copy, scale=Gam[:, n:n + 1]).then_inc(s_dec, 1)

                def place_o(m):
                    for i in range(C):
                        act.wait_ge(s_os, 2 * m + i // 2 + 1)
                        src = bank(o_bank(m, i))[:, i % 2 * NB * D:(i % 2 + 1) * NB * D]
                        nc.scalar.copy(blocks(g.o[:, :, :])[:, :, m * NB:(m + 1) * NB, i],
                                       src.rearrange("p (n v) -> p v n", v=D)).then_inc(s_oe, 1)
                    act.wait_ge(s_oe, C * (m + 1))
                    t = slice(m * TC, (m + 1) * TC)
                    nc.scalar.activation(osq[:, :, t], g.o[:, :, t], ACT.Square).then_inc(s_osq, 1)

                def rms(m):
                    act.wait_ge(s_ms, m + 1)
                    t = slice(m * TC, (m + 1) * TC)
                    nc.scalar.activation(ms[:, t], bank(o_bank(m, 0))[:, 0:TC], ACT.Sqrt, scale=1.0 / D, bias=g.eps5[:, :]).then_inc(s_rms, 1)

                for i in range(C):
                    place_x(0, i)
                u_to_ring(0)
                u_to_ring(1)
                for m in range(M):
                    for n in range(m * NB, (m + 1) * NB):
                        decay(n)
                        b = n % NB
                        if b == 3 and m >= 2:
                            place_o(m - 2)
                        if b == 7 and m >= 2:
                            rms(m - 2)
                        if b == NB - 3 and m == M - 1:
                            place_o(M - 2)
                        if m + 1 < M and b in PLACE_AT:
                            place_x(m + 1, PLACE_AT.index(b))
                        if m + 1 < M and b == NB - 2:
                            u_to_ring(2 * (m + 1))
                    if m + 1 < M:
                        u_to_ring(2 * (m + 1) + 1)
                rms(M - 2)
                place_o(M - 1)
                rms(M - 1)

            @block.vector
            def _(dve):
                v, do = nc.vector, Chain(dve, s_dve)
                do(v.tensor_scalar(g.z[:, :], g.z[:, :], g.dt_bias[:, :], None, ALU.add))
                v.scalar_tensor_tensor(out=zabs, in0=g.z[:, :], scalar=-1.0, in1=g.z[:, :], op0=ALU.mult,
                                       op1=ALU.min).then_inc(s_z, 1)
                dve.wait_ge(s_ee, 1)
                do(v.tensor_tensor(a_s, a_s, a_ex, ALU.mult))
                do(v.tensor_tensor(a_s2, a_s, a_s, ALU.mult))
                do(v.tensor_scalar(a_p, a_s2, 2.0 / 17, None, ALU.mult))
                for c in (15, 13, 11, 9, 7, 5, 3):
                    do(v.scalar_tensor_tensor(out=a_p, in0=a_p, scalar=2.0 / c, in1=a_s2, op0=ALU.add, op1=ALU.mult))
                do(v.scalar_tensor_tensor(out=a_p, in0=a_p, scalar=2.0, in1=a_s, op0=ALU.add, op1=ALU.mult))
                do(v.scalar_tensor_tensor(out=a_p, in0=g.z[:, :], scalar=0.0, in1=a_p, op0=ALU.max, op1=ALU.add))
                dve.wait_ge(s_ea, 1)
                dve.wait_ge(s_G0, 1)
                do(v.tensor_scalar(G[:, 0, :], a_p, g.A_log[:, :], -1.0, ALU.mult, ALU.mult))
                for d in range(1, C):
                    ins = v.tensor_tensor(G4[:, d, :, d:C], G4[:, d - 1, :, d:C], G4[:, 0, :, 0:C - d], ALU.add)
                    if d < C - 1:
                        do(ins)
                ins.then_inc(s_G, 1)
                dve.wait_ge(s_E, 1)
                do(v.tensor_copy(Gam[:, :], E4[:, C - 1, :, C - 1]))
                at = slice(0, EARLY * NB)
                dve.wait_ge(s_rt, 1)
                dve.wait_ge(s_sig, 1)
                do(v.scalar_tensor_tensor(out=nb3[:, at, :], in0=b3[:, at, :], scalar=-1.0, in1=rk3[:, at, :],
                                          op0=ALU.mult, op1=ALU.mult))
                for i in range(C):
                    v.tensor_tensor(nbg[:, at, i], E4[:, i, at, i], nb3[:, at, i], ALU.mult).then_inc(s_nbg, 1)
                dve.wait_ge(s_rt, 2)
                for n, (dst, a, b) in enumerate(pair_coefficients(0, EARLY)):
                    if n in (C - 1, 2 * (C - 1)):
                        dve.wait_ge(s_cq, n)
                    v.tensor_tensor(dst, a, b, ALU.mult).then_inc(s_cq, 1)
                dve.wait_ge(s_cq, 3 * C - 2)
                dve.wait_ge(s_nbg, C)

                def scale_pairs(m, piece, pieces):
                    w = NB * NP // pieces
                    at = slice(piece * w, (piece + 1) * w)
                    dve.wait_ge(s_pqs, m + 1)
                    if m >= EARLY and piece == 0:
                        dve.wait_ge(s_cf, 1)
                    v.tensor_tensor(QK[:, m, at], bank(m % 2)[:, at], QK[:, m, at], ALU.mult).then_inc(s_qk, QKP // pieces)

                def prep(m, step):
                    at = slice(m * NB, (m + 1) * NB)
                    kk = [None] + [pairs(QK[:, m, :], kk_at[d], W_OF[d]) for d in range(1, C)]
                    diag = lambda ap, d: ap.rearrange("p n i j -> p n (i j)")[:, :, d * C::C + 1]
                    if step == 0:
                        dve.wait_ge(s_qk, QKP * (m + 1))
                        ins = v.tensor_tensor(T2[:, :, :], kk[1][:, :, 1:3], kk[1][:, :, 0:2], ALU.mult)
                        return ins.then_inc(s_prep, 1)
                    dve.wait_ge(s_prep, m * PREP + step)
                    if step == 1:
                        ins = v.tensor_tensor(T2[:, :, :], T2[:, :, :], kk[2], ALU.add)
                    elif step == 2:
                        ins = v.tensor_tensor(T3[:, 0, :], kk[2][:, :, 1], kk[1][:, :, 0], ALU.mult)
                    elif step == 3:
                        ins = v.tensor_tensor(T3[:, 1, :], kk[1][:, :, 2], T2[:, :, 0], ALU.mult)
                    elif step == 4:
                        ins = v.tensor_tensor(T3[:, 0, :], T3[:, 0, :], T3[:, 1, :], ALU.add)
                    elif step == 5:
                        ins = v.tensor_tensor(T3[:, 2, :], T3[:, 0, :], kk[3][:, :, 0], ALU.add)
                    else:
                        dst, src = ((TW, nbg), (TU, b3))[(step - 6) % 2]
                        d = (step - 6) // 2
                        if dst is TU and m >= 1:
                            dve.wait_ge(s_xpu, m * C)
                        if d == 0:
                            ins = v.tensor_copy(diag(dst[:, :, :, :], 0), src[:, at, :])
                        else:
                            t = (kk[1], T2[:, :, :], T3[:, 2:3, :].rearrange("p o n -> p n o"))[d - 1]
                            ins = v.tensor_tensor(diag(dst[:, :, :, :], d), t, src[:, at, 0:C - d], ALU.mult)
                    return ins.then_inc(s_prep, 1)

                def w_terms(m, i, js, ds):
                    dve.wait_ge(s_prep, (m + 1) * PREP)
                    if m >= 1:
                        dve.wait_ge(s_xs, (m - 1) * C + i + 1)
                    x0, at = i * (i + 1) // 2, slice(m * NB, (m + 1) * NB)
                    return v.tensor_tensor(XP[:, x0 + js.start:x0 + js.stop, ds, :],
                                           k4[:, ds, at, js].rearrange("p d n j -> p j d n"),
                                           bc(TW[:, :, i, js].rearrange("p n j -> p j n"), 2, ds.stop - ds.start),
                                           ALU.mult)

                def fill_gap(m, n):
                    if n < QKP:
                        scale_pairs(m, n, QKP)
                    elif n < QKP + PREP:
                        prep(m, n - QKP)
                    elif n < GAPS:
                        i, j, h = W_PIECES[n - QKP - PREP]
                        w_terms(m, i, slice(j, j + 1), slice(h * D // 2, (h + 1) * D // 2)).then_inc(s_xp, 1)

                def inverse(m):
                    dve.wait_ge(s_rms, m + 1)
                    t = slice(m * TC, (m + 1) * TC)
                    v.reciprocal(ms[:, t], ms[:, t]).then_inc(s_inv, 1)

                scale_pairs(0, 0, 1)
                for step in range(PREP):
                    prep(0, step)
                for i in range(C):
                    js, x0 = slice(0, i + 1), i * (i + 1) // 2
                    w_terms(0, i, js, slice(0, D)).then_inc(s_xp, 2 * (i + 1))
                    v.tensor_tensor(XP[:, x0:x0 + i + 1, D:2 * D, :], v4[:, :, 0:NB, js].rearrange("p d n j -> p j d n"),
                                    bc(TU[:, :, i, js].rearrange("p n j -> p j n"), 2, D), ALU.mult).then_inc(s_xpu, 1)
                v.memset(S[:, 0, :, :], 0.0).then_inc(s_r2, 1)
                for n in range(N):
                    m, b = divmod(n, NB)
                    if b == 0:
                        dve.wait_ge(s_kd, m + 1)
                        dve.wait_ge(s_w, C * (m + 1))
                    if b % RP == 0:
                        dve.wait_ge(s_ur, n // RP + 1)
                    dve.wait_ge(s_r2, n + 1)
                    v.tensor_tensor(P1[:, n % (2 * RP), :, :, 0:D],
                                    bc(S[:, n % SR, :, :].rearrange("p k v -> p v k"), 1, C),
                                    bc(W[:, m % 2, b, :, :], 2, D), ALU.mult).then_inc(s_p1, 1)
                    if m + 1 < M:
                        fill_gap(m + 1, 4 * b)
                    if b == 0 and m >= 2:
                        dve.wait_ge(s_op, C * (m - 1))
                    dve.wait_ge(s_p1, n + 1)
                    v.tensor_reduce(V[:, m % 2, b, :, :], P1[:, n % (2 * RP), :, :, :], AX_X,
                                    ALU.add).then_inc(s_r1, 1)
                    if m + 1 < M:
                        fill_gap(m + 1, 4 * b + 1)
                    dve.wait_ge(s_r1, n + 1)
                    v.tensor_tensor(P2[:, n % 2, :, 0:C].rearrange("p (k v) c -> p k v c", v=D),
                                    bc(V[:, m % 2, b, :, :].rearrange("p c v -> p v c"), 1, D),
                                    bc(kd[:, m % 2, :, b, :], 2, D), ALU.mult).then_inc(s_p2, 1)
                    if b == NB - 1 and m >= 2:
                        dve.wait_ge(s_op, C * (m - 1))
                    if m + 1 < M:
                        fill_gap(m + 1, 4 * b + 2)
                    if b == NB - 4 and m >= 2:
                        inverse(m - 2)
                    dve.wait_ge(s_p2, n + 1)
                    dve.wait_ge(s_dec, n + 1)
                    v.tensor_reduce(S[:, (n + 1) % SR, :, :].rearrange("p k v -> p (k v)"), P2[:, n % 2, :, :],
                                    AX_X, ALU.add).then_inc(s_r2, 1)
                    if m + 1 < M:
                        fill_gap(m + 1, 4 * b + 3)
                dve.wait_ge(s_r1, N)
                dve.wait_ge(s_qg, M)
                dve.wait_ge(s_os, 2 * (M - 2))
                for i in range(C):
                    output_products(v, M - 1, i).then_inc(s_opl, 1)
                inverse(M - 2)
                inverse(M - 1)
                dve.wait_ge(s_inv, M)
                t = slice((M - 1) * TC, M * TC)
                v.tensor_tensor(g.o[:, :, t], g.o[:, :, t], bc(ms[:, t], 1, D), ALU.mult)


class Norm:

    def __init__(self, core, g, name, banks, dve_tiles=0):
        self.nc, self.g, self.TB, self.banks = core.nc, g, g.T // P, banks
        self.dve_tiles, self.s_xnv = dve_tiles, core.sem(name + "_xn_dve")
        self.s_st, self.s_mv, self.s_std, self.s_rc, self.s_scale, self.s_xn, self.s_tr, self.s_ev = (
            core.sem(f"{name}_{n}") for n in ("stats", "mv", "std", "recip", "scale", "xn", "tr", "evac"))

    def tiles(self, b):
        return range(b * self.TB, (b + 1) * self.TB)

    def statistics(self, dve, b):
        for t in self.tiles(b):
            self.nc.vector.bn_stats(self.g.nstats[:, t, :], self.g.x[:, t, :]).then_inc(self.s_st, 1)
        for t in self.tiles(b):
            dve.wait_ge(self.s_st, t + 1)
            self.nc.vector.bn_aggr(self.g.nmv[:, t, :], self.g.nstats[:, t, :]).then_inc(self.s_mv, 1)

    def std(self, act, b):
        t = self.tiles(b)
        act.wait_ge(self.s_mv, t.stop)
        self.nc.scalar.activation(self.g.rstd[:, t.start:t.stop], self.g.nmv[:, t.start:t.stop, 1], ACT.Sqrt,
                                  bias=self.g.eps5[:, :]).then_inc(self.s_std, 1)

    def scale(self, dve, b):
        t = self.tiles(b)
        r = self.g.rstd[:, t.start:t.stop]
        dve.wait_ge(self.s_std, b + 1)
        self.nc.vector.reciprocal(r, r).then_inc(self.s_rc, 1)
        dve.wait_ge(self.s_rc, b + 1)
        self.nc.vector.scalar_tensor_tensor(out=self.g.nmr[:, t.start:t.stop], in0=self.g.nmv[:, t.start:t.stop, 0],
                                            scalar=-1.0, in1=r, op0=ALU.mult, op1=ALU.mult).then_inc(self.s_scale, 1)

    def normalize(self, act, b):
        act.wait_ge(self.s_scale, b + 1)
        for t in self.tiles(b)[:self.TB - self.dve_tiles]:
            self.nc.scalar.activation(self.g.xn[:, t, :], self.g.x[:, t, :], ACT.Identity,
                                      scale=self.g.rstd[:, t:t + 1], bias=self.g.nmr[:, t:t + 1]).then_inc(self.s_xn, 1)

    def normalize_dve(self, dve, b):
        dve.wait_ge(self.s_scale, b + 1)
        for t in self.tiles(b)[self.TB - self.dve_tiles:]:
            self.nc.vector.tensor_scalar(self.g.xn[:, t, :], self.g.x[:, t, :], self.g.nmv[:, t, 0:1],
                                         self.g.rstd[:, t:t + 1], ALU.subtract, ALU.mult).then_inc(self.s_xnv, 1)

    def turn(self, pe, b):
        if b >= 2:
            pe.wait_ge(self.s_ev, b - 1)
        pe.wait_ge(self.s_xn, (b + 1) * (self.TB - self.dve_tiles))
        if self.dve_tiles:
            pe.wait_ge(self.s_xnv, (b + 1) * self.dve_tiles)
        for i, t in enumerate(self.tiles(b)):
            tr = self.nc.tensor.transpose(self.g.bank(self.banks[b % 2])[:, i * P:(i + 1) * P], self.g.xn[:, t, :],
                                          self.g.ident[:, :])
        tr.then_inc(self.s_tr, 1)

    def evacuate(self, act, b):
        act.wait_ge(self.s_tr, b + 1)
        self.nc.scalar.copy(self.g.xT[:, b, 1:], self.g.bank(self.banks[b % 2])).then_inc(self.s_ev, 1)


def delta_out(core, g):
    nc = core.nc
    T, B = g.T, g.B
    TB = T // P
    with ExitStack() as ctx:
        oT = core.sb("C_oT", [P, B, T], F32, ctx)
        s_oT = [core.sem(f"C_oT{b}") for b in range(B)]
        s_g, s_mm, s_add = (core.sem("C_" + n) for n in ("gated", "mm", "added"))
        ln = Norm(core, g, "C_ln", (0, 1))
        ybank = lambda b: g.bank(2 + b % 6)
        with nc.Block() as block:

            @block.sync
            def _(sp):
                for b in range(B):
                    sp.dma_start(oT[:, b, :], g.o[b * g.NH:(b + 1) * g.NH, :, :]).then_inc(s_oT[b], 16)

            @block.gpsimd
            def _(pool):
                for b in range(B):
                    pool.wait_ge(s_oT[b], 16)
                    nc.gpsimd.tensor_tensor(oT[:, b, :], oT[:, b, :], g.gateT[:, b, :], ALU.mult).then_inc(s_g, 1)

            @block.tensor
            def _(pe):
                for b in range(B + 4):
                    if b < B:
                        pe.wait_ge(s_g, b + 1)
                        if b >= 6:
                            pe.wait_ge(s_add, b - 5)
                        for t in range(TB):
                            mm = nc.tensor.matmul(ybank(b)[:, t * P:(t + 1) * P], oT[:, b, t * P:(t + 1) * P],
                                                  g.woT[:, :], start=True, stop=True)
                        mm.then_inc(s_mm, 1)
                    if b >= 4:
                        ln.turn(pe, b - 4)

            @block.vector
            def _(dve):
                for b in range(B + 1):
                    if b < B:
                        dve.wait_ge(s_mm, b + 1)
                        xb = g.x[:, b * TB:(b + 1) * TB, :].rearrange("p a c -> p (a c)")
                        nc.vector.tensor_tensor(xb, xb, ybank(b), ALU.add).then_inc(s_add, 1)
                        dve.wait_ge(s_add, b + 1)
                        ln.statistics(dve, b)
                    if b >= 1:
                        ln.scale(dve, b - 1)

            @block.scalar
            def _(act):
                for b in range(B + 3):
                    if b < B:
                        ln.std(act, b)
                    if 1 <= b <= B:
                        ln.normalize(act, b - 1)
                    if b >= 3:
                        ln.evacuate(act, b - 3)


def moe(core, g, din):
    nc, T, B, NT = core.nc, g.T, g.B, g.NT
    E = din["L0_ffn_w_router"].shape[1]
    NX = E - 1
    HID = din["L0_ffn_ws_up"].shape[1]
    HC = HID // P
    NS = (NT * P + E * (P - 1)) // P
    ALPHA = 2.0
    with ExitStack() as ctx:
        sb = lambda n, s, dt=F32: core.sb(n, s, dt, ctx)
        xn, xT = g.xn, g.xT[:, :, 1:]
        w_up, w_gate = sb("M_w_up", [P, NX * HID]), sb("M_w_gate", [P, NX * HID])
        w_down = sb("M_w_down", [P, NX * HC * P])
        ws_up, ws_gate, ws_down = sb("M_ws_up", [P, HID]), sb("M_ws_gate", [P, HID]), sb("M_ws_down", [P, HC, P])
        w_r = sb("M_w_router", [P, E])
        weight = sb("M_weight", [P, NT])
        slot = sb("M_slot", [P, NT], I32)
        tile_expert = sb("M_tile_expert", [1, NS], I32)
        s_wr, s_ws, s_wx = (core.sem("M_" + n) for n in ("router_loaded", "shared_loaded", "experts_loaded"))

        def load_weights(sp):
            sp.dma_start(ws_up[:, :], din["L0_ffn_ws_up"]).then_inc(s_ws, 16)
            sp.dma_start(ws_gate[:, :], din["L0_ffn_ws_gate"]).then_inc(s_ws, 16)
            sp.dma_start(ws_down[:, :, :], din["L0_ffn_ws_down"].rearrange("(c p) n -> p c n", p=P)).then_inc(s_ws, 16)
            sp.dma_start(w_up[:, :].rearrange("p (e n) -> p e n", e=NX),
                         din["L0_ffn_w_up"].rearrange("e p n -> p e n")).then_inc(s_wx, 16)
            sp.dma_start(w_gate[:, :].rearrange("p (e n) -> p e n", e=NX),
                         din["L0_ffn_w_gate"].rearrange("e p n -> p e n")).then_inc(s_wx, 16)
            sp.dma_start(w_down[:, :].rearrange("p (e n) -> p e n", e=NX * HC),
                         din["L0_ffn_w_down"].rearrange("e (c p) n -> p (e c) n", p=P)).then_inc(s_wx, 16)

        with ExitStack() as rctx:
            rb = lambda n, s, dt=F32: core.sb(n, s, dt, rctx)
            route(core, g, din, rb, xT, w_r, weight, slot, tile_expert, E, NS, ALPHA, s_wr, load_weights)
        experts(core, g, din, sb, xn, xT, w_up, w_gate, w_down, ws_up, ws_gate, ws_down,
                slot, tile_expert, weight, NX, HID, HC, NS, s_ws, s_wx)


def route(core, g, din, rb, xT, w_r, weight, slot, tile_expert, E, NS, ALPHA, s_wr, load_weights):
    nc, NT, T = core.nc, g.NT, g.T
    lg, oh = rb("R_logits", [P, NT, E]), rb("R_onehot", [P, NT, E])
    ex, rank = rb("R_exp", [P, NT, E]), rb("R_rank", [P, NT, E])
    cum = [rb(f"R_cum{i}", [P, NT, E]) for i in range(2)]
    tot = rb("R_tot", [P, NT, E])
    mx, best, slot_f = rb("R_max", [P, NT]), rb("R_best", [P, NT]), rb("R_slot_f", [P, NT])
    iota_e, iota_t = rb("R_iota_e", [P, E]), rb("R_iota_t", [P, NS])
    low, ones = rb("R_lower", [P, P]), rb("R_ones", [P, P])
    big = rb("R_big", [P, E, NS])
    big2 = rb("R_big2", [P, NS, E])
    nt, end = rb("R_ntiles", [P, E]), [rb(f"R_end{i}", [P, E]) for i in range(2)]
    te = rb("R_te", [P, NS])
    s_c, s_lg, s_ex, s_sub, s_oh, s_cnt, s_dve = (
        core.sem("R_" + n) for n in ("const", "logits", "exp", "sub", "onehot", "count", "dve"))
    with nc.Block() as block:

        @block.sync
        def _(sp):
            sp.dma_start(w_r[:, :], din["L0_ffn_w_router"]).then_inc(s_wr, 16)
            load_weights(sp)
            sp.wait_ge(s_wr, 16)

        @block.gpsimd
        def _(pool):
            nc.gpsimd.iota(iota_e[:, :], [[1, E]], base=-E, channel_multiplier=0,
                           allow_small_or_imprecise_dtypes=True).then_inc(s_c, 1)
            nc.gpsimd.iota(iota_t[:, :], [[1, NS]], base=0, channel_multiplier=0,
                           allow_small_or_imprecise_dtypes=True).then_inc(s_c, 1)
            nc.gpsimd.memset(ones[:, :], 1.0).then_inc(s_c, 1)
            pool.wait_ge(s_c, 3)
            nc.gpsimd.affine_select(out=low[:, :], in_=ones[:, :], compare_op=ALU.is_gt, fill=0.0, base=0,
                                    pattern=[[1, P]], channel_multiplier=-1).then_inc(s_c, 1)

        @block.tensor
        def _(pe):
            pe.wait_ge(s_wr, 16)
            for t in range(NT):
                b, o = t // 4, t % 4 * P
                mm = nc.tensor.matmul(g.bank(0)[:, t * E:(t + 1) * E], xT[:, b, o:o + P], w_r[:, :],
                                      start=True, stop=True)
            mm.then_inc(s_lg, 1)
            pe.wait_ge(s_c, 4)
            pe.wait_ge(s_oh, 1)
            ohf = oh[:, :, :].rearrange("p t e -> p (t e)")
            nc.tensor.matmul(g.bank(1)[:, 0:NT * E], low[:, :], ohf, start=True, stop=True).then_inc(s_cnt, 1)
            nc.tensor.matmul(g.bank(2)[:, 0:NT * E], ones[:, :], ohf, start=True, stop=True).then_inc(s_cnt, 1)

        @block.scalar
        def _(act):
            act.wait_ge(s_sub, 1)
            nc.scalar.activation(ex[:, :, :], ex[:, :, :], ACT.Exp).then_inc(s_ex, 1)

        @block.vector
        def _(dve):
            v, do = nc.vector, Chain(dve, s_dve)
            dve.wait_ge(s_lg, 1)
            do(v.tensor_copy(lg[:, :, :].rearrange("p t e -> p (t e)"), g.bank(0)[:, 0:NT * E]))
            do(v.tensor_reduce(mx[:, :], lg[:, :, :], AX_X, ALU.max))
            v.tensor_tensor(ex[:, :, :], lg[:, :, :], bc(mx[:, :], 2, E), ALU.subtract).then_inc(s_sub, 1)
            do(v.tensor_tensor(oh[:, :, :], lg[:, :, :], bc(mx[:, :], 2, E), ALU.is_equal))
            dve.wait_ge(s_c, 4)
            do(v.tensor_tensor(oh[:, :, :], oh[:, :, :], bc(iota_e[:, :], 1, NT), ALU.mult))
            do(v.tensor_reduce(best[:, :], oh[:, :, :], AX_X, ALU.min))
            v.tensor_tensor(oh[:, :, :], bc(iota_e[:, :], 1, NT), bc(best[:, :], 2, E),
                            ALU.is_equal).then_inc(s_oh, 1)
            dve.wait_ge(s_oh, 1)
            dve.wait_ge(s_ex, 1)
            do(v.tensor_reduce(weight[:, :], ex[:, :, :], AX_X, ALU.add))
            do(v.reciprocal(weight[:, :], weight[:, :]))
            do(v.tensor_scalar(best[:, :], best[:, :], -1.0, ALPHA, ALU.is_lt, ALU.mult))
            do(v.tensor_tensor(weight[:, :], weight[:, :], best[:, :], ALU.mult))
            dve.wait_ge(s_cnt, 2)
            do(v.tensor_copy(rank[:, :, :].rearrange("p t e -> p (t e)"), g.bank(1)[:, 0:NT * E]))
            do(v.tensor_copy(tot[:, :, :].rearrange("p t e -> p (t e)"), g.bank(2)[:, 0:NT * E]))
            src, i, w = tot, 0, 1
            while w < NT:
                dst = cum[i % 2]
                do(v.tensor_copy(dst[:, 0:w, :], src[:, 0:w, :]))
                do(v.tensor_tensor(dst[:, w:, :], src[:, w:, :], src[:, 0:NT - w, :], ALU.add))
                src, i, w = dst, i + 1, 2 * w
            do(v.tensor_scalar(te[:, :], iota_t[:, :], float(P), None, ALU.mult))
            do(v.tensor_tensor(big[:, :, :], bc(src[:, NT - 1, :], 2, NS), bc(te[:, :], 1, E), ALU.is_gt))
            do(v.tensor_reduce(nt[:, :], big[:, :, :], AX_X, ALU.add))
            esrc, i, w = nt, 0, 1
            while w < E:
                dst = end[i % 2]
                do(v.tensor_copy(dst[:, 0:w], esrc[:, 0:w]))
                do(v.tensor_tensor(dst[:, w:], esrc[:, w:], esrc[:, 0:E - w], ALU.add))
                esrc, i, w = dst, i + 1, 2 * w
            do(v.tensor_tensor(big2[:, :, :], bc(esrc[:, :], 1, NS), bc(iota_t[:, :], 2, E), ALU.is_le))
            do(v.tensor_reduce(te[:, :], big2[:, :, :], AX_X, ALU.add))
            do(v.tensor_scalar(te[:, :], te[:, :], float(E - 2), None, ALU.min))
            do(v.tensor_copy(tile_expert[:, :], te[0:1, :]))
            do(v.tensor_tensor(nt[:, :], esrc[:, :], nt[:, :], ALU.subtract))
            do(v.tensor_scalar(nt[:, :], nt[:, :], float(P), None, ALU.mult))
            do(v.tensor_tensor(rank[:, :, :], rank[:, :, :], src[:, :, :], ALU.add))
            do(v.tensor_tensor(rank[:, :, :], rank[:, :, :], tot[:, :, :], ALU.subtract))
            do(v.tensor_tensor(rank[:, :, :], rank[:, :, :], bc(nt[:, :], 1, NT), ALU.add))
            do(v.tensor_tensor(rank[:, :, :], rank[:, :, :], oh[:, :, :], ALU.mult))
            do(v.tensor_reduce(slot_f[:, :], rank[:, :, :], AX_X, ALU.add))
            do(v.tensor_copy(slot[:, :], slot_f[:, :]))


def experts(core, g, din, sb, xn, xT, w_up, w_gate, w_down, ws_up, ws_gate, ws_down,
            slot, tile_expert, weight, NX, HID, HC, NS, s_ws, s_wx):
    nc, T, B, NT = core.nc, g.T, g.B, g.NT
    TB = T // P
    bank = g.bank
    NG = (NS + 3) // 4
    FIRST = B // 2
    xd = sb("X_xd", [P, NG * 4, P])
    xdT = sb("X_xdT", [P, 2, 4 * P])
    sg = sb("X_sg", [P, 2, T])
    hT = sb("X_hT", [P, 2, HC, T])
    h = sb("X_h", [P, 2, HID])
    eT = sb("X_eT", [P, 2, HC * P])
    s_sc, s_ld = core.sem("X_scattered"), core.sem("X_sorted_loaded")
    s_up, s_gt, s_silu, s_h, s_y, s_yadd = (core.sem("X_s_" + n) for n in ("up", "gate", "silu", "h", "y", "yadd"))
    s_xt, s_xe, s_eu, s_eg, s_es, s_eh, s_et, s_ee, s_ey, s_ye, s_yo, s_gi = (
        core.sem("X_e_" + n) for n in ("xT", "xT_evac", "up", "gate", "silu", "h", "hT", "hT_evac", "y",
                                       "y_evac", "y_written", "gathered"))
    s_fin = core.sem("X_added")
    ln = Norm(core, g, "X_ln", (6, 7))
    with nc.Block() as block:

        @block.sync
        def _(sp):
            sp.wait_ge(s_sc, 16 * NT)
            sp.dma_start(xd[:, :, :], g.sorted_x.rearrange("(n p) c -> p n c", p=P)).then_inc(s_ld, 16)
            for j in range(NS):
                sp.wait_ge(s_ye, j + 1)
                sp.dma_start(g.sorted_y[j * P:(j + 1) * P, :], xd[:, j, :]).then_inc(s_yo, 16)
            sp.wait_ge(s_yo, 16 * NS)

        @block.gpsimd
        def _(pool):
            for t in range(NT):
                nc.gpsimd.indirect_dma_start(g.sorted_x, bass.IndirectOffsetOnAxis(slot[:, t:t + 1], 0),
                                             xn[:, t, :], None).then_inc(s_sc, 16)
            pool.wait_ge(s_sc, 16 * NT)
            pool.wait_ge(s_yo, 16 * NS)
            for t in range(NT):
                nc.gpsimd.indirect_dma_start(xn[:, t, :], None, g.sorted_y[0:NS * P, :],
                                             bass.IndirectOffsetOnAxis(slot[:, t:t + 1], 0)).then_inc(s_gi, 16)
            pool.wait_ge(s_gi, 16 * NT)

        @block.tensor
        def _(pe):
            def shared_down(b):
                pe.wait_ge(s_h, (b + 1) * HC)
                if b >= 2:
                    pe.wait_ge(s_yadd, b - 1)
                for t in range(TB):
                    for c in range(HC):
                        mm = nc.tensor.matmul(bank(4 + b % 2)[:, t * P:(t + 1) * P],
                                              hT[:, b % 2, c, t * P:(t + 1) * P], ws_down[:, c, :],
                                              start=(c == 0), stop=(c == HC - 1))
                mm.then_inc(s_y, 1)

            def shared(first, last):
                for b in range(first, last):
                    for c in range(HC):
                        n = b * HC + c
                        if n >= 2:
                            pe.wait_ge(s_h, n - 1)
                        nc.tensor.matmul(bank(n % 2), ws_up[:, c * P:(c + 1) * P], xT[:, b, :],
                                         start=True, stop=True).then_inc(s_up, 1)
                        nc.tensor.matmul(bank(2 + n % 2), ws_gate[:, c * P:(c + 1) * P], xT[:, b, :],
                                         start=True, stop=True).then_inc(s_gt, 1)
                    if b > first:
                        shared_down(b - 1)
                shared_down(last - 1)

            pe.wait_ge(s_ws, 48)
            shared(0, FIRST)
            pe.wait_ge(s_h, FIRST * HC)
            pe.wait_ge(s_yadd, FIRST)
            pe.wait_ge(s_ld, 16)
            pe.wait_ge(s_wx, 48)

            def x_columns(q):
                if q >= 1:
                    pe.wait_ge(s_xe, q)
                for t in range(4):
                    tr = nc.tensor.transpose(bank(4)[:, t * P:(t + 1) * P], xd[:, q * 4 + t, :], g.ident[:, :])
                tr.then_inc(s_xt, 1)

            def h_columns(j):
                pe.wait_ge(s_eh, j + 1)
                if j >= 2:
                    pe.wait_ge(s_ee, j - 1)
                for c in range(HC):
                    tr = nc.tensor.transpose(bank(5 + j % 2)[:, c * P:(c + 1) * P], h[:, j % 2, c * P:(c + 1) * P],
                                             g.ident[:, :])
                tr.then_inc(s_et, 1)

            def down(j, e):
                pe.wait_ge(s_ee, j + 1)
                if j >= 1:
                    pe.wait_ge(s_ye, j)
                for c in range(HC):
                    mm = nc.tensor.matmul(bank(7)[:, 0:P], eT[:, j % 2, c * P:(c + 1) * P],
                                          w_down[:, bass.ds(e * (HC * P) + c * P, P)],
                                          start=(c == 0), stop=(c == HC - 1))
                mm.then_inc(s_ey, 1)

            x_columns(0)
            experts_of = {}
            for j in range(NS):
                if j % 4 == 0 and j // 4 + 1 < NG:
                    if j >= 4:
                        pe.wait_ge(s_ey, j - 2)
                    x_columns(j // 4 + 1)
                e = pe.value_load(tile_expert[0:1, j:j + 1], min_val=0, max_val=NX - 1)
                experts_of[j] = e
                pe.wait_ge(s_xe, j // 4 + 1)
                if j >= 2:
                    pe.wait_ge(s_eh, j - 1)
                xc = xdT[:, (j // 4) % 2, (j % 4) * P:(j % 4 + 1) * P]
                nc.tensor.matmul(bank(j % 2), xc, w_up[:, bass.ds(e * HID, HID)], start=True, stop=True).then_inc(s_eu, 1)
                nc.tensor.matmul(bank(2 + j % 2), xc, w_gate[:, bass.ds(e * HID, HID)], start=True,
                                 stop=True).then_inc(s_eg, 1)
                if j >= 1:
                    h_columns(j - 1)
                if j >= 2:
                    down(j - 2, experts_of[j - 2])
            h_columns(NS - 1)
            down(NS - 2, experts_of[NS - 2])
            down(NS - 1, experts_of[NS - 1])
            pe.wait_ge(s_eh, NS)
            pe.wait_ge(s_ee, NS)
            pe.wait_ge(s_xe, NG)
            shared(FIRST, B)
            pe.wait_ge(s_ye, NS)
            for b in range(B):
                ln.turn(pe, b)

        @block.scalar
        def _(act):
            def shared(first, last):
                for n in range(first * HC, last * HC):
                    act.wait_ge(s_gt, n + 1)
                    if n >= 2:
                        act.wait_ge(s_h, n - 1)
                    nc.scalar.activation(sg[:, n % 2, :], bank(2 + n % 2), ACT.Silu).then_inc(s_silu, 1)

            shared(0, FIRST)
            act.wait_ge(s_h, FIRST * HC)

            def x_evac(q):
                act.wait_ge(s_xt, q + 1)
                if q >= 2:
                    act.wait_ge(s_eg, (q - 1) * 4)
                nc.scalar.copy(xdT[:, q % 2, :], bank(4)).then_inc(s_xe, 1)

            def y_evac(j):
                act.wait_ge(s_ey, j + 1)
                act.wait_ge(s_xt, j // 4 + 1)
                nc.scalar.copy(xd[:, j, :], bank(7)[:, 0:P]).then_inc(s_ye, 1)

            x_evac(0)
            for j in range(NS):
                if j % 4 == 0 and j // 4 + 1 < NG:
                    x_evac(j // 4 + 1)
                act.wait_ge(s_eg, j + 1)
                if j >= 2:
                    act.wait_ge(s_eh, j - 1)
                nc.scalar.activation(sg[:, j % 2, :], bank(2 + j % 2), ACT.Silu).then_inc(s_es, 1)
                if j >= 1:
                    act.wait_ge(s_et, j)
                    if j >= 3:
                        act.wait_ge(s_ey, j - 2)
                    nc.scalar.copy(eT[:, (j - 1) % 2, :], bank(5 + (j - 1) % 2)).then_inc(s_ee, 1)
                if j >= 2:
                    y_evac(j - 2)
            act.wait_ge(s_et, NS)
            act.wait_ge(s_ey, NS - 2)
            nc.scalar.copy(eT[:, (NS - 1) % 2, :], bank(5 + (NS - 1) % 2)).then_inc(s_ee, 1)
            y_evac(NS - 2)
            y_evac(NS - 1)
            act.wait_ge(s_eh, NS)
            shared(FIRST, B)
            for b in range(B + 2):
                if b < B:
                    ln.std(act, b)
                if 1 <= b <= B:
                    ln.normalize(act, b - 1)
                if b >= 2:
                    ln.evacuate(act, b - 2)

        @block.vector
        def _(dve):
            v = nc.vector

            def add_shared(b):
                dve.wait_ge(s_y, b + 1)
                xb = g.x[:, b * TB:(b + 1) * TB, :].rearrange("p a c -> p (a c)")
                v.tensor_tensor(xb, xb, bank(4 + b % 2), ALU.add).then_inc(s_yadd, 1)

            def shared(first, last):
                for b in range(first, last):
                    for c in range(HC):
                        n = b * HC + c
                        dve.wait_ge(s_silu, n + 1)
                        dve.wait_ge(s_up, n + 1)
                        if b >= 2:
                            dve.wait_ge(s_y, b - 1)
                        v.tensor_tensor(hT[:, b % 2, c, :], sg[:, n % 2, :], bank(n % 2), ALU.mult).then_inc(s_h, 1)
                    if b > first:
                        add_shared(b - 1)
                add_shared(last - 1)

            shared(0, FIRST)
            for j in range(NS):
                dve.wait_ge(s_es, j + 1)
                dve.wait_ge(s_eu, j + 1)
                if j >= 2:
                    dve.wait_ge(s_et, j - 1)
                v.tensor_tensor(h[:, j % 2, :], sg[:, j % 2, :], bank(j % 2), ALU.mult).then_inc(s_eh, 1)
            shared(FIRST, B)
            dve.wait_ge(s_yadd, B)
            dve.wait_ge(s_gi, 16 * NT)
            for b in range(B + 1):
                if b < B:
                    for t in ln.tiles(b):
                        v.scalar_tensor_tensor(out=g.x[:, t, :], in0=xn[:, t, :], scalar=weight[:, t:t + 1],
                                               in1=g.x[:, t, :], op0=ALU.mult, op1=ALU.add).then_inc(s_fin, 1)
                    dve.wait_ge(s_fin, (b + 1) * TB)
                    ln.statistics(dve, b)
                if b >= 1:
                    ln.scale(dve, b - 1)


def attention(core, g, din):
    nc, T, B, NT = core.nc, g.T, g.B, g.NT
    bank = g.bank
    HD = 64
    NHD = P // HD
    HALF, R = HD // 2, HD // 4
    KT = T // P
    BASE, LRP, ARM = 10000.0, 17, 2.0
    MIN_L = 1.0 - LRP / 100.0
    SDT_L = (BASE - MIN_L * BASE) * 2.0
    with ExitStack() as ctx:
        sb = lambda n, s, dt=F32: core.sb(n, s, dt, ctx)
        qm = sb("T_qm", [P, NHD, B * T])
        kT = sb("T_kT", [P, B * T])
        vr = sb("T_vr", [P, NT, P])
        wo = sb("T_wo", [P, P])
        bo = sb("T_bo", [P, P])
        orow = sb("T_o", [P, NT, P])
        with ExitStack() as pctx:
            pb = lambda n, s, dt=F32: core.sb(n, s, dt, pctx)
            xT = g.xT[:, :, 1:]
            w = pb("T_w", [P, 5, P])
            bcol = pb("T_bcol", [P, 4])
            bv = pb("T_bv", [P, P])
            freq = pb("T_freq", [P, 4])
            ch = pb("T_ch", [P, 2])
            chi = pb("T_chi", [P, 6], I32)
            cos, sin = pb("T_cos", [P, 2, T]), pb("T_sin", [P, 2, T])
            ang, sq = pb("T_ang", [P, T]), pb("T_sq", [P, T])
            t1, t2 = pb("T_t1", [P, 4, T]), pb("T_t2", [P, 4, T])
            s_w, s_b, s_rot, s_dve, s_act = (core.sem("T_" + n) for n in ("w", "b", "rot", "dve", "act"))
            s_pad = core.sem("T_pad")
            s_io, s_mm, s_t, s_q, s_vm, s_ve = (core.sem("T_" + n) for n in ("iota", "mm", "t", "q", "vmm", "vevac"))
            s_f1, s_f2, s_f3, s_z, s_tab, s_bo = (core.sem("T_" + n) for n in ("f1", "f2", "f3", "zero", "tab", "bo"))
            with nc.Block() as block:

                @block.sync
                def _(sp):
                    for i, n in enumerate(("Wq", "Wk", "Wv")):
                        sp.dma_start(w[:, i, :], din["L1_attn_" + n]).then_inc(s_w, 16)
                    sp.dma_start(wo[:, :], din["L1_attn_Wo"]).then_inc(s_w, 16)
                    sp.dma_start(bo[:, :], bc(din["L1_attn_bo"], 0, P)).then_inc(s_b, 16)
                    sp.dma_start(bv[:, :], bc(din["L1_attn_bv"], 0, P)).then_inc(s_b, 16)
                    sp.dma_start(freq[:, 0:1], bc(din["L1_attn_nrope_freq"], 0, P)).then_inc(s_b, 16)
                    for i, n in enumerate(("bq", "bk")):
                        col = din["L1_attn_" + n].unsqueeze(1)
                        sp.dma_start(bcol[:, i:i + 1], col).then_inc(s_b, 16)
                        for h in range(NHD):
                            o = h * HD
                            sp.dma_start(bcol[o:o + HALF, 2 + i:3 + i], col[o:o + HALF, :]).then_inc(s_b, 16)
                            o += HALF
                            sp.dma_start(bcol[o:o + R, 2 + i:3 + i], col[o + R:o + 2 * R, :]).then_inc(s_b, 16)
                            sp.dma_start(bcol[o + R:o + 2 * R, 2 + i:3 + i], col[o:o + R, :]).then_inc(s_b, 16)
                    sp.wait_ge(s_b, 16 * (3 + 2 * (1 + 3 * NHD)))
                    sp.wait_ge(s_w, 64)

                @block.gpsimd
                def _(pool):
                    nc.gpsimd.memset(qm[:, :, :], 0.0).then_inc(s_z, 1)
                    nc.gpsimd.memset(g.xT[:, :, 0:1], 0.0).then_inc(s_pad, 1)
                    nc.gpsimd.iota(chi[:, 0:1], [[0, 1]], base=0, channel_multiplier=1).then_inc(s_io, 1)
                    nc.gpsimd.iota(ang[:, :], [[1, T]], base=0, channel_multiplier=0,
                                   allow_small_or_imprecise_dtypes=True).then_inc(s_io, 1)
                    pool.wait_ge(s_b, 16 * (3 + 2 * (1 + 3 * NHD)))
                    pool.wait_ge(s_z, 1)
                    nc.gpsimd.tensor_tensor(g.x[:, :, :], g.x[:, :, :], bc(bo[:, :], 1, NT), ALU.add).then_inc(s_bo, 1)
                    pool.wait_ge(s_bo, 1)
                    for b in range(B):
                        for i in range(2):
                            n = b * 2 + i
                            if n >= 1:
                                pool.wait_ge(s_q, b * 4 + 2 * i)
                            pool.wait_ge(s_t, 2 * n + 2)
                            a, c = t1[:, n % 4, :], t2[:, n % 4, :]
                            if i == 0:
                                for h in range(NHD):
                                    if h:
                                        pool.wait_ge(s_q, b * 4 + h)
                                    r = slice(h * HD, (h + 1) * HD)
                                    nc.gpsimd.tensor_tensor(qm[r, h, b * T:(b + 1) * T], a[r, :], c[r, :],
                                                            ALU.add).then_inc(s_q, 1)
                            else:
                                nc.gpsimd.tensor_tensor(kT[:, b * T:(b + 1) * T], a, c, ALU.add).then_inc(s_q, 2)

                @block.scalar
                def _(act):
                    act.wait_ge(s_b, 16 * (3 + 2 * (1 + 3 * NHD)))
                    nc.scalar.activation(freq[:, 1:2], freq[:, 0:1], ACT.Sigmoid).then_inc(s_f1, 1)
                    act.wait_ge(s_f2, 1)
                    nc.scalar.activation(freq[:, 2:3], freq[:, 2:3], ACT.Ln).then_inc(s_f1, 1)
                    act.wait_ge(s_f1, 2)
                    act.wait_ge(s_f3, 1)
                    nc.scalar.activation(freq[:, 3:4], ch[:, 0:1], ACT.Exp, scale=freq[:, 2:3]).then_inc(s_act, 1)
                    act.wait_ge(s_tab, 1)
                    nc.scalar.activation(sin[:, 1, :], ang[:, :], ACT.Sin).then_inc(s_act, 1)
                    nc.scalar.activation(sq[:, :], ang[:, :], ACT.Sin, scale=0.5).then_inc(s_act, 1)

                @block.vector
                def _(dve):
                    v, do = nc.vector, Chain(dve, s_dve)
                    dve.wait_ge(s_w, 64)
                    do(v.memset(w[:, 3:5, :], 0.0))
                    for i in range(2):
                        for h in range(NHD):
                            o = h * HD + HALF
                            do(v.tensor_scalar(w[:, 3 + i, o:o + R], w[:, i, o + R:o + 2 * R], -1.0, None, ALU.mult))
                            do(v.tensor_copy(w[:, 3 + i, o + R:o + 2 * R], w[:, i, o:o + R]))
                    v.nop().then_inc(s_rot, 1)
                    dve.wait_ge(s_io, 2)
                    do(v.tensor_scalar(chi[:, 1:2], chi[:, 0:1], R - 1, None, ALU.bitwise_and))
                    do(v.tensor_scalar(chi[:, 2:3], chi[:, 0:1], HALF, None, ALU.bitwise_and))
                    do(v.tensor_scalar(chi[:, 3:4], chi[:, 0:1], R, None, ALU.bitwise_and))
                    do(v.tensor_copy(ch[:, 0:1], chi[:, 1:2]))
                    do(v.tensor_copy(ch[:, 1:2], chi[:, 2:3]))
                    do(v.tensor_scalar(ch[:, 0:1], ch[:, 0:1], -1.0 / R, None, ALU.mult))
                    do(v.tensor_scalar(ch[:, 1:2], ch[:, 1:2], 1.0 / HALF, None, ALU.mult))
                    f = freq
                    sgn = t1[:, 0, 0:1]
                    do(v.tensor_copy(sgn, chi[:, 3:4]))
                    do(v.tensor_scalar(sgn, sgn, 2.0 / R, -1.0, ALU.mult, ALU.add))
                    dve.wait_ge(s_b, 16 * (3 + 2 * (1 + 3 * NHD)))
                    do(v.tensor_scalar(bcol[:, 2:4], bcol[:, 2:4], sgn, ch[:, 1:2], ALU.mult, ALU.mult))
                    dve.wait_ge(s_f1, 1)
                    v.tensor_scalar(f[:, 2:3], f[:, 1:2], SDT_L, MIN_L * BASE, ALU.mult, ALU.add).then_inc(s_f2, 1)
                    v.nop().then_inc(s_f3, 1)
                    dve.wait_ge(s_act, 1)
                    scale = ARM * float(np.pi) / max(T - 1, 1)
                    do(v.tensor_scalar(ang[:, :], ang[:, :], f[:, 3:4], scale, ALU.mult, ALU.mult))
                    do(v.tensor_scalar(ang[:, :], ang[:, :], -float(np.pi), 3.1415925, ALU.add, ALU.min))
                    v.tensor_scalar(ang[:, :], ang[:, :], -3.1415925, None, ALU.max).then_inc(s_tab, 1)
                    dve.wait_ge(s_act, 3)
                    rot = ch[:, 1:2]
                    do(v.tensor_tensor(sq[:, :], sq[:, :], sq[:, :], ALU.mult))
                    do(v.tensor_scalar(sq[:, :], sq[:, :], 2.0, -2.0, ALU.mult, ALU.add))
                    do(v.tensor_scalar(cos[:, 1, :], sq[:, :], rot, 1.0, ALU.mult, ALU.add))
                    do(v.tensor_scalar(sin[:, 1, :], sin[:, 1, :], rot, -1.0, ALU.mult, ALU.mult))
                    qs = float(HD) ** -0.5
                    do(v.tensor_scalar(cos[:, 0, :], cos[:, 1, :], qs, None, ALU.mult))
                    do(v.tensor_scalar(sin[:, 0, :], sin[:, 1, :], qs, None, ALU.mult))
                    for b in range(B):
                        for i in range(2):
                            n = b * 2 + i
                            dve.wait_ge(s_mm, 2 * n + 1)
                            if n >= 4:
                                dve.wait_ge(s_q, (n // 2 - 2) * 4 + 2 + 2 * i)
                            v.scalar_tensor_tensor(out=t1[:, n % 4, :], in0=bank(2 * i), scalar=bcol[:, i:i + 1],
                                                   in1=cos[:, i, :], op0=ALU.add, op1=ALU.mult).then_inc(s_t, 1)
                            dve.wait_ge(s_mm, 2 * n + 2)
                            v.scalar_tensor_tensor(out=t2[:, n % 4, :], in0=bank(2 * i + 1),
                                                   scalar=bcol[:, 2 + i:3 + i], in1=sin[:, i, :], op0=ALU.add,
                                                   op1=ALU.mult).then_inc(s_t, 1)
                        dve.wait_ge(s_vm, b + 1)
                        v.tensor_tensor(vr[:, b * 4:b * 4 + 4, :], bank(4 + b % 2).rearrange("p (a c) -> p a c", c=P),
                                        bc(bv[:, :], 1, 4), ALU.add).then_inc(s_ve, 1)

                @block.tensor
                def _(pe):
                    pe.wait_ge(s_rot, 1)
                    for b in range(B):
                        for i in range(2):
                            for k in range(2):
                                n = (b * 2 + i) * 2 + k
                                if b >= 1:
                                    pe.wait_ge(s_t, n - 3)
                                nc.tensor.matmul(bank(2 * i + k), w[:, i + 3 * k, :], xT[:, b, :],
                                                 start=True, stop=True).then_inc(s_mm, 1)
                        if b >= 2:
                            pe.wait_ge(s_ve, b - 1)
                        for t in range(KT):
                            mm = nc.tensor.matmul(bank(4 + b % 2)[:, t * P:(t + 1) * P],
                                                  xT[:, b, t * P:(t + 1) * P], w[:, 2, :], start=True, stop=True)
                        mm.then_inc(s_vm, 1)

        with ExitStack() as actx:
            ab = lambda n, s, dt=F32: core.sb(n, s, dt, actx)
            pr = ab("U_p", [P, 3, T])
            pT = ab("U_pT", [P, 2, T])
            nmax, ssum = ab("U_nmax", [P, B * NHD * KT]), ab("U_sum", [P, B * NHD * KT])
            oT = ab("U_oT", [P, 2, T])
            s_sc, s_mx, s_ex, s_pt, s_pe, s_pv, s_rc, s_or, s_ot, s_oe, s_y, s_ya = (
                core.sem("U_" + n) for n in ("scores", "max", "exp", "pT", "pT_evac", "pv", "recip", "o", "oT",
                                             "oT_evac", "y", "added"))
            N = B * NHD * KT
            ln = Norm(core, g, "U_ln", (0, 1), dve_tiles=3)

            def where(n):
                b, rest = divmod(n, NHD * KT)
                qt, h = divmod(rest, NHD)
                return b, h, qt

            with nc.Block() as block:

                @block.tensor
                def _(pe):
                    def scores(n):
                        b, h, qt = where(n)
                        if n >= 3:
                            pe.wait_ge(s_ex, n - 2)
                        nc.tensor.matmul(bank(n % 3), qm[:, h, b * T + qt * P:b * T + (qt + 1) * P],
                                         kT[:, b * T:(b + 1) * T], start=True, stop=True).then_inc(s_sc, 1)

                    def turn(n):
                        pe.wait_ge(s_ex, n + 1)
                        if n >= 2:
                            pe.wait_ge(s_pe, n - 1)
                        for c in range(KT):
                            tr = nc.tensor.transpose(bank(3 + n % 2)[:, c * P:(c + 1) * P],
                                                     pr[:, n % 3, c * P:(c + 1) * P], g.ident[:, :])
                        tr.then_inc(s_pt, 1)

                    def values(n):
                        b, h, qt = where(n)
                        pe.wait_ge(s_pe, n + 1)
                        if n >= 2:
                            pe.wait_ge(s_or, n - 1)
                        for c in range(KT):
                            mm = nc.tensor.matmul(bank(5 + n % 2)[:, 0:P], pT[:, n % 2, c * P:(c + 1) * P],
                                                  vr[:, b * KT + c, :], start=(c == 0), stop=(c == KT - 1))
                        mm.then_inc(s_pv, 1)

                    def project(t):
                        pe.wait_ge(s_or, NHD * (t + 1))
                        if t >= 1:
                            pe.wait_ge(s_ya, t)
                        nc.tensor.transpose(bank(7)[:, 0:P], orow[:, t, :], g.ident[:, :]).then_inc(s_ot, 1)
                        pe.wait_ge(s_oe, t + 1)
                        nc.tensor.matmul(bank(7)[:, P:2 * P], oT[:, t % 2, 0:P], wo[:, :],
                                         start=True, stop=True).then_inc(s_y, 1)

                    for n in range(N + 4):
                        if n < N:
                            scores(n)
                        if 1 <= n <= N:
                            turn(n - 1)
                        if 2 <= n <= N + 1:
                            values(n - 2)
                        if n >= 5 and (n - 5) % NHD == 0 and (n - 5) // NHD < NT:
                            project((n - 5) // NHD)
                    for b in range(B):
                        ln.turn(pe, b)

                def o_evac(act, t):
                    act.wait_ge(s_ot, t + 1)
                    nc.scalar.copy(oT[:, t % 2, 0:P], bank(7)[:, 0:P]).then_inc(s_oe, 1)

                @block.scalar
                def _(act):
                    for n in range(N):
                        act.wait_ge(s_mx, n + 1)
                        if n >= 3:
                            act.wait_ge(s_pt, n - 2)
                        nc.scalar.activation(pr[:, n % 3, :], bank(n % 3), ACT.Exp, bias=nmax[:, n:n + 1],
                                             accum_out=ssum[:, n:n + 1]).then_inc(s_ex, 1)
                        if n >= 5 and (n - 5) % NHD == 0:
                            o_evac(act, (n - 5) // NHD)
                    for t in range((N - 6) // NHD + 1, NT):
                        o_evac(act, t)
                    for b in range(B + 2):
                        if b < B:
                            ln.std(act, b)
                        if 1 <= b <= B:
                            ln.normalize(act, b - 1)
                        if b >= 2:
                            ln.evacuate(act, b - 2)

                @block.vector
                def _(dve):
                    v = nc.vector

                    def finish(n):
                        b, h, qt = where(n)
                        dve.wait_ge(s_rc, n + 1)
                        dve.wait_ge(s_pv, n + 1)
                        v.tensor_scalar(orow[:, b * KT + qt, h * HD:(h + 1) * HD],
                                        bank(5 + n % 2)[:, h * HD:(h + 1) * HD], ssum[:, n:n + 1], None,
                                        ALU.mult).then_inc(s_or, 1)

                    def add(t):
                        dve.wait_ge(s_y, t + 1)
                        v.tensor_tensor(g.x[:, t, :], g.x[:, t, :], bank(7)[:, P:2 * P], ALU.add).then_inc(s_ya, 1)
                        if t % KT == KT - 1:
                            dve.wait_ge(s_ya, t + 1)
                            ln.statistics(dve, t // KT)

                    for n in range(N + 2):
                        if n < N:
                            dve.wait_ge(s_sc, n + 1)
                            v.tensor_reduce(nmax[:, n:n + 1], bank(n % 3), AX_X, ALU.max, negate=True).then_inc(s_mx, 1)
                        if 1 <= n <= N:
                            dve.wait_ge(s_ex, n)
                            v.reciprocal(ssum[:, n - 1:n], ssum[:, n - 1:n]).then_inc(s_rc, 1)
                            dve.wait_ge(s_pt, n)
                            if n >= 3:
                                dve.wait_ge(s_pv, n - 2)
                            v.tensor_copy(pT[:, (n - 1) % 2, :], bank(3 + (n - 1) % 2)).then_inc(s_pe, 1)
                        if n >= 2:
                            finish(n - 2)
                        if n >= 6 and (n - 6) % NHD == 0:
                            add((n - 6) // NHD)
                    for t in range((N + 1 - 6) // NHD + 1, NT):
                        add(t)
                    for b in range(B):
                        ln.scale(dve, b)
                        ln.normalize_dve(dve, b)


def channel_mix(core, g, din, out):
    nc, T, B, NT = core.nc, g.T, g.B, g.NT
    bank = g.bank
    KT = T // P
    with ExitStack() as ctx:
        sb = lambda n, s, dt=F32: core.sb(n, s, dt, ctx)
        xT = g.xT
        w, wT = sb("D_w", [P, 3, P]), sb("D_wT", [P, 3, P])
        mu, imu = sb("D_mu", [P, 2]), sb("D_imu", [P, 2])
        mix = sb("D_mix", [P, 2, 2, T])
        rel, ka = sb("D_rel", [P, 2, T]), sb("D_ka", [P, 2, T])
        r, rv = sb("D_r", [P, 2, T]), sb("D_rv", [P, 2, T])
        s_w, s_mu, s_wt, s_we, s_im = (core.sem("D_" + n) for n in ("w", "mu", "wT", "wT_evac", "imu"))
        s_pv, s_mx, s_k, s_r, s_rel, s_ka, s_sig, s_v, s_rv, s_o = (
            core.sem("D_" + n) for n in ("prev", "mixed", "k", "r", "relu", "kact", "sig", "v", "rv", "o"))
        s_out = g.s_out
        out_v = out.rearrange("b (t p) c -> b p t c", p=P)
        with nc.Block() as block:

            @block.sync
            def _(sp):
                for i, n in enumerate(("W_r", "W_k", "W_v")):
                    sp.dma_start(w[:, i, :], din["L1_ffn_" + n]).then_inc(s_w, 16)
                sp.dma_start(mu[:, 0:1], din["L1_ffn_mu_r"].unsqueeze(1)).then_inc(s_mu, 16)
                sp.dma_start(mu[:, 1:2], din["L1_ffn_mu_k"].unsqueeze(1)).then_inc(s_mu, 16)
                for b in range(B):
                    sp.wait_ge(s_o, b + 1)
                    sp.dma_start(out_v[b], g.x[:, b * KT:(b + 1) * KT, :]).then_inc(s_out, 16)
                sp.wait_ge(s_out, 16 * B)

            @block.tensor
            def _(pe):
                pe.wait_ge(s_w, 48)
                for i in range(3):
                    tr = nc.tensor.transpose(bank(0)[:, i * P:(i + 1) * P], w[:, i, :], g.ident[:, :])
                tr.then_inc(s_wt, 1)
                pe.wait_ge(s_we, 1)

                def values(b):
                    pe.wait_ge(s_ka, b + 1)
                    if b >= 2:
                        pe.wait_ge(s_rv, b - 1)
                    for t in range(KT):
                        mm = nc.tensor.matmul(bank(4 + b % 2)[:, t * P:(t + 1) * P], ka[:, b % 2, t * P:(t + 1) * P],
                                              wT[:, 2, :], start=True, stop=True)
                    mm.then_inc(s_v, 1)

                for b in range(B):
                    pe.wait_ge(s_mx, 2 * b + 2)
                    if b >= 2:
                        pe.wait_ge(s_ka, b - 1)
                        pe.wait_ge(s_sig, b - 1)
                    nc.tensor.matmul(bank(b % 2), wT[:, 1, :], mix[:, b % 2, 1, :], start=True, stop=True).then_inc(s_k, 1)
                    for t in range(KT):
                        mm = nc.tensor.matmul(bank(2 + b % 2)[:, t * P:(t + 1) * P],
                                              mix[:, b % 2, 0, t * P:(t + 1) * P], wT[:, 0, :], start=True, stop=True)
                    mm.then_inc(s_r, 1)
                    if b >= 1:
                        values(b - 1)
                values(B - 1)

            def evac(act, b):
                act.wait_ge(s_k, b + 1)
                if b >= 2:
                    act.wait_ge(s_ka, b - 1)
                nc.scalar.activation(rel[:, b % 2, :], bank(b % 2), ACT.Relu).then_inc(s_rel, 1)
                act.wait_ge(s_r, b + 1)
                if b >= 2:
                    act.wait_ge(s_rv, b - 1)
                nc.scalar.activation(r[:, b % 2, :], bank(2 + b % 2), ACT.Sigmoid).then_inc(s_sig, 1)

            @block.scalar
            def _(act):
                act.wait_ge(s_im, 1)
                for b in range(B):
                    if b >= 2:
                        act.wait_ge(s_r, b - 1)
                        act.wait_ge(s_k, b - 1)
                    for i in range(2):
                        nc.scalar.activation(mix[:, b % 2, i, :], xT[:, b, 0:T], ACT.Copy,
                                             scale=imu[:, i:i + 1]).then_inc(s_pv, 1)
                    if b >= 1:
                        evac(act, b - 1)
                evac(act, B - 1)

            def act_k(dve, b):
                dve.wait_ge(s_rel, b + 1)
                if b >= 2:
                    dve.wait_ge(s_v, b - 1)
                nc.vector.tensor_tensor(ka[:, b % 2, :], rel[:, b % 2, :], bank(b % 2), ALU.mult).then_inc(s_ka, 1)

            @block.vector
            def _(dve):
                v = nc.vector
                dve.wait_ge(s_mu, 32)
                v.tensor_scalar(imu[:, :], mu[:, :], -1.0, 1.0, ALU.mult, ALU.add).then_inc(s_im, 1)
                dve.wait_ge(s_wt, 1)
                v.tensor_copy(wT[:, :, :].rearrange("p a c -> p (a c)"), bank(0)[:, 0:3 * P]).then_inc(s_we, 1)

                def gate(b):
                    dve.wait_ge(s_v, b + 1)
                    dve.wait_ge(s_sig, b + 1)
                    if b >= 2:
                        dve.wait_ge(s_o, b - 1)
                    v.tensor_tensor(rv[:, b % 2, :], r[:, b % 2, :], bank(4 + b % 2), ALU.mult).then_inc(s_rv, 1)

                for b in range(B):
                    for i in range(2):
                        dve.wait_ge(s_pv, 2 * b + i + 1)
                        v.scalar_tensor_tensor(out=mix[:, b % 2, i, :], in0=xT[:, b, 1:1 + T], scalar=mu[:, i:i + 1],
                                               in1=mix[:, b % 2, i, :], op0=ALU.mult, op1=ALU.add).then_inc(s_mx, 1)
                    if b >= 1:
                        act_k(dve, b - 1)
                    if b >= 2:
                        gate(b - 2)
                act_k(dve, B - 1)
                gate(B - 2)
                gate(B - 1)

            @block.gpsimd
            def _(pool):
                for b in range(B):
                    pool.wait_ge(s_rv, b + 1)
                    xb = g.x[:, b * KT:(b + 1) * KT, :].rearrange("p a c -> p (a c)")
                    nc.gpsimd.tensor_tensor(xb, xb, rv[:, b % 2, :], ALU.add).then_inc(s_o, 1)


class Globals:
    pass


STAGES = 99


def build(nc, din, out):
    ctx = ExitStack()
    with ctx:
        core = Core(nc, ctx)
        g = Globals()
        g.B, g.T, H = din["L0_attn_hidden"].shape
        assert H == P
        g.NH = din["L0_attn_A_log"].shape[0]
        g.D = P // g.NH
        g.KC = din["L0_attn_conv_q"].shape[1]
        g.NT = g.B * g.T // P
        g.x_dram, g.din, g.out = din["L0_attn_hidden"], din, out
        psum = [ctx.enter_context(nc.psum_tensor(f"bank{i}", [P, BANK], F32)) for i in range(8)]
        g.bank = lambda i: psum[i][:, :]
        g.ident = core.sb("ident", [P, P])
        g.eps5 = core.sb("eps5", [P, 1])
        g.eps6, g.eps6d = core.sb("eps6", [P, 1]), core.sb("eps6d", [P, 1])
        g.one, g.two = core.sb("one", [P, 1]), core.sb("two", [P, 1])
        g.s_out = nc.alloc_semaphore("out_written")
        s_eps = core.sem("eps")
        with nc.Block() as block:

            @block.vector
            def _(dve):
                nc.vector.memset(g.eps5[:, :], 1e-5).then_inc(s_eps, 1)
                nc.vector.memset(g.eps6[:, :], 1e-6).then_inc(s_eps, 1)
                nc.vector.memset(g.eps6d[:, :], 1e-6 * g.D).then_inc(s_eps, 1)
                nc.vector.memset(g.one[:, :], 1.0).then_inc(s_eps, 1)
                nc.vector.memset(g.two[:, :], 2.0).then_inc(s_eps, 1)

        x1_dram = out.rearrange("b t c -> (b t) c").rearrange("(n p) c -> p n c", p=P)
        g.x = core.sb("x", [P, g.NT, P])
        NS = (g.NT + din["L0_ffn_w_router"].shape[1] + 3) // 4 * 4
        g.sorted_x = nc.dram_tensor("sorted_x", [NS * P, P], F32, kind="Internal").ap()
        g.sorted_y = nc.dram_tensor("sorted_y", [NS * P, P], F32, kind="Internal").ap()
        g.work = core.sb("work", [P, 3 * g.NT * P])[:, :]
        NTP = g.NT * P
        g.xn = g.work[:, 0:NTP].rearrange("p (n c) -> p n c", n=g.NT)
        g.xT = g.work[:, NTP:2 * NTP + g.B].rearrange("p (b t) -> p b t", b=g.B)
        g.nstats, g.nmv = core.sb("nstats", [P, g.NT, 6]), core.sb("nmv", [P, g.NT, 2])
        g.rstd, g.nmr = core.sb("rstd", [P, g.NT]), core.sb("nmr", [P, g.NT])
        with ExitStack() as actx:
            sb = lambda n, s: core.sb(n, s, F32, actx)
            g.woT, g.norm_w = sb("woT", [P, P]), sb("norm_w", [P, 1])
            g.gateT = sb("gateT", [P, g.B, g.T])
            g.A_log, g.dt_bias = sb("A_log", [P, 1]), sb("dt_bias", [P, 1])
            g.beta, g.z = sb("beta", [P, g.T]), sb("z", [P, g.T])
            g.q, g.v = sb("q", [P, g.D, g.T]), sb("v", [P, g.D, g.T])
            g.k = g.x[:, :, :].rearrange("p n c -> p (n c)").rearrange("p (d t) -> p d t", d=g.D)
            g.o = g.v
            delta_in(core, g, din)
            delta_rule(core, g)
            delta_out(core, g)
        core.end_layer_part()
        if STAGES >= 2:
            moe(core, g, din)
            core.end_layer_part()
        if STAGES >= 3:
            attention(core, g, din)
            core.end_layer_part()
        if STAGES >= 4:
            channel_mix(core, g, din, out)
        else:
            with nc.Block() as block:

                @block.sync
                def _(sp):
                    sp.dma_start(x1_dram, g.x[:, :, :]).then_inc(g.s_out, 16)
                    sp.wait_ge(g.s_out, 16)


def kernel(**inputs):
    import concourse.bacc as bacc
    from concourse.bass_utils import run_bass_kernel_spmd

    nc = bacc.Bacc("TRN2", target_bir_lowering=False, num_devices=1)
    arrays, din = {}, {}
    for name, value in inputs.items():
        a = np.ascontiguousarray(value)
        arrays["in_" + name] = a
        din[name] = nc.dram_tensor("in_" + name, a.shape, mybir.dt.from_np(a.dtype), kind="ExternalInput").ap()
    shape = inputs["L0_attn_hidden"].shape
    out = nc.dram_tensor("out_x", shape, F32, kind="ExternalOutput").ap()
    build(nc, din, out)
    r = run_bass_kernel_spmd(nc, [arrays], core_ids=[0])
    return r.results[0]["out_x"]
```
